# Optimizing a Trainium2 kernel written in Bass

```python
import numpy as np
import jax
import jax.numpy as jnp

def _softmax(x, axis=-1):
    return jax.nn.softmax(x, axis=axis)

def _gelu(x):
    return jax.nn.gelu(x, approximate=True)

def _silu(x):
    return jax.nn.silu(x)

def _sigmoid(x):
    return jax.nn.sigmoid(x)

def _layernorm(x, axis=-1, eps=1e-05):
    m = jnp.mean(x, axis=axis, keepdims=True)
    v = jnp.var(x, axis=axis, keepdims=True)
    return (x - m) / jnp.sqrt(v + eps)

def _scatter_add(tgt, idx, src, axis=0):
    return tgt.at[idx].add(src)

def _segment_sum(src, seg, n):
    return jax.ops.segment_sum(src, seg, n)
kernel_name = 'mk_gnn_ffn_d2_gnn_r32_d12b84'

def setup_inputs(seed: int=0):
    np.random.seed(seed)
    _w = jnp.asarray

    def _rec_inputs():
        import jax
        import jax.numpy as jnp
        _gk = jax.random.key(seed)
        x = -8.776e-05 + 1 * jax.random.normal(jax.random.fold_in(_gk, 1), (3125, 256), jnp.float32)
        src = jax.random.randint(jax.random.fold_in(_gk, 2), (50000,), 0, 3125, jnp.int32)
        dst = jnp.minimum((3125 * jax.random.uniform(jax.random.fold_in(_gk, 3), (50000,)) ** 2.0).astype(jnp.int32), 99999)
        _o = jnp.argsort(dst, stable=True)
        src = src[_o]
        dst = dst[_o]
        edge_type_8 = jax.random.randint(jax.random.fold_in(_gk, 13), (50000,), 0, 8, jnp.int32)
        return (x, src, dst, edge_type_8)
    x, src, dst, edge_type_8 = _rec_inputs()

    def _L0_gnn_setup():
        import jax, jax.numpy as jnp
        import numpy as np
        N_NODES = 625
        N_EDGES = 10000
        NUM_RELS = 8
        DIM = 256
        BN_EPS = 1e-05
        key = jax.random.key(seed)
        k1, k2, k3, k4, k5 = jax.random.split(key, 5)
        h = jax.random.normal(k1, (N_NODES, DIM), dtype=jnp.float32)
        weight = jax.random.normal(k2, (NUM_RELS, DIM, DIM), dtype=jnp.float32) * 0.05
        gamma = jnp.ones((DIM,), dtype=jnp.float32)
        beta = jnp.zeros((DIM,), dtype=jnp.float32)
        src = jax.random.randint(k3, (N_EDGES,), 0, N_NODES, dtype=jnp.int32)
        dst = jax.random.randint(k4, (N_EDGES,), 0, N_NODES, dtype=jnp.int32)
        rel = jax.random.randint(k5, (N_EDGES,), 0, NUM_RELS, dtype=jnp.int32)
        return {'h': h, 'weight': weight, 'gamma': gamma, 'beta': beta, 'src': src, 'dst': dst, 'rel': rel}
    _L0_gnn_all = _L0_gnn_setup()
    _L0_gnn_in = {k: v for k, v in _L0_gnn_all.items() if k in ('weight', 'gamma', 'beta')}
    del _L0_gnn_all

    def _L0_ffn_setup():
        import jax, jax.numpy as jnp
        import numpy as np
        DIM = 256
        H = 8
        D = 64
        G = 64
        INNER = H * D
        SCALE = D ** (-0.5)
        key = jax.random.key(seed)
        ks = jax.random.split(key, 12)
        B, N = (4, 512)
        x = jax.random.normal(ks[0], (B, N, DIM), dtype=jnp.float32)
        s = lambda fan_in: 1.0 / np.sqrt(fan_in)
        W_fx = jax.random.normal(ks[1], (DIM, INNER), dtype=jnp.float32) * s(DIM)
        b_fx = jnp.zeros((INNER,), dtype=jnp.float32)
        W_x = jax.random.normal(ks[2], (DIM, INNER), dtype=jnp.float32) * s(DIM)
        b_x = jnp.zeros((INNER,), dtype=jnp.float32)
        A = jax.random.normal(ks[3], (G, D), dtype=jnp.float32)
        Q, _ = jnp.linalg.qr(A.T)
        W_slice = Q[:, :G].astype(jnp.float32)
        b_slice = jnp.zeros((G,), dtype=jnp.float32)
        W_q = jax.random.normal(ks[4], (D, D), dtype=jnp.float32) * s(D)
        W_k = jax.random.normal(ks[5], (D, D), dtype=jnp.float32) * s(D)
        W_v = jax.random.normal(ks[6], (D, D), dtype=jnp.float32) * s(D)
        W_out = jax.random.normal(ks[7], (INNER, DIM), dtype=jnp.float32) * s(INNER)
        b_out = jnp.zeros((DIM,), dtype=jnp.float32)
        temperature = jnp.ones((1, H, 1, 1), dtype=jnp.float32) * 0.5
        return {'x': x, 'W_fx': W_fx, 'b_fx': b_fx, 'W_x': W_x, 'b_x': b_x, 'W_slice': W_slice, 'b_slice': b_slice, 'W_q': W_q, 'W_k': W_k, 'W_v': W_v, 'W_out': W_out, 'b_out': b_out, 'temperature': temperature}
    _L0_ffn_all = _L0_ffn_setup()
    _L0_ffn_in = {k: v for k, v in _L0_ffn_all.items() if k in ('W_fx', 'b_fx', 'W_x', 'b_x', 'W_slice', 'b_slice', 'W_q', 'W_k', 'W_v', 'W_out', 'b_out', 'temperature')}
    del _L0_ffn_all

    def _L1_gnn_setup():
        import jax, jax.numpy as jnp
        import numpy as np
        N_NODES = 50000
        N_EDGES = 25000
        H = 256

        def sage_layer(x, src, dst, Wl, bl, Wr, n_nodes):
            msg = x[src]
            agg = jax.ops.segment_sum(msg, dst, num_segments=n_nodes)
            deg = jax.ops.segment_sum(jnp.ones_like(src, dtype=x.dtype), dst, num_segments=n_nodes)
            agg = agg / jnp.maximum(deg, 1.0)[:, None]
            return agg @ Wl.T + bl + x @ Wr.T
        key = jax.random.key(seed)
        ks = jax.random.split(key, 12)
        scale = 1.0 / np.sqrt(H)
        inp = {'x': jax.random.normal(ks[0], (N_NODES, H), dtype=jnp.float32), 'edge_index': jax.random.randint(ks[1], (2, N_EDGES), 0, N_NODES, dtype=jnp.int64)}
        for i, name in enumerate(['Wl1', 'Wr1', 'Wl2', 'Wr2', 'Wl3', 'Wr3']):
            inp[name] = jax.random.normal(ks[2 + i], (H, H), dtype=jnp.float32) * scale
        for name in ['bl1', 'bl2', 'bl3']:
            inp[name] = jnp.zeros((H,), dtype=jnp.float32)
        return inp
    _L1_gnn_all = _L1_gnn_setup()
    _L1_gnn_in = {k: v for k, v in _L1_gnn_all.items() if k in ('Wl1', 'bl1', 'Wr1', 'Wl2', 'bl2', 'Wr2', 'Wl3', 'bl3', 'Wr3')}
    del _L1_gnn_all

    def _L1_ffn_setup():
        import jax, jax.numpy as jnp
        import numpy as np
        B, S, H, F, E, K = (8, 128, 256, 512, 16, 2)
        EPS = 1e-05
        key = jax.random.key(seed)
        ks = jax.random.split(key, 9)
        sc = 0.02
        return {'x': jax.random.normal(ks[0], (B, S, H), dtype=jnp.float32), 'gate_w': jax.random.normal(ks[1], (H, E), dtype=jnp.float32) * sc, 'gate_b': jnp.zeros((E,), dtype=jnp.float32), 'w1': jax.random.normal(ks[2], (E, H, F), dtype=jnp.float32) * sc, 'b1': jnp.zeros((E, F), dtype=jnp.float32), 'w2': jax.random.normal(ks[3], (E, F, H), dtype=jnp.float32) * sc, 'b2': jnp.zeros((E, H), dtype=jnp.float32), 'gamma': jnp.ones((H,), dtype=jnp.float32), 'beta': jnp.zeros((H,), dtype=jnp.float32)}
    _L1_ffn_all = _L1_ffn_setup()
    _L1_ffn_in = {k: v for k, v in _L1_ffn_all.items() if k in ('gate_w', 'gate_b', 'w1', 'b1', 'w2', 'b2', 'gamma', 'beta')}
    del _L1_ffn_all
    return {'x': x, 'src': src, 'dst': dst, 'edge_type_8': edge_type_8, 'L0_gnn_weight': _L0_gnn_in['weight'], 'L0_gnn_gamma': _L0_gnn_in['gamma'], 'L0_gnn_beta': _L0_gnn_in['beta'], 'L0_ffn_W_fx': _L0_ffn_in['W_fx'], 'L0_ffn_b_fx': _L0_ffn_in['b_fx'], 'L0_ffn_W_x': _L0_ffn_in['W_x'], 'L0_ffn_b_x': _L0_ffn_in['b_x'], 'L0_ffn_W_slice': _L0_ffn_in['W_slice'], 'L0_ffn_b_slice': _L0_ffn_in['b_slice'], 'L0_ffn_W_q': _L0_ffn_in['W_q'], 'L0_ffn_W_k': _L0_ffn_in['W_k'], 'L0_ffn_W_v': _L0_ffn_in['W_v'], 'L0_ffn_W_out': _L0_ffn_in['W_out'], 'L0_ffn_b_out': _L0_ffn_in['b_out'], 'L0_ffn_temperature': _L0_ffn_in['temperature'], 'L1_gnn_Wl1': _L1_gnn_in['Wl1'], 'L1_gnn_bl1': _L1_gnn_in['bl1'], 'L1_gnn_Wr1': _L1_gnn_in['Wr1'], 'L1_gnn_Wl2': _L1_gnn_in['Wl2'], 'L1_gnn_bl2': _L1_gnn_in['bl2'], 'L1_gnn_Wr2': _L1_gnn_in['Wr2'], 'L1_gnn_Wl3': _L1_gnn_in['Wl3'], 'L1_gnn_bl3': _L1_gnn_in['bl3'], 'L1_gnn_Wr3': _L1_gnn_in['Wr3'], 'L1_ffn_gate_w': _L1_ffn_in['gate_w'], 'L1_ffn_gate_b': _L1_ffn_in['gate_b'], 'L1_ffn_w1': _L1_ffn_in['w1'], 'L1_ffn_b1': _L1_ffn_in['b1'], 'L1_ffn_w2': _L1_ffn_in['w2'], 'L1_ffn_b2': _L1_ffn_in['b2'], 'L1_ffn_gamma': _L1_ffn_in['gamma'], 'L1_ffn_beta': _L1_ffn_in['beta']}

def reference(x, src, dst, edge_type_8, L0_gnn_weight, L0_gnn_gamma, L0_gnn_beta, L0_ffn_W_fx, L0_ffn_b_fx, L0_ffn_W_x, L0_ffn_b_x, L0_ffn_W_slice, L0_ffn_b_slice, L0_ffn_W_q, L0_ffn_W_k, L0_ffn_W_v, L0_ffn_W_out, L0_ffn_b_out, L0_ffn_temperature, L1_gnn_Wl1, L1_gnn_bl1, L1_gnn_Wr1, L1_gnn_Wl2, L1_gnn_bl2, L1_gnn_Wr2, L1_gnn_Wl3, L1_gnn_bl3, L1_gnn_Wr3, L1_ffn_gate_w, L1_ffn_gate_b, L1_ffn_w1, L1_ffn_b1, L1_ffn_w2, L1_ffn_b2, L1_ffn_gamma, L1_ffn_beta):
    import jax
    import jax.numpy as jnp

    def _L0_gnn_ref(h, weight, gamma, beta, src, dst, rel):
        import jax, jax.numpy as jnp
        import numpy as np
        N_NODES = 625
        N_EDGES = 10000
        NUM_RELS = 8
        DIM = 256
        BN_EPS = 1e-05
        all_h = jnp.einsum('ni,rio->nro', h, weight)
        msg = all_h[src, rel]
        agg = jax.ops.segment_sum(msg, dst, num_segments=h.shape[0])
        mean = jnp.mean(agg, axis=0)
        var = jnp.mean(jnp.square(agg - mean), axis=0)
        out = (agg - mean) * jax.lax.rsqrt(var + BN_EPS) * gamma + beta
        return out

    def _L0_ffn_ref(x, W_fx, b_fx, W_x, b_x, W_slice, b_slice, W_q, W_k, W_v, W_out, b_out, temperature):
        import jax, jax.numpy as jnp
        import numpy as np
        DIM = 256
        H = 8
        D = 64
        G = 64
        INNER = H * D
        SCALE = D ** (-0.5)
        B, N, _ = x.shape
        fx_mid = (x @ W_fx + b_fx).reshape(B, N, H, D).transpose(0, 2, 1, 3)
        x_mid = (x @ W_x + b_x).reshape(B, N, H, D).transpose(0, 2, 1, 3)
        temp = jnp.clip(temperature, 0.1, 5.0)
        slice_weights = jax.nn.softmax((x_mid @ W_slice + b_slice) / temp, axis=-1)
        slice_norm = slice_weights.sum(axis=2)
        slice_token = jnp.einsum('bhnc,bhng->bhgc', fx_mid, slice_weights)
        slice_token = slice_token / (slice_norm[..., None] + 1e-05)
        q = slice_token @ W_q
        k = slice_token @ W_k
        v = slice_token @ W_v
        attn = jax.nn.softmax(jnp.einsum('bhgc,bhkc->bhgk', q, k) * SCALE, axis=-1)
        out_slice = jnp.einsum('bhgk,bhkc->bhgc', attn, v)
        out_x = jnp.einsum('bhgc,bhng->bhnc', out_slice, slice_weights)
        out_x = out_x.transpose(0, 2, 1, 3).reshape(B, N, INNER)
        return out_x @ W_out + b_out

    def _L1_gnn_ref(x, edge_index, Wl1, bl1, Wr1, Wl2, bl2, Wr2, Wl3, bl3, Wr3):
        import jax, jax.numpy as jnp
        import numpy as np
        N_NODES = 50000
        N_EDGES = 25000
        H = 256

        def sage_layer(x, src, dst, Wl, bl, Wr, n_nodes):
            msg = x[src]
            agg = jax.ops.segment_sum(msg, dst, num_segments=n_nodes)
            deg = jax.ops.segment_sum(jnp.ones_like(src, dtype=x.dtype), dst, num_segments=n_nodes)
            agg = agg / jnp.maximum(deg, 1.0)[:, None]
            return agg @ Wl.T + bl + x @ Wr.T
        src, dst = (edge_index[0], edge_index[1])
        n = x.shape[0]
        h = jax.nn.elu(sage_layer(x, src, dst, Wl1, bl1, Wr1, n))
        h = jax.nn.elu(sage_layer(h, src, dst, Wl2, bl2, Wr2, n))
        h = jax.nn.elu(sage_layer(h, src, dst, Wl3, bl3, Wr3, n))
        return h

    def _L1_ffn_ref(x, gate_w, gate_b, w1, b1, w2, b2, gamma, beta):
        import jax, jax.numpy as jnp
        import numpy as np
        B, S, H, F, E, K = (8, 128, 256, 512, 16, 2)
        EPS = 1e-05
        gate_logits = x @ gate_w + gate_b
        topk_vals, topk_idx = jax.lax.top_k(gate_logits, K)
        topk_w = jax.nn.softmax(topk_vals, axis=-1)
        h = jax.nn.relu(jnp.einsum('bsh,ehf->bsef', x, w1) + b1)
        expert_out = jnp.einsum('bsef,efh->bseh', h, w2) + b2
        sel = jnp.take_along_axis(expert_out, topk_idx[:, :, :, None], axis=2)
        moe = jnp.sum(topk_w[..., None] * sel, axis=2)
        y = x + moe
        mu = jnp.mean(y, axis=-1, keepdims=True)
        var = jnp.var(y, axis=-1, keepdims=True)
        return (y - mu) / jnp.sqrt(var + EPS) * gamma + beta
    edge_index = jnp.stack([src, dst])
    x = x + _L0_gnn_ref(_layernorm(x, axis=-1), L0_gnn_weight, L0_gnn_gamma, L0_gnn_beta, src, dst, edge_type_8)
    x = x + _L0_ffn_ref(_layernorm(x, axis=-1)[None], L0_ffn_W_fx, L0_ffn_b_fx, L0_ffn_W_x, L0_ffn_b_x, L0_ffn_W_slice, L0_ffn_b_slice, L0_ffn_W_q, L0_ffn_W_k, L0_ffn_W_v, L0_ffn_W_out, L0_ffn_b_out, L0_ffn_temperature)[0]
    x = x + _L1_gnn_ref(_layernorm(x, axis=-1), edge_index, L1_gnn_Wl1, L1_gnn_bl1, L1_gnn_Wr1, L1_gnn_Wl2, L1_gnn_bl2, L1_gnn_Wr2, L1_gnn_Wl3, L1_gnn_bl3, L1_gnn_Wr3)
    x = x + _L1_ffn_ref(_layernorm(x, axis=-1)[None], L1_ffn_gate_w, L1_ffn_gate_b, L1_ffn_w1, L1_ffn_b1, L1_ffn_w2, L1_ffn_b2, L1_ffn_gamma, L1_ffn_beta)[0]
    return x

_drawn_inputs = setup_inputs


def setup_inputs(seed=0):
    import zlib

    import numpy as np

    out = dict(_drawn_inputs(seed))
    spreads = {'L0_gnn_gamma': (1.0, 0.2),
     'L0_gnn_beta': (0.0, 0.1),
     'L0_ffn_b_fx': (0.0, 0.1),
     'L0_ffn_b_x': (0.0, 0.8),
     'L0_ffn_b_slice': (0.0, 0.8),
     'L0_ffn_b_out': (0.0, 0.1),
     'L0_ffn_temperature': (0.5, 0.6),
     'L1_gnn_bl1': (0.0, 0.1),
     'L1_gnn_bl2': (0.0, 0.1),
     'L1_gnn_bl3': (0.0, 0.1),
     'L1_ffn_gate_b': (0.0, 0.346),
     'L1_ffn_b1': (0.0, 0.8),
     'L1_ffn_b2': (0.0, 0.282),
     'L1_ffn_gamma': (1.0, 0.2),
     'L1_ffn_beta': (0.0, 0.1)}
    factors = {'L0_ffn_W_x': 8.0, 'L0_ffn_W_slice': 8.0, 'L0_ffn_W_q': 8.0, 'L0_ffn_W_k': 8.0}
    for name, (base, spread) in spreads.items():
        noise = np.random.default_rng([zlib.crc32(name.encode()), seed]).standard_normal(out[name].shape)
        drawn = base * np.exp(spread * noise) if base else spread * noise
        out[name] = jnp.asarray(drawn.astype(out[name].dtype))
    for name, factor in factors.items():
        out[name] = (out[name] * factor).astype(out[name].dtype)
    return out
```

```python
from contextlib import ExitStack, contextmanager

import concourse.bass as bass
from concourse import mybir

FP32 = mybir.dt.float32
I32 = mybir.dt.int32
U32 = mybir.dt.uint32
ALU = mybir.AluOpType
ACT = mybir.ActivationFunctionType
AX = mybir.AxisListType.X

P = 128
D = 256
KD = D // P
N = 3125
T = -(-N // P)
LAST = N - (T - 1) * P
NP = T * P
E = 50000
R = 8
EC = -(-E // P)
EK = -(-EC // P)
EP, EF = 125, 400
RING = 16
GROUP = RING // 2
PAIRS = -(-(EC + T - 1) // RING) * RING
ROUNDS = PAIRS // RING
HEADS, HD = 8, 64
INNER = HEADS * HD
HP = INNER // P
SCALE = HD ** -0.5
LAYERS = 3
X16, FF, TOPK = 16, 512, 2
KF = FF // P
ENTRIES = T * TOPK
ETILES = (N * TOPK + X16 * (P - 1)) // P
EPS = 1e-5
NOWHERE = -1.0e6


class Chain:

    def __init__(self, eng, sem):
        self.eng, self.sem, self.n, self.shift = eng, sem, 0, 0

    def mark(self, ins):
        ins.then_inc(self.sem, 1)
        self.n += 1

    def settle(self):
        self.eng.wait_ge(self.sem, self.n + self.shift)

    def __call__(self, ins):
        self.mark(ins)
        self.settle()

    @contextmanager
    def loop(self, start, end, per):
        before, at = self.shift, self.n
        with self.eng.Fori(start, end) as i:
            self.shift = (i - start) * per + before
            yield i
            assert self.n - at == per, (self.n - at, per)
        self.shift, self.n = before, at + per * (end - start)


def node_tiles(eng, body, chain=None, per=0):
    body(0, 0, 0)
    body(1, 0, 1)
    loop = chain.loop(1, T // 2, 2 * per) if chain else eng.Fori(1, T // 2)
    with loop as i:
        body(2 * i, i, 0)
        body(2 * i + 1, i, 1)
    body(T - 1, T // 2, 0)


def first_use(t):
    return isinstance(t, int) and t < 2


def gnn_ffn_moe_program(nc, A, out):
    ctx = ExitStack()
    sems = {}

    def sem(name):
        if name not in sems:
            sems[name] = ctx.enter_context(nc.semaphore(name))
        return sems[name]

    def sb(name, shape, dt=FP32):
        return ctx.enter_context(nc.sbuf_tensor(name, shape, dt))

    with ctx:
        projected = nc.dram_tensor("projected", (NP * R, D), FP32)
        nodes = nc.dram_tensor("nodes", (NP, D), FP32)
        in_order = nc.dram_tensor("in_order", (EC * P, 2), FP32)
        slots = nc.dram_tensor("slots", (P * ETILES, 1), I32)
        expert_rows = nc.dram_tensor("expert_rows", (ETILES * P, D), FP32)

        x = sb("x_res", [P, T, D])
        h = sb("h_now", [P, T, D + 1])
        acc = sb("acc", [P, (T + 1) * (D + 1)])
        accv = acc[:, :].rearrange("p (t d) -> p t d", d=D + 1)
        sw = sb("sw", [P, T * INNER])
        swv = sw[:, :].rearrange("p (t d) -> p t d", d=INNER)
        rows = sb("rows", [P, RING, D + 1])
        ident = sb("ident", [P, P])
        before = sb("before", [P, P])
        ones = sb("ones", [P, P])
        inv_n = sb("inv_n", [P, P])
        iota = sb("iota", [P, PAIRS + 2])
        pidx = sb("pidx", [P, EK])
        eps = sb("eps", [P, 1])
        onehot = sb("onehot", [P, 4, P])
        pair_dst = sb("pair_dst", [P, PAIRS + 2])
        pair_row0 = sb("pair_row0", [P, PAIRS], I32)
        pair_row = sb("pair_row", [P, PAIRS], I32)
        pair_tile = sb("pair_tile", [P, PAIRS], I32)
        staged = sb("staged", [P, 2, GROUP], I32)
        staged_tok = sb("staged_tok", [P, 2, GROUP], I32)
        bst = sb("bst", [P, T, 6])
        mv = sb("mv", [P, T, 2])
        nrm = sb("nrm", [P, 4, T])
        hT = sb("hT", [P, 2, 4, P])
        wide = sb("wide", [P, 8, D])
        gamma_b, beta_b, bout_b, gf_b, bf_b = (wide[:, j, :] for j in range(5))
        bl_b = wide[:, 5:8, :]
        col = sb("col", [P, 4, D])
        w_fx = sb("w_fx", [P, KD, INNER])
        w_out = sb("w_out", [HD, HEADS, D])
        wc = sb("wc", [P, KD, INNER])
        bc = sb("bc", [P, INNER])
        sage_w = sb("sage_w", [P, LAYERS * 4, D])
        gate_w = sb("gate_w", [P, KD, X16])
        smalls = sb("smalls", [P, 640])
        small_i = sb("small_i", [P, 6, 32], I32)
        small_f = sb("small_f", [P, 10, 32])
        flag = sb("flag", [P, 1], I32)

        at = [0]

        def small(shape):
            n = 1
            for s in shape[1:]:
                n *= s
            v = smalls[0:shape[0], at[0]:at[0] + n]
            at[0] += n
            return v

        w_slice2 = small([P, P])
        w_q, w_k, w_v = (small([HD, HD]) for _ in range(3))
        bslice_b = small([P, HD])
        temp_b = small([P, HEADS])
        gb_b = small([P, X16])
        bx_col = small([P, HP])
        hs = small([P, 16])
        soft = small([P, 4 * HEADS])

        def carve(tile, start, shape, dt=FP32):
            n = 1
            for s in shape[1:]:
                n *= s
            v = tile[0:shape[0], start:start + n]
            return (v.bitcast(dt) if dt != FP32 else v), start + n

        dst_a, a = carve(acc, 0, [EP, EF], I32)
        dst_b, a = carve(acc, a, [EP, EF], I32)
        src_a, a = carve(acc, a, [EP, EF], I32)
        rel_a, a = carve(acc, a, [EP, EF], I32)
        junk, a = carve(acc, a, [EP, EF])
        edge_int, a = carve(acc, a, [P, EK * P], I32)
        edges, a = carve(acc, a, [P, EK * P * 2])
        chosen, a = carve(acc, a, [P, EK * PAIRS])
        pair_c, a = carve(acc, a, [P, PAIRS])
        pair_b, a = carve(acc, a, [P, PAIRS])
        assert a <= (T + 1) * (D + 1), a
        edges_v = edges.rearrange("p (k e w) -> p k e w", k=EK, w=2)
        chosen_v = chosen.rearrange("p (k t) -> p k t", k=EK)
        w_rel, a = carve(sw, 0, [P, KD * R * D])
        w_rel = w_rel.rearrange("p (k r o) -> p k r o", k=KD, r=R)
        w_rel_mm = sw[:, 0:KD * R * D].rearrange("p (k n) -> p k n", k=KD)
        proj, a = carve(sw, a, [P, 2 * R * D])
        proj = proj.rearrange("p (s n) -> p s n", s=2)
        edge_src, a = carve(sw, a, [P, EK * P], I32)
        edge_rel, a = carve(sw, a, [P, EK * P], I32)
        cum, a = carve(sw, a, [EP, T + 2])
        f_blk, a = carve(sw, a, [EP, EF])
        f_m, a = carve(sw, a, [EP, EF])
        f_s, a = carve(sw, a, [EP, EF])
        f_pos, a = carve(sw, a, [EP, EF])
        f_posi, a = carve(sw, a, [EP, EF], I32)
        f_pay, a = carve(sw, a, [EP, EF * 2])
        f_pay = f_pay.rearrange("p (e w) -> p e w", w=2)
        h_stage1, a = carve(sw, a, [P, 2 * D])
        h_stage1 = h_stage1.rearrange("p (s d) -> p s d", s=2)
        assert a <= T * INNER, a
        fone_idx = staged[0:EP, 0, 0:1]
        fone_pay = small_f[0:EP, 9, 0:2]
        squares = sw[:, 0:T * D].rearrange("p (t d) -> p t d", d=D)
        w_x, a = carve(sw, T * D, [P, KD * INNER])
        w_x = w_x.rearrange("p (k n) -> p k n", k=KD)
        w_xT, a = carve(sw, a, [P, HP * D])
        w_xT = w_xT.rearrange("p (g n) -> p g n", g=HP)
        bx_rep, a = carve(sw, a, [P, HP * P])
        bx_rep = bx_rep.rearrange("p (g n) -> p g n", g=HP)
        assert a <= T * INNER, a
        sage_raw = rows[:, :, :].rearrange("p a b -> p (a b)")[:, 0:6 * KD * D]
        sage_raw = sage_raw.rearrange("p (m k i) -> p m k i", m=6, k=KD)
        tn, a = carve(acc, 0, [P, HP * (D + 1)])
        tn = tn.rearrange("p (g d) -> p g d", g=HP)
        tnT, a = carve(acc, a, [P, KD * INNER])
        tnT = tnT.rearrange("p (k n) -> p k n", k=KD)
        norm_row, a = carve(acc, a, [1, INNER])
        slice_t, a = carve(acc, a, [HD, INNER])
        q_t, a = carve(acc, a, [HD, INNER])
        k_t, a = carve(acc, a, [HD, INNER])
        v_s, a = carve(acc, a, [HD, INNER])
        attn, a = carve(acc, a, [HD, INNER])
        attn_t, o_t = q_t, k_t
        mid, a = carve(acc, a, [P, HP * D])
        mid = mid.rearrange("p (g d) -> p g d", g=HP)
        b_fx, a = carve(acc, a, [1, INNER])
        odd = wc[0:HD, :, :].rearrange("p k n -> p (k n)").rearrange("p (g d) -> p g d", g=HP)
        assert a <= (T + 1) * (D + 1), a
        sw_stage, a = carve(acc, 0, [P, 2 * INNER])
        sw_stage = sw_stage.rearrange("p (s n) -> p s n", s=2)
        h_stage2, a = carve(acc, a, [P, 2 * D])
        h_stage2 = h_stage2.rearrange("p (s d) -> p s d", s=2)
        stage4, a = carve(sw, 0, [P, 2 * 4 * P])
        stage4 = stage4.rearrange("p (s n) -> p s n", s=2)
        elu_v, a = carve(sw, a, [P, 2 * D])
        elu_v = elu_v.rearrange("p (s d) -> p s d", s=2)
        elu_n, a = carve(sw, a, [P, 2 * D])
        elu_n = elu_n.rearrange("p (s d) -> p s d", s=2)
        elu_e, a = carve(sw, a, [P, 2 * D])
        elu_e = elu_e.rearrange("p (s d) -> p s d", s=2)
        w1, a = carve(sw, a, [P, 2 * KD * FF])
        w1 = w1.rearrange("p (s k f) -> p s k f", s=2, k=KD)
        w2, a = carve(sw, a, [P, 2 * KF * D])
        w2 = w2.rearrange("p (s k d) -> p s k d", s=2, k=KF)
        hidden, a = carve(sw, a, [P, 2 * KF * P])
        hidden = hidden.rearrange("p (s k n) -> p s k n", s=2, k=KF)
        y_out, a = carve(sw, a, [P, 2 * D])
        y_out = y_out.rearrange("p (s d) -> p s d", s=2)
        b2_row, a = carve(sw, a, [1, 2 * D])
        b2_row = b2_row.rearrange("p (s d) -> p s d", s=2)
        b1_col, a = carve(sw, a, [P, 2 * KF])
        b1_col = b1_col.rearrange("p (s k) -> p s k", s=2)
        logits, a = carve(sw, a, [P, T * X16])
        logits = logits.rearrange("p (t e) -> p t e", t=T)
        top8, a = carve(sw, a, [P, T * 8])
        top8 = top8.rearrange("p (t e) -> p t e", t=T)
        at8, a = carve(sw, a, [P, T * 8], U32)
        at8 = at8.rearrange("p (t e) -> p t e", t=T)
        ent, a = carve(sw, a, [P, ENTRIES])
        ent_m, a = carve(sw, a, [P, ENTRIES])
        ent_s, a = carve(sw, a, [P, ENTRIES])
        ent_pos, a = carve(sw, a, [P, ENTRIES])
        ent_posi, a = carve(sw, a, [P, ENTRIES], I32)
        ent_row, a = carve(sw, a, [P, ENTRIES], I32)
        ent_row2, a = carve(sw, a, [P, ENTRIES], I32)
        ent_tok, a = carve(sw, a, [P, ENTRIES], I32)
        gates, a = carve(sw, a, [P, ENTRIES])
        gates = gates.rearrange("p (t k) -> p t k", k=TOPK)
        gate_t, a = carve(sw, a, [P, 3 * T])
        gate_t = gate_t.rearrange("p (s t) -> p s t", s=3)
        counts, a = carve(sw, a, [P, X16])
        cmp_e, a = carve(sw, a, [P, ETILES * (X16 - 1)])
        cmp_e = cmp_e.rearrange("p (c e) -> p c e", e=X16 - 1)
        tile_x, a = carve(sw, a, [P, ETILES])
        tile_xi, a = carve(sw, a, [P, ETILES], I32)
        slot_tok, a = carve(sw, a, [P, ETILES], I32)
        assert a <= T * INNER, a

        ps = [ctx.enter_context(nc.psum_tensor(f"bank{j}", [P, 512], FP32)) for j in range(8)]

        edge_rows = 16 * ROUNDS * (LAYERS + 1)

        def scattered(k):
            return edge_rows + 16 * (ENTRIES // RING + (1 if k < ENTRIES % RING else 0))

        SCORES, SPREAD, SAGE, GATE, EXPERTS = T, 2 * T, 3 * T, 6 * T, 7 * T

        def hid_bank(slot, f):
            return ps[(2 if slot == 0 else 6) + f // 2][:, f % 2 * P:(f % 2 + 1) * P]

        block = ctx.enter_context(nc.Block())

        @block.sync
        def _(sp):
            sp.wait_ge(sem("x_padded"), 1)
            sp.dma_start(dst_a, A["dst"].rearrange("(p f) -> p f", f=EF)).then_inc(sem("dst_in"), 16)
            sp.wait_ge(sem("dst_b_set"), 1)
            sp.dma_start(dst_b[0:EP - 1, :], A["dst"][1:1 + (EP - 1) * EF].rearrange("(p f) -> p f", f=EF))\
                .then_inc(sem("dst_in"), 16)
            sp.dma_start(dst_b[EP - 1:EP, 0:EF - 1], A["dst"][1 + (EP - 1) * EF:E].unsqueeze(0))\
                .then_inc(sem("dst_in"), 16)
            sp.dma_start(x[:, 0:T - 1, :], A["x"][0:(T - 1) * P, :].rearrange("(t p) d -> p t d", p=P))\
                .then_inc(sem("x_in"), 16)
            sp.dma_start(x[0:LAST, T - 1, :], A["x"][(T - 1) * P:N, :]).then_inc(sem("x_in"), 16)
            for k in range(KD):
                sp.dma_start(w_rel[:, k], A["L0_gnn_weight"][:, k * P:(k + 1) * P, :]
                             .rearrange("r p o -> p r o")).then_inc(sem("w_rel_in"), 16)
            sp.wait_ge(sem("edges_zero"), 3)
            full = (EC - 1) // P
            part = EC - 1 - full * P
            for name, tile in (("dst", edge_int), ("src", edge_src), ("edge_type_8", edge_rel)):
                v = tile.rearrange("p (k e) -> p k e", k=EK)
                s = sem("edge_in")
                sp.dma_start(v[:, 0:full, :], A[name][0:full * P * P].rearrange("(k p e) -> p k e", p=P, e=P))\
                    .then_inc(s, 16)
                sp.dma_start(v[0:part, full, :], A[name][full * P * P:(EC - 1) * P].rearrange("(p e) -> p e", e=P))\
                    .then_inc(s, 16)
                sp.dma_start(v[part:part + 1, full, 0:E - (EC - 1) * P], A[name][(EC - 1) * P:E].unsqueeze(0))\
                    .then_inc(s, 16)
            sp.dma_start(src_a, A["src"].rearrange("(p f) -> p f", f=EF)).then_inc(sem("spare_in"), 16)
            sp.dma_start(rel_a, A["edge_type_8"].rearrange("(p f) -> p f", f=EF)).then_inc(sem("spare_in"), 16)

            s = sem("param_in")
            for m in range(6):
                name = f"L1_gnn_W{'lr'[m % 2]}{m // 2 + 1}"
                sp.dma_start(sage_raw[:, m], A[name].rearrange("(k p) i -> p k i", p=P)).then_inc(s, 16)
            for tile, name in ((gamma_b, "L0_gnn_gamma"), (beta_b, "L0_gnn_beta"), (bout_b, "L0_ffn_b_out"),
                               (gf_b, "L1_ffn_gamma"), (bf_b, "L1_ffn_beta"), (bl_b[:, 0, :], "L1_gnn_bl1"),
                               (bl_b[:, 1, :], "L1_gnn_bl2"), (bl_b[:, 2, :], "L1_gnn_bl3"),
                               (bslice_b, "L0_ffn_b_slice"), (gb_b, "L1_ffn_gate_b")):
                sp.dma_start(tile, A[name].partition_broadcast(P)).then_inc(s, 16)
            sp.dma_start(temp_b, A["L0_ffn_temperature"].rearrange("a h b c -> (a h b c)").partition_broadcast(P))\
                .then_inc(s, 16)
            sp.dma_start(w_fx[:, :, :], A["L0_ffn_W_fx"].rearrange("(k p) n -> p k n", p=P)).then_inc(s, 16)
            sp.dma_start(w_out[:, :, :], A["L0_ffn_W_out"].rearrange("(h c) d -> c h d", c=HD)).then_inc(s, 16)
            sp.dma_start(gate_w[:, :, :], A["L1_ffn_gate_w"].rearrange("(k p) e -> p k e", p=P)).then_inc(s, 16)
            for tile, name in ((w_q, "L0_ffn_W_q"), (w_k, "L0_ffn_W_k"), (w_v, "L0_ffn_W_v")):
                sp.dma_start(tile, A[name]).then_inc(s, 16)
            sp.dma_start(bx_col, A["L0_ffn_b_x"].rearrange("(g p) -> p g", p=P),
                         allow_slow_non_contiguous=True).then_inc(s, 16)
            sp.wait_ge(sem("slice2_zero"), 1)
            for b in range(2):
                sp.dma_start(w_slice2[b * HD:(b + 1) * HD, b * HD:(b + 1) * HD], A["L0_ffn_W_slice"])\
                    .then_inc(s, 16)

            table = projected.ap().rearrange("(t p r) d -> t p (r d)", p=P, r=R)

            def store_projected(t, use, slot):
                sp.wait_ge(sem("proj_copied"), t + 1)
                sp.dma_start(table[bass.ds(t, 1), :, :].rearrange("a p n -> p (a n)"), proj[:, slot, :])\
                    .then_inc(sem(f"proj_stored{slot}"), 16)

            node_tiles(sp, store_projected)
            sp.wait_ge(sem("proj_stored0"), 16 * (T // 2 + 1))
            sp.wait_ge(sem("proj_stored1"), 16 * (T // 2))
            sp.wait_ge(sem("edges_ready"), 1)
            sp.dma_start(w_x, A["L0_ffn_W_x"].rearrange("(k p) n -> p k n", p=P)).then_inc(sem("w_x_in"), 16)

            sp.wait_ge(sem("h_ready"), 2 * T)
            sp.dma_start(b_fx, A["L0_ffn_b_fx"].unsqueeze(0)).then_inc(sem("b_fx_in"), 16)
            sp.wait_ge(sem("odd_heads"), 1)
            sp.dma_start(mid[HD:P, :, :], odd).then_inc(sem("mid_moved"), 16)

            nodes_v = nodes.ap().rearrange("(t p) d -> p t d", p=P)
            sp.wait_ge(sem("h_ready"), 3 * T)
            sp.dma_start(nodes_v, h[:, :, 0:D]).then_inc(sem("nodes_stored"), 16)
            with sp.Fori(0, LAYERS - 1) as layer:
                sp.wait_ge(sem("layer_out"), layer * T + T)
                sp.dma_start(nodes_v, h[:, :, 0:D]).then_inc(sem("nodes_stored"), 16)
            sp.wait_ge(sem("h_ready"), 4 * T)
            sp.dma_start(nodes_v, h[:, :, 0:D]).then_inc(sem("nodes_stored"), 16)
            sp.wait_ge(sem("slots_set"), 1)
            sp.dma_start(slots.ap().rearrange("(p c) a -> p (c a)", p=P), slot_tok)\
                .then_inc(sem("slots_cleared"), 16)
            for j in range(RING):
                sp.wait_ge(sem(f"rows_in{j}"), scattered(j))
            sp.wait_ge(sem("slots_cleared"), 16)
            sp.dma_start(slot_tok, slots.ap().rearrange("(p c) a -> p (c a)", p=P))\
                .then_inc(sem("slot_tok_in"), 16)

            def load_expert(c, use, slot):
                e = sp.value_load(tile_xi[0:1, bass.ds(c, 1)], min_val=0, max_val=X16 - 1)
                if not first_use(c):
                    sp.wait_ge(sem("y_done"), c - 1)
                s = sem(f"expert_in{slot}")
                sp.dma_start(w1[:, slot], A["L1_ffn_w1"][bass.ds(e, 1), :, :]
                             .rearrange("a (k p) f -> p (a k) f", p=P)).then_inc(s, 16)
                sp.dma_start(w2[:, slot], A["L1_ffn_w2"][bass.ds(e, 1), :, :]
                             .rearrange("a (k p) d -> p (a k) d", p=P)).then_inc(s, 16)
                sp.dma_start(b1_col[:, slot], A["L1_ffn_b1"][bass.ds(e, 1), :]
                             .rearrange("a (k p) -> p (a k)", p=P),
                             allow_slow_non_contiguous=True).then_inc(s, 16)
                sp.dma_start(b2_row[:, slot], A["L1_ffn_b2"][bass.ds(e, 1), :]).then_inc(s, 16)

            def store_y(c, slot):
                sp.wait_ge(sem("y_copied"), c + 1)
                sp.dma_start(expert_rows.ap()[bass.ds(c * P, P), :], y_out[:, slot])\
                    .then_inc(sem(f"y_stored{slot}"), 16)

            sp.wait_ge(sem("tile_experts"), 1)
            load_expert(0, 0, 0)
            load_expert(1, 0, 1)
            with sp.Fori(1, ETILES // 2) as i:
                store_y(2 * i - 2, 0)
                load_expert(2 * i, i, 0)
                store_y(2 * i - 1, 1)
                load_expert(2 * i + 1, i, 1)
            store_y(ETILES - 2, 0)
            store_y(ETILES - 1, 1)
            result = h
            sp.wait_ge(sem("result_ready"), 1)
            sp.dma_start(out[0:(T - 1) * P, :].rearrange("(t p) d -> p t d", p=P), result[:, 0:T - 1, 0:D])\
                .then_inc(sem("out_stored"), 16)
            sp.dma_start(out[(T - 1) * P:N, :], result[0:LAST, T - 1, 0:D]).then_inc(sem("out_stored"), 16)
            sp.wait_ge(sem("out_stored"), 32)

        @block.gpsimd
        def _(pool):
            pool.memset(x[:, T - 1, :], 0.0).then_inc(sem("x_padded"), 1)
            pool.memset(dst_b[:, EF - 1:EF], N).then_inc(sem("dst_b_set"), 1)
            pool.iota(iota[:, :], [[1, PAIRS + 2]], base=0, channel_multiplier=0,
                      allow_small_or_imprecise_dtypes=True).then_inc(sem("const"), 1)
            pool.iota(pidx[:, :], [[P, EK]], base=0, channel_multiplier=1,
                      allow_small_or_imprecise_dtypes=True).then_inc(sem("const"), 1)
            pool.memset(ones[:, :], 1.0).then_inc(sem("const"), 1)
            pool.memset(inv_n[:, :], 1.0 / N).then_inc(sem("const"), 1)
            pool.memset(eps[:, :], EPS).then_inc(sem("const"), 1)
            pool.memset(h[:, :, D:D + 1], 1.0).then_inc(sem("const"), 1)
            pool.memset(edge_int, int(NOWHERE)).then_inc(sem("edges_zero"), 1)
            pool.memset(edge_rel, 0).then_inc(sem("edges_zero"), 1)
            pool.memset(edge_src, 0).then_inc(sem("edges_zero"), 1)
            pool.memset(w_slice2, 0.0).then_inc(sem("slice2_zero"), 1)

            def stage(t, slot, out_, tile, ready, used):
                if ready:
                    pool.wait_ge(*ready)
                if not first_use(t):
                    pool.wait_ge(*used)
                pool.nop(nofuse=True)
                pool.tensor_copy(out_, tile[:, bass.ds(t, 1), 0:out_.shape[1]].rearrange("p a n -> p (a n)"))\
                    .then_inc(sem("tile_staged"), 1)

            node_tiles(pool, lambda t, use, slot: stage(
                t, slot, h_stage1[:, slot, :], h, (sem("h_ready"), t + 1), (sem("transposed"), t - 1)))

            pool.wait_ge(sem("flag_ready"), 1)
            late = pool.value_load(flag[0:1, 0:1], min_val=0, max_val=E)
            with pool.If(late > 0):
                pool.wait_ge(sem("f_ready"), 1)
                behind = junk[0:1, 0:2 * P].rearrange("p (e w) -> p e w", w=2)
                pool.memset(behind[:, :, 0], 0.0).then_inc(sem("f_tail"), 1)
                pool.memset(behind[:, :, 1], NOWHERE).then_inc(sem("f_tail"), 1)
                pool.wait_ge(sem("f_tail"), 2)
                tail = in_order.ap().rearrange("(c e) w -> c (e w)", e=P)[EC - 1:EC, :]
                pool.dma_start(tail, junk[0:1, 0:2 * P]).then_inc(sem("f_moved"), 16)
                pool.wait_ge(sem("f_moved"), 16)
                with pool.Fori(0, EF) as c:
                    pool.tensor_copy(fone_idx, f_posi[:, bass.ds(c, 1)]).then_inc(sem("f_staged"), 1)
                    pool.tensor_copy(fone_pay, f_pay[:, bass.ds(c, 1), :].rearrange("p a w -> p (a w)"))\
                        .then_inc(sem("f_staged"), 1)
                    pool.wait_ge(sem("f_staged"), 2 * c + 2)
                    pool.nop(nofuse=True)
                    pool.indirect_dma_start(out=in_order.ap(), out_offset=bass.IndirectOffsetOnAxis(ap=fone_idx, axis=0),
                                            in_=fone_pay, in_offset=None).then_inc(sem("f_moved"), 16)
                    pool.wait_ge(sem("f_moved"), 16 * c + 32)
                back = in_order.ap().rearrange("(c e) w -> c (e w)", e=P)
                flat = edges.rearrange("p (k n) -> p k n", k=EK)
                pool.wait_ge(sem("edges_float"), 1)
                pool.dma_start(flat[:, 0:EK - 1, :], back[0:(EK - 1) * P, :].rearrange("(k p) n -> p k n", p=P))\
                    .then_inc(sem("f_back"), 16)
                pool.dma_start(flat[0:EC - (EK - 1) * P, EK - 1, :], back[(EK - 1) * P:EC, :])\
                    .then_inc(sem("f_back"), 16)
                pool.wait_ge(sem("f_back"), 32)
            pool.wait_ge(sem("spare_in"), 32)
            pool.wait_ge(sem("edges_float"), 1)
            pool.memset(onehot[:, 0, 0:1], 0.0).then_inc(sem("edges_ready"), 1)
            pool.wait_ge(sem("edges_ready"), 1)
            pool.wait_ge(sem("sage_done"), 6)
            pool.memset(rows[:, :, D:D + 1], 1.0).then_inc(sem("rows_ones"), 1)
            pool.wait_ge(sem("rows_ones"), 1)

            def gathers(i, table, index, done, base, count, groups=(0, 1)):
                for g in groups:
                    t = i * RING + g * GROUP
                    if not (isinstance(i, int) and i == 0):
                        pool.wait_ge(sem(done), base + t + (GROUP - RING))
                    pool.nop(nofuse=True)
                    pool.tensor_copy(staged[:, g, :], index[:, bass.ds(t, GROUP)]).then_inc(sem("staged"), 1)
                    count[0] = count[0] + 1
                    pool.wait_ge(sem("staged"), count[0])
                    pool.nop(nofuse=True)
                    for k in range(GROUP):
                        slot = g * GROUP + k
                        pool.indirect_dma_start(
                            out=rows[:, slot, 0:D], out_offset=None, in_=table,
                            in_offset=bass.IndirectOffsetOnAxis(ap=staged[:, g, k:k + 1], axis=0),
                        ).then_inc(sem(f"rows_in{slot}"), 16)

            def gather_edges(r, table, index):
                gathers(0, table, index, "pair_done", r * PAIRS, [r * 2 * ROUNDS])
                with pool.Fori(1, ROUNDS) as i:
                    gathers(i, table, index, "pair_done", r * PAIRS, [r * 2 * ROUNDS + i * 2])

            pool.wait_ge(sem("pair_tables"), 1)
            pool.wait_ge(sem("proj_stored0"), 16 * (T // 2 + 1))
            pool.wait_ge(sem("proj_stored1"), 16 * (T // 2))
            gather_edges(0, projected.ap(), pair_row0)
            def stage_scores(t, slot):
                stage(t, slot, h_stage2[:, slot, :], h, (sem("h_ready"), t + (T + 1)), (sem("transposed"), t + (SCORES - 1)))

            def keep_weights(t, slot):
                pool.wait_ge(sem("sw_ready"), t + 1)
                pool.nop(nofuse=True)
                pool.tensor_copy(swv[:, bass.ds(t, 1), :].rearrange("p a n -> p (a n)"), sw_stage[:, slot, :])\
                    .then_inc(sem("sw_kept"), 1)

            stage_scores(0, 0)
            stage_scores(1, 1)
            stage_scores(2, 0)
            keep_weights(0, 0)
            with pool.Fori(1, T // 2) as i:
                stage_scores(2 * i + 1, 1)
                keep_weights(2 * i - 1, 1)
                stage_scores(2 * i + 2, 0)
                keep_weights(2 * i, 0)
            keep_weights(T - 2, 1)
            keep_weights(T - 1, 0)
            pool.wait_ge(sem("sw_kept"), T)
            pool.wait_ge(sem("m_mm"), HP)
            node_tiles(pool, lambda t, use, slot: stage(
                t, slot, sw_stage[:, slot, :], swv, None, (sem("transposed"), t + (SPREAD - 1))))
            with pool.Fori(1, LAYERS + 1) as r:
                pool.wait_ge(sem("nodes_stored"), 16 * r)
                pool.nop(nofuse=True)
                gather_edges(r, nodes.ap(), pair_row)
                b = (r - 1) * T

                def stage_layer(t, use, slot):
                    pool.wait_ge(sem("pair_added"), r * PAIRS + PAIRS)
                    stage(t, slot, stage4[:, slot, D:2 * D], h, None, (sem("transposed"), b + (t + (SAGE - 1))))

                node_tiles(pool, stage_layer)
            n = 2 * ROUNDS * (LAYERS + 1)
            node_tiles(pool, lambda t, use, slot: stage(
                t, slot, stage4[:, slot, 0:D], h, (sem("h_ready"), t + (3 * T + 1)), (sem("transposed"), t + (GATE - 1))))
            pool.wait_ge(sem("layers_done"), 1)
            pool.iota(ent_tok.rearrange("p (t k) -> p t k", k=TOPK), [[P, T], [0, TOPK]], base=0,
                      channel_multiplier=1).then_inc(sem("toks"), 1)
            pool.memset(slot_tok, 0).then_inc(sem("slots_set"), 1)
            pool.wait_ge(sem("toks"), 1)
            pool.wait_ge(sem("places"), 1)
            pool.wait_ge(sem("slots_cleared"), 16)

            def scatter(j0, m, parts, g, before_):
                for k in before_:
                    pool.wait_ge(*k)
                pool.nop(nofuse=True)
                pool.tensor_copy(staged[0:parts, g, 0:m], ent_row[0:parts, bass.ds(j0, m)])\
                    .then_inc(sem("staged"), 1)
                pool.tensor_copy(staged_tok[0:parts, g, 0:m], ent_tok[0:parts, bass.ds(j0, m)])\
                    .then_inc(sem("staged"), 1)

            def send(g, m, parts):
                for k in range(m):
                    pool.indirect_dma_start(
                        out=slots.ap(), out_offset=bass.IndirectOffsetOnAxis(ap=staged[0:parts, g, k:k + 1], axis=0),
                        in_=staged_tok[0:parts, g, k:k + 1], in_offset=None,
                    ).then_inc(sem(f"rows_in{g * GROUP + k}"), 16)

            for g in range(2):
                scatter(g * GROUP, GROUP, P, g, ())
                n += 2
                pool.wait_ge(sem("staged"), n)
                send(g, GROUP, P)
            with pool.Fori(1, 3) as i:
                for g in range(2):
                    scatter(i * RING + g * GROUP, GROUP, P, g,
                            [(sem(f"rows_in{g * GROUP + k}"), 16 * i + edge_rows) for k in range(GROUP)])
                    pool.wait_ge(sem("staged"), (i - 1) * 4 + (n + 2 * g + 2))
                    pool.nop(nofuse=True)
                    send(g, GROUP, P)
            n += 8
            scatter(3 * RING, TOPK, LAST, 0, [(sem(f"rows_in{k}"), edge_rows + 48) for k in range(GROUP)])
            n += 2
            pool.wait_ge(sem("staged"), n)
            send(0, TOPK, LAST)

            pool.wait_ge(sem("slot_tok_in"), 16)
            pool.wait_ge(sem("nodes_stored"), 16 * (LAYERS + 1))
            gathers(0, nodes.ap(), slot_tok, "x_used", 0, [n])
            with pool.Fori(1, ETILES // RING) as i:
                gathers(i, nodes.ap(), slot_tok, "x_used", 0, [n + i * 2])
            n += 2 * (ETILES // RING)
            pool.wait_ge(sem("y_stored0"), 16 * (ETILES // 2))
            pool.wait_ge(sem("y_stored1"), 16 * (ETILES // 2))
            pool.wait_ge(sem("x_used"), ETILES)
            gathers(0, expert_rows.ap(), ent_posi, "combined", 0, [n])
            with pool.Fori(1, 3) as i:
                gathers(i, expert_rows.ap(), ent_posi, "combined", 0, [n + i * 2])
            n += 6
            pool.wait_ge(sem("combined"), 2 * RING + GROUP)
            pool.tensor_copy(staged[:, 0, 0:TOPK], ent_posi[:, 3 * RING:3 * RING + TOPK]).then_inc(sem("staged"), 1)
            pool.wait_ge(sem("staged"), n + 1)
            for k in range(TOPK):
                pool.indirect_dma_start(
                    out=rows[:, k, 0:D], out_offset=None, in_=expert_rows.ap(),
                    in_offset=bass.IndirectOffsetOnAxis(ap=staged[:, 0, k:k + 1], axis=0),
                ).then_inc(sem(f"rows_in{k}"), 16)

        @block.scalar
        def _(act):
            def root(k):
                act.wait_ge(sem("var_ready"), k + 1)
                act.activation(nrm[:, 0, :], mv[:, :, 1], ACT.Sqrt, bias=eps[:, 0:1]).then_inc(sem("sd_ready"), 1)

            act.wait_ge(sem("const"), 6)
            root(0)

            def project(t, use, slot):
                act.wait_ge(sem("transposed"), t + 1)
                if not first_use(t):
                    act.wait_ge(sem("p_mm"), t * 4 - 4)
                act.copy(hT[:, slot, 0:KD, :], ps[slot][:, 0:D].rearrange("p (k n) -> p k n", k=KD))\
                    .then_inc(sem("hT_ready"), 1)
                if not first_use(t):
                    act.wait_ge(sem(f"proj_stored{slot}"), 16 * use)
                for j in range(4):
                    act.wait_ge(sem("p_mm"), t * 4 + (j + 1))
                    ins = act.copy(proj[:, slot, j * 512:(j + 1) * 512], ps[2 + j][:, :])
                    ins.then_inc(sem("proj_copied") if j == 3 else sem("p_evac"), 1)
                    if j == 3:
                        act.wait_ge(sem("proj_copied"), t + 1)
                        act.sem_inc(sem("p_evac"), 1)

            node_tiles(act, project)
            for m in range(6):
                act.wait_ge(sem("sage_tp"), m + 1)
                act.copy(sage_w[:, 2 * m:2 * m + 2, :], ps[m % 2][:, :].rearrange("p (k n) -> p k n", k=KD))\
                    .then_inc(sem("sage_done"), 1)
            for k in range(KD):
                act.wait_ge(sem("wx_tp"), k + 1)
                act.copy(w_xT[:, :, k * P:(k + 1) * P], ps[2 + k][:, :].rearrange("p (g n) -> p g n", g=HP))\
                    .then_inc(sem("wxT_ready"), 1)
            act.wait_ge(sem("centred"), 1)
            act.activation(squares, accv[:, 0:T, 0:D], ACT.Square).then_inc(sem("squared"), 1)
            act.wait_ge(sem("bn_var"), 1)
            act.activation(col[:, 0, :], ps[5][:, 0:D], ACT.Sqrt, bias=eps[:, 0:1]).then_inc(sem("bn_sd"), 1)
            root(1)

            def scores(t, use, slot):
                act.wait_ge(sem("transposed"), t + (SCORES + 1))
                act.copy(hT[:, slot, 0:KD, :], ps[slot][:, 0:D].rearrange("p (k n) -> p k n", k=KD))\
                    .then_inc(sem("hT_ready"), 1)
                act.wait_ge(sem("l_shifted"), t + 1)
                v = swv[:, bass.ds(t, 1), :].rearrange("p a n -> p (a n)")
                act.activation(v, v, ACT.Exp).then_inc(sem("l_exp"), 1)

            node_tiles(act, scores)
            for k in range(KD):
                act.wait_ge(sem("tn_tp"), k + 1)
                act.copy(tnT[:, k, :], ps[k][:, :]).then_inc(sem("s_evac"), 1)
            act.wait_ge(sem("tn_tp"), 3)
            act.copy(norm_row, ps[2][0:1, :]).then_inc(sem("s_evac"), 1)
            act.wait_ge(sem("st_mm"), 1)
            act.copy(slice_t, ps[3][0:HD, :]).then_inc(sem("s_evac"), 1)
            for j, tile in enumerate((q_t, k_t, v_s)):
                act.wait_ge(sem("qkv_mm"), j + 1)
                act.copy(tile, ps[j][0:HD, :]).then_inc(sem("s_evac"), 1)
            act.wait_ge(sem("attn_shifted"), 1)
            act.activation(attn, attn, ACT.Exp, scale=SCALE).then_inc(sem("attn_exp"), 1)
            act.wait_ge(sem("attn_tp"), 1)
            act.copy(attn_t, ps[4][0:HD, :]).then_inc(sem("s_evac"), 1)
            act.wait_ge(sem("o_mm"), 1)
            act.copy(o_t, ps[5][0:HD, :]).then_inc(sem("s_evac"), 1)
            for g in range(HP):
                act.wait_ge(sem("m_mm"), g + 1)
                act.copy(mid[0:HD, g, :], ps[g][0:HD, 0:D]).then_inc(sem("mid_even"), 1)
                ins = act.copy(odd[:, g, :], ps[g][0:HD, D:2 * D])
                ins.then_inc(sem("odd_copied"), 1)
            act.wait_ge(sem("odd_copied"), HP)
            act.sem_inc(sem("odd_heads"), 1)

            def spread(t, use, slot):
                act.wait_ge(sem("transposed"), t + (SPREAD + 1))
                act.copy(hT[:, slot, :, :], ps[slot][:, :].rearrange("p (k n) -> p k n", k=4))\
                    .then_inc(sem("hT_ready"), 1)

            node_tiles(act, spread)
            root(2)
            with act.Fori(0, LAYERS) as layer:
                b = layer * T

                def layer_tile(t, use, slot):
                    act.wait_ge(sem("transposed"), b + (t + (SAGE + 1)))
                    act.copy(hT[:, slot, :, :], ps[slot][:, :].rearrange("p (k n) -> p k n", k=4))\
                        .then_inc(sem("hT_ready"), 1)
                    act.wait_ge(sem("elu_neg"), b + (t + 1))
                    act.activation(elu_e[:, slot], elu_n[:, slot], ACT.Exp).then_inc(sem("elu_exp"), 1)

                node_tiles(act, layer_tile)
            root(3)

            def gate_tile(t, use, slot):
                act.wait_ge(sem("transposed"), t + (GATE + 1))
                act.copy(hT[:, slot, 0:KD, :], ps[slot][:, 0:D].rearrange("p (k n) -> p k n", k=KD))\
                    .then_inc(sem("hT_ready"), 1)

            node_tiles(act, gate_tile)
            act.wait_ge(sem("gate_diff"), 1)
            act.activation(gate_t[:, 1, :], gate_t[:, 0, :], ACT.Exp).then_inc(sem("gate_exp"), 1)

            def x_copy(c, slot):
                act.wait_ge(sem("x_used"), c + 1)
                act.copy(hT[:, slot, 0:KD, :], ps[slot][:, 0:D].rearrange("p (k n) -> p k n", k=KD))\
                    .then_inc(sem("hT_ready"), 1)

            def expert_act(c, slot, last=False):
                if not last:
                    x_copy(c + 1, 1 - slot)
                for f in range(KF):
                    if f % 2 == 0:
                        act.wait_ge(sem("hid_mm"), c * KF + (f + 2))
                    act.activation(hidden[:, slot, f, :], hid_bank(slot, f), ACT.Relu,
                                   bias=b1_col[:, slot, f:f + 1]).then_inc(sem("hid_ready"), 1)

            x_copy(0, 0)
            with act.Fori(0, ETILES // 2 - 1) as i:
                expert_act(2 * i, 0)
                expert_act(2 * i + 1, 1)
            expert_act(ETILES - 2, 0)
            expert_act(ETILES - 1, 1, last=True)
            root(4)

        @block.tensor
        def _(pe):
            pe.wait_ge(sem("ident_ready"), 1)
            pe.wait_ge(sem("const"), 6)
            pe.wait_ge(sem("cum_ready"), 1)
            pe.matmul(ps[6][:, 0:T + 2], ones[0:EP, :], cum, start=True, stop=True).then_inc(sem("tot_mm"), 1)
            pe.matmul(ps[7][:, 0:T + 2], before[0:EP, :], cum, start=True, stop=True).then_inc(sem("tot_mm"), 1)

            def tile_of(v, t):
                return v[:, bass.ds(t, 1), :].rearrange("p a n -> p (a n)")

            def transpose_h(t, slot, stage, phase):
                pe.wait_ge(sem("tile_staged"), t + (phase + 1))
                for k in range(KD):
                    ins = pe.transpose(ps[slot][:, k * P:(k + 1) * P], stage[:, slot, k * P:(k + 1) * P], ident[:, :])
                ins.then_inc(sem("transposed"), 1)

            pe.wait_ge(sem("w_rel_in"), 32)

            def project(t, use, slot):
                if not (isinstance(t, int) and t == T - 1):
                    transpose_h(t + 1, 1 - slot, h_stage1, 0)
                pe.wait_ge(sem("hT_ready"), t + 1)
                for j in range(4):
                    if not (isinstance(t, int) and t == 0):
                        pe.wait_ge(sem("p_evac"), t * 4 + (j - 3))
                    for k in range(KD):
                        ins = pe.matmul(ps[2 + j][:, :], hT[:, slot, k, :], w_rel_mm[:, k, j * 512:(j + 1) * 512],
                                        start=k == 0, stop=k == KD - 1)
                    ins.then_inc(sem("p_mm"), 1)

            transpose_h(0, 0, h_stage1, 0)
            node_tiles(pe, project)

            pe.wait_ge(sem("param_in"), PARAMS * 16)
            for m in range(6):
                if m >= 2:
                    pe.wait_ge(sem("sage_done"), m - 1)
                for ki in range(KD):
                    for ko in range(KD):
                        c = (ki * KD + ko) * P
                        ins = pe.transpose(ps[m % 2][:, c:c + P], sage_raw[:, m, ko, ki * P:(ki + 1) * P], ident[:, :])
                ins.then_inc(sem("sage_tp"), 1)
            pe.wait_ge(sem("w_x_in"), 16)
            pe.wait_ge(sem("p_evac"), 4 * T)
            for k in range(KD):
                for g in range(HP):
                    ins = pe.transpose(ps[2 + k][:, g * P:(g + 1) * P], w_x[:, k, g * P:(g + 1) * P], ident[:, :])
                ins.then_inc(sem("wx_tp"), 1)
            pe.wait_ge(sem("wxT_ready"), KD)
            pe.wait_ge(sem("bx_ready"), 1)
            for k in range(KD):
                for g in range(HP):
                    ins = pe.matmul(ps[4 + k][:, g * P:(g + 1) * P], w_xT[:, g, k * P:(k + 1) * P], w_slice2,
                                    start=True, stop=True)
                ins.then_inc(sem("wc_mm"), 1)
            for g in range(HP):
                ins = pe.matmul(ps[3][:, g * P:(g + 1) * P], bx_rep[:, g, :], w_slice2, start=True, stop=True)
            ins.then_inc(sem("wc_mm"), 1)

            pe.wait_ge(sem("chosen_ready"), 1)
            pe.wait_ge(sem("edges_ready"), 1)
            for w in range(2):
                for k in range(EK):
                    ins = pe.matmul(ps[6 + w][:, 0:PAIRS], edges_v[:, k, :, w], chosen_v[:, k, :],
                                    start=k == 0, stop=k == EK - 1)
                ins.then_inc(sem("pairs_mm"), 1)

            def pair_sums(i, r, first):
                for k in range(RING):
                    t = r * PAIRS + (i * RING + k)
                    pe.wait_ge(sem("onehot_ready"), r * (PAIRS + 2) + (i * RING + k + 1))
                    if not (first and k < 4):
                        pe.wait_ge(sem("pair_added"), t - 3)
                    pe.wait_ge(sem(f"rows_in{k}"), r * (16 * ROUNDS) + (i * 16 + 16))
                    pe.matmul(ps[4 + k % 4][:, 0:D + 1], onehot[:, k % 4, :], rows[:, k, :],
                              start=True, stop=True).then_inc(sem("pair_done"), 1)

            def gather_edges(r):
                pair_sums(0, r, isinstance(r, int))
                with pe.Fori(1, ROUNDS) as i:
                    pair_sums(i, r, False)

            pe.wait_ge(sem("pair_tables"), 1)
            gather_edges(0)
            pe.wait_ge(sem("pair_added"), PAIRS)

            def column_mean(bank, v, done, last):
                pe.matmul(bank, inv_n[:, :], v[:, 0, 0:D], start=True, stop=False)
                with pe.Fori(1, T - 1) as t:
                    pe.matmul(bank, inv_n[:, :], tile_of(v, t)[:, 0:D], start=False, stop=False)
                pe.matmul(bank, inv_n[0:last, :], v[0:last, T - 1, 0:D], start=False, stop=True)\
                    .then_inc(sem(done), 1)

            column_mean(ps[4][:, 0:D], accv, "bn_mean", LAST)
            pe.wait_ge(sem("squared"), 1)
            column_mean(ps[5][:, 0:D], squares, "bn_var", LAST)
            pe.wait_ge(sem("wc_ready"), 1)

            def slice_sums(t, slot, rows_, start=False, stop=False):
                pe.wait_ge(sem("sw_ready"), t + 1)
                v = sw_stage[:, slot, :]
                x1 = tile_of(h, t)
                for g in range(HP):
                    ins = pe.matmul(ps[4 + g][:, 0:D + 1], v[0:rows_, g * P:(g + 1) * P], x1[0:rows_, :],
                                    start=start, stop=stop)
                ins.then_inc(sem("slices_mm"), 1)

            def scores(t, use, slot):
                if not (isinstance(t, int) and t == T - 1):
                    transpose_h(t + 1, 1 - slot, h_stage2, SCORES)
                pe.wait_ge(sem("hT_ready"), t + (SCORES + 1))
                if not first_use(t):
                    pe.wait_ge(sem("l_read"), t - 1)
                for k in range(KD):
                    ins = pe.matmul(ps[2 + slot][:, :], hT[:, slot, k, :], wc[:, k, :],
                                    start=k == 0, stop=k == KD - 1)
                ins.then_inc(sem("l_mm"), 1)
                if not first_use(t):
                    slice_sums(t - 2, slot, P, start=isinstance(t, int) and t == 2)

            transpose_h(0, 0, h_stage2, SCORES)
            scores(0, 0, 0)
            scores(1, 0, 1)
            scores(2, 1, 0)
            with pe.Fori(1, T // 2 - 1) as i:
                scores(2 * i + 1, i, 1)
                scores(2 * i + 2, i + 1, 0)
            scores(T - 2, T // 2 - 1, 1)
            scores(T - 1, T // 2, 0)
            slice_sums(T - 2, 1, P)
            slice_sums(T - 1, 0, LAST, stop=True)

            pe.wait_ge(sem("tn_ready"), 1)
            for k in range(KD):
                for g in range(HP):
                    ins = pe.transpose(ps[k][:, g * P:(g + 1) * P], tn[:, g, k * P:(k + 1) * P], ident[:, :])
                ins.then_inc(sem("tn_tp"), 1)
            for g in range(HP):
                ins = pe.transpose(ps[2][0:1, g * P:(g + 1) * P], tn[:, g, D:D + 1], ident[:, :])
            ins.then_inc(sem("tn_tp"), 1)
            pe.wait_ge(sem("s_evac"), 3)
            pe.wait_ge(sem("b_fx_in"), 16)
            for a_ in range(HEADS):
                c = slice(a_ * HD, (a_ + 1) * HD)
                for k in range(KD):
                    pe.matmul(ps[3][0:HD, c], w_fx[:, k, c], tnT[:, k, c], start=k == 0, stop=False)
                ins = pe.matmul(ps[3][0:HD, c], b_fx[0:1, c], norm_row[0:1, c], start=False, stop=True)
            ins.then_inc(sem("st_mm"), 1)
            pe.wait_ge(sem("s_evac"), 4)
            pe.matmul(ps[0][0:HD, :], w_q, slice_t, start=True, stop=True).then_inc(sem("qkv_mm"), 1)
            pe.matmul(ps[1][0:HD, :], w_k, slice_t, start=True, stop=True).then_inc(sem("qkv_mm"), 1)
            for a_ in range(HEADS):
                c = slice(a_ * HD, (a_ + 1) * HD)
                ins = pe.matmul(ps[2][0:HD, c], slice_t[:, c], w_v, start=True, stop=True)
            ins.then_inc(sem("qkv_mm"), 1)
            pe.wait_ge(sem("s_evac"), 7)
            for a_ in range(HEADS):
                c = slice(a_ * HD, (a_ + 1) * HD)
                ins = pe.matmul(ps[3][0:HD, c], q_t[:, c], k_t[:, c], start=True, stop=True)
            ins.then_inc(sem("attn_mm"), 1)
            pe.wait_ge(sem("attn_ready"), 1)
            for a_ in range(HEADS):
                c = slice(a_ * HD, (a_ + 1) * HD)
                ins = pe.transpose(ps[4][0:HD, c], attn[:, c], ident[0:HD, 0:HD])
            ins.then_inc(sem("attn_tp"), 1)
            pe.wait_ge(sem("s_evac"), 8)
            for a_ in range(HEADS):
                c = slice(a_ * HD, (a_ + 1) * HD)
                ins = pe.matmul(ps[5][0:HD, c], v_s[:, c], attn_t[:, c], start=True, stop=True)
            ins.then_inc(sem("o_mm"), 1)
            pe.wait_ge(sem("s_evac"), 9)
            for g in range(HP):
                for b in range(2):
                    a_ = 2 * g + b
                    ins = pe.matmul(ps[g][0:HD, b * D:(b + 1) * D], o_t[:, a_ * HD:(a_ + 1) * HD], w_out[:, a_, :],
                                    start=True, stop=True)
                ins.then_inc(sem("m_mm"), 1)
            pe.wait_ge(sem("mid_even"), HP)
            pe.wait_ge(sem("odd_heads"), 1)
            pe.wait_ge(sem("mid_moved"), 16)

            def transpose_sw(t, slot):
                pe.wait_ge(sem("tile_staged"), t + (SPREAD + 1))
                for g in range(HP):
                    ins = pe.transpose(ps[slot][:, g * P:(g + 1) * P], sw_stage[:, slot, g * P:(g + 1) * P],
                                       ident[:, :])
                ins.then_inc(sem("transposed"), 1)

            def spread(t, use, slot):
                if not (isinstance(t, int) and t == T - 1):
                    transpose_sw(t + 1, 1 - slot)
                pe.wait_ge(sem("hT_ready"), t + (SPREAD + 1))
                if not first_use(t):
                    pe.wait_ge(sem("o_added"), t - 1)
                for g in range(HP):
                    ins = pe.matmul(ps[4 + slot][:, 0:D], hT[:, slot, g, :], mid[:, g, :],
                                    start=g == 0, stop=g == HP - 1)
                ins.then_inc(sem("spread_mm"), 1)

            transpose_sw(0, 0)
            node_tiles(pe, spread)
            with pe.Fori(1, LAYERS + 1) as r:
                gather_edges(r)
                b = (r - 1) * T

                def transposes(t, slot):
                    pe.wait_ge(sem("agg_ready"), b + (t + 1))
                    pe.wait_ge(sem("tile_staged"), b + (t + (SAGE + 1)))
                    for q in range(4):
                        ins = pe.transpose(ps[slot][:, q * P:(q + 1) * P], stage4[:, slot, q * P:(q + 1) * P],
                                           ident[:, :])
                    ins.then_inc(sem("transposed"), 1)

                def layer_tile(t, use, slot):
                    if not (isinstance(t, int) and t == T - 1):
                        transposes(t + 1, 1 - slot)
                    pe.wait_ge(sem("hT_ready"), b + (t + (SAGE + 1)))
                    if not first_use(t):
                        pe.wait_ge(sem("elu_read"), b + (t - 1))
                    for q in range(4):
                        w = sage_w[:, bass.ds((r - 1) * 4 + q, 1), :].rearrange("p a d -> p (a d)")
                        ins = pe.matmul(ps[2 + slot][:, 0:D], hT[:, slot, q, :], w, start=q == 0, stop=q == 3)
                    ins.then_inc(sem("g_mm"), 1)

                transposes(0, 0)
                node_tiles(pe, layer_tile)
            def gate_tile(t, use, slot):
                if not (isinstance(t, int) and t == T - 1):
                    transpose_h(t + 1, 1 - slot, stage4, GATE)
                pe.wait_ge(sem("hT_ready"), t + (GATE + 1))
                for k in range(KD):
                    ins = pe.matmul(ps[7][:, bass.ds(t * X16, X16)], hT[:, slot, k, :], gate_w[:, k, :],
                                    start=k == 0, stop=k == KD - 1)
                ins.then_inc(sem("gate_mm"), 1)

            transpose_h(0, 0, stage4, GATE)
            node_tiles(pe, gate_tile)
            pe.wait_ge(sem("counts_ready"), 1)
            pe.matmul(ps[6][:, 0:X16], ones[:, :], counts, start=True, stop=True).then_inc(sem("counts_mm"), 1)
            pe.matmul(ps[6][:, 32:32 + X16], before[:, :], counts, start=True, stop=True)\
                .then_inc(sem("counts_mm"), 1)

            def transpose_tokens(c, use, k16, slot):
                pe.wait_ge(sem(f"rows_in{k16}"), scattered(k16) + 16 + use * 16)
                for k in range(KD):
                    ins = pe.transpose(ps[slot][:, k * P:(k + 1) * P], rows[:, k16, k * P:(k + 1) * P], ident[:, :])
                ins.then_inc(sem("x_used"), 1)

            def expert(c, use, j, last=False):
                slot = j % 2
                pe.wait_ge(sem(f"expert_in{slot}"), use * (64 * RING // 2) + 64 * (j // 2 + 1))
                pe.wait_ge(sem("hT_ready"), c + (EXPERTS + 1))
                for f in range(KF):
                    for k in range(KD):
                        ins = pe.matmul(hid_bank(slot, f), w1[:, slot, k, f * P:(f + 1) * P],
                                        hT[:, slot, k, :], start=k == 0, stop=k == KD - 1)
                    ins.then_inc(sem("hid_mm"), 1)
                if not last:
                    transpose_tokens(c + 1, use + (j + 1) // RING, (j + 1) % RING, 1 - slot)
                if not (isinstance(use, int) and use == 0 and j < 2):
                    pe.wait_ge(sem("y_copied"), c - 1)
                pe.matmul(ps[4 + slot][:, 0:D], ones[0:1, :], b2_row[0:1, slot, :], start=True, stop=False)
                for f in range(KF):
                    pe.wait_ge(sem("hid_ready"), c * KF + (f + 1))
                    ins = pe.matmul(ps[4 + slot][:, 0:D], hidden[:, slot, f, :], w2[:, slot, f, :],
                                    start=False, stop=f == KF - 1)
                ins.then_inc(sem("y_done"), 1)

            transpose_tokens(0, 0, 0, 0)
            for j in range(RING):
                expert(j, 0, j)
            with pe.Fori(1, ETILES // RING - 1) as i:
                for j in range(RING):
                    expert(i * RING + j, i, j)
            use = ETILES // RING - 1
            for j in range(RING):
                expert(use * RING + j, use, j, last=j == RING - 1)

        @block.vector
        def _(dve):
            link = Chain(dve, sem("link"))

            dve.wait_ge(sem("const"), 6)
            link(dve.tensor_scalar(before[:, :], iota[:, 0:P], pidx[:, 0:1], None, ALU.is_gt))
            dve.tensor_scalar(ident[:, :], iota[:, 0:P], pidx[:, 0:1], None, ALU.is_equal).then_inc(sem("ident_ready"), 1)

            dve.wait_ge(sem("dst_in"), 48)
            blk_a = f_posi
            blk_b = f_pay.rearrange("p e w -> p (e w)")[:, 0:EF].bitcast(I32)
            link.mark(dve.tensor_scalar(blk_a, dst_a, 7, None, ALU.arith_shift_right))
            link(dve.tensor_scalar(blk_b, dst_b, 7, None, ALU.arith_shift_right))
            link(dve.tensor_tensor(junk, blk_a, blk_b, ALU.is_gt))
            link.mark(dve.tensor_reduce(cum[:, T + 1:T + 2], junk, AX, ALU.add))
            link(dve.tensor_copy(f_blk, blk_a))
            with link.loop(0, T + 1, 1) as b:
                dve_out = cum[:, bass.ds(b, 1)]
                link(dve.tensor_scalar(junk, f_blk, iota[0:EP, bass.ds(b, 1)], 0.0, ALU.is_lt, ALU.add,
                                       accum_out=dve_out))
            dve.sem_inc(sem("cum_ready"), 1)

            def normalise(src, dst, k):
                with link.loop(0, T, 1) as t:
                    link.mark(dve.bn_stats(bst[:, bass.ds(t, 1), :].rearrange("p a n -> p (a n)"),
                                           src[:, bass.ds(t, 1), 0:D].rearrange("p a n -> p (a n)")))
                link.settle()
                mean, var, half, tmp = mv[:, :, 0], mv[:, :, 1], nrm[:, 2, :], nrm[:, 3, :]
                link.mark(dve.tensor_tensor(mean, bst[:, :, 1], bst[:, :, 4], ALU.add))
                link.mark(dve.tensor_tensor(half, bst[:, :, 1], bst[:, :, 4], ALU.subtract))
                link(dve.tensor_tensor(var, bst[:, :, 2], bst[:, :, 5], ALU.add))
                link.mark(dve.tensor_scalar(mean, mean, 0.5, None, ALU.mult))
                link.mark(dve.tensor_scalar(var, var, 1.0 / D, None, ALU.mult))
                link(dve.scalar_tensor_tensor(tmp, half, 0.25, half, ALU.mult, ALU.mult))
                link(dve.tensor_tensor(var, var, tmp, ALU.add))
                dve.sem_inc(sem("var_ready"), 1)
                link(dve.tensor_scalar(nrm[:, 1, :], mv[:, :, 1], EPS, None, ALU.add))
                dve.wait_ge(sem("sd_ready"), k + 1)
                refine(nrm[:, 0, :], nrm[:, 1, :], nrm[:, 2, :], nrm[:, 3, :])
                with dve.Fori(0, T) as t:
                    dve.tensor_scalar(dst[:, bass.ds(t, 1), 0:D].rearrange("p a n -> p (a n)"),
                                      src[:, bass.ds(t, 1), 0:D].rearrange("p a n -> p (a n)"),
                                      mv[:, bass.ds(t, 1), 0:1].rearrange("p a n -> p (a n)"),
                                      nrm[:, 2, bass.ds(t, 1)], ALU.subtract, ALU.mult).then_inc(sem("h_ready"), 1)
                dve.wait_ge(sem("h_ready"), (k + 1) * T)

            def refine(sd, v, y, tmp):
                link(dve.reciprocal(y, sd))
                link(dve.tensor_tensor(tmp, y, y, ALU.mult))
                link(dve.tensor_tensor(tmp, tmp, v, ALU.mult))
                link(dve.tensor_scalar(tmp, tmp, -0.5, 1.5, ALU.mult, ALU.add))
                link(dve.tensor_tensor(y, y, tmp, ALU.mult))

            dve.wait_ge(sem("x_in"), 32)
            normalise(x, h, 0)

            dve.wait_ge(sem("tot_mm"), 2)
            tot, pre, cf, np_, ps_, dl, dd = (small_f[:, j, 0:T + 2] for j in range(7))
            link.mark(dve.tensor_copy(tot, ps[6][:, 0:T + 2]))
            link(dve.tensor_copy(pre, ps[7][:, 0:T + 2]))
            dve.tensor_copy(flag[:, :], tot[:, T + 1:T + 2]).then_inc(sem("flag_ready"), 1)
            dve.wait_ge(sem("flag_ready"), 1)

            late = dve.value_load(flag[0:1, 0:1], min_val=0, max_val=E)
            n_before = link.n
            flink = Chain(dve, sem("flink"))
            with dve.If(late > 0):
                off = small_f[0:EP, 7, 0:T]
                dve.wait_ge(sem("spare_in"), 32)
                flink(dve.tensor_tensor(off, pre[0:EP, 1:T + 1], pre[0:EP, 0:T], ALU.subtract))
                flink(dve.tensor_tensor(off, off, tot[0:EP, 0:T], ALU.add))
                flink(dve.tensor_scalar(off, off, -1.0, None, ALU.add))
                flink(dve.memset(junk, 1.0))
                flink(dve.memset(f_pos, 0.0))
                with flink.loop(0, T, 4) as b:
                    flink(dve.tensor_scalar(f_m, f_blk, iota[0:EP, bass.ds(b, 1)], None, ALU.is_equal))
                    flink(dve.tensor_tensor_scan(f_s, junk, f_m, 0.0, ALU.mult, ALU.add))
                    flink(dve.scalar_tensor_tensor(f_s, f_s, off[:, bass.ds(b, 1)], f_m, ALU.add, ALU.mult))
                    flink(dve.tensor_tensor(f_pos, f_pos, f_s, ALU.add))
                flink(dve.tensor_copy(f_posi, f_pos))
                flink(dve.tensor_copy(f_m, src_a))
                flink(dve.scalar_tensor_tensor(f_pay[:, :, 0], f_m, float(R), rel_a, ALU.mult, ALU.add))
                flink(dve.tensor_copy(f_pay[:, :, 1], dst_a))
                dve.sem_inc(sem("f_ready"), 1)
            assert link.n == n_before
            dve.wait_ge(sem("edge_in"), 9 * 16)
            ev = edges.rearrange("p (n w) -> p n w", w=2)
            link(dve.tensor_copy(ev[:, :, 1], edge_int))
            link(dve.tensor_copy(ev[:, :, 0], edge_src))
            link(dve.scalar_tensor_tensor(ev[:, :, 0], ev[:, :, 0], float(R), edge_rel, ALU.mult, ALU.add))
            dve.sem_inc(sem("edges_float"), 1)

            first, last_, seg = (small_i[:, j, 0:T + 1] for j in range(3))
            link.mark(dve.tensor_copy(seg, tot[:, 0:T + 1]))
            link(dve.tensor_scalar(cf[:, 0:T], tot[:, 1:T + 1], -1.0, None, ALU.add))
            link(dve.tensor_copy(last_[:, 0:T], cf[:, 0:T]))
            link.mark(dve.tensor_scalar(first, seg, 7, None, ALU.arith_shift_right))
            link(dve.tensor_scalar(last_[:, 0:T], last_[:, 0:T], 7, None, ALU.arith_shift_right))
            link.mark(dve.tensor_copy(cf[:, 0:T], first[:, 0:T]))
            link(dve.tensor_copy(np_[:, 0:T], last_[:, 0:T]))
            link(dve.tensor_tensor(np_[:, 0:T], np_[:, 0:T], cf[:, 0:T], ALU.subtract))
            link.mark(dve.tensor_scalar(np_[:, 0:T], np_[:, 0:T], 1.0, None, ALU.add))
            link(dve.tensor_tensor(dd[:, 0:T], tot[:, 1:T + 1], tot[:, 0:T], ALU.is_gt))
            link(dve.tensor_tensor(np_[:, 0:T], np_[:, 0:T], dd[:, 0:T], ALU.mult))
            link.mark(dve.memset(ps_[:, 0:1], 0.0))
            link(dve.tensor_tensor_scan(ps_[:, 1:T + 1], ones[:, 0:T], np_[:, 0:T], 0.0, ALU.mult, ALU.add))
            link.mark(dve.tensor_tensor(dl[:, 0:T], cf[:, 0:T], ps_[:, 0:T], ALU.subtract))
            link(dve.memset(dl[:, T:T + 1], 0.0))
            link(dve.tensor_tensor(dd[:, 1:T + 1], dl[:, 1:T + 1], dl[:, 0:T], ALU.subtract))
            link.mark(dve.tensor_scalar(pair_c, iota[:, 0:PAIRS], dl[:, 0:1], None, ALU.add))
            link(dve.memset(pair_b, 0.0))
            tm = pair_dst[:, 0:PAIRS]
            with link.loop(1, T + 1, 3) as b:
                link(dve.tensor_scalar(tm, iota[:, 0:PAIRS], ps_[:, bass.ds(b, 1)], None, ALU.is_ge))
                link.mark(dve.scalar_tensor_tensor(pair_c, tm, dd[:, bass.ds(b, 1)], pair_c, ALU.mult, ALU.add))
                link(dve.tensor_tensor(pair_b, pair_b, tm, ALU.add))
            link.mark(dve.tensor_copy(pair_tile[:, :], pair_b))
            link(dve.tensor_scalar(pair_c, pair_c, float(EC - 1), None, ALU.min))
            for k in range(EK):
                link.mark(dve.tensor_scalar(chosen_v[:, k, :], pair_c, pidx[:, k:k + 1], None, ALU.is_equal))
            link.settle()
            dve.sem_inc(sem("chosen_ready"), 1)

            dve.wait_ge(sem("param_in"), PARAMS * 16)
            dve.wait_ge(sem("edges_ready"), 1)
            dve.wait_ge(sem("proj_stored0"), 16 * (T // 2 + 1))
            dve.wait_ge(sem("proj_stored1"), 16 * (T // 2))
            for g in range(HP):
                link.mark(dve.tensor_scalar(bx_rep[:, g, :], ones[:, :], bx_col[:, g:g + 1], None, ALU.mult))
            link(dve.tensor_scalar(temp_b, temp_b, 0.1, 5.0, ALU.max, ALU.min))
            link(dve.reciprocal(temp_b, temp_b))
            dve.sem_inc(sem("bx_ready"), 1)
            tb = temp_b.unsqueeze(2).to_broadcast([P, HEADS, HD])
            for k in range(KD):
                dve.wait_ge(sem("wc_mm"), k + 1)
                link.mark(dve.tensor_tensor(wc[:, k, :].rearrange("p (a n) -> p a n", a=HEADS),
                                            ps[4 + k][:, :].rearrange("p (a n) -> p a n", a=HEADS), tb, ALU.mult))
            dve.wait_ge(sem("wc_mm"), 3)
            bcv = bc[:, :].rearrange("p (a n) -> p a n", a=HEADS)
            link(dve.tensor_tensor(bcv, ps[3][:, :].rearrange("p (a n) -> p a n", a=HEADS),
                                   bslice_b.unsqueeze(1).to_broadcast([P, HEADS, HD]), ALU.add))
            link(dve.tensor_tensor(bcv, bcv, tb, ALU.mult))
            dve.sem_inc(sem("wc_ready"), 1)

            dve.wait_ge(sem("pairs_mm"), 2)
            link.mark(dve.tensor_copy(pair_row0[:, :], ps[6][:, 0:PAIRS]))
            link.mark(dve.memset(pair_dst[:, PAIRS:PAIRS + 2], -1.0))
            link(dve.scalar_tensor_tensor(pair_dst[:, 0:PAIRS], pair_b, -float(P), ps[7][:, 0:PAIRS], ALU.mult, ALU.add))
            link(dve.tensor_scalar(pair_row[:, :], pair_row0[:, :], 3, None, ALU.arith_shift_right))
            dve.sem_inc(sem("pair_tables"), 1)

            def build_onehot(t, base, k):
                dve.tensor_scalar(onehot[:, k % 4, :], iota[:, 0:P], pair_dst[:, bass.ds(t, 1)], None, ALU.is_equal)\
                    .then_inc(sem("onehot_ready"), 1)

            def add_pairs(i, r, first):
                for k in range(RING):
                    t = i * RING + k
                    g = r * PAIRS + t
                    build_onehot(t + 2, 0, k + 2)
                    b = dve.value_load(pair_tile[0:1, bass.ds(t, 1)], min_val=0, max_val=T)
                    if not (first and k == 0):
                        dve.wait_ge(sem("pair_added"), g)
                    dve.wait_ge(sem("pair_done"), g + 1)
                    v = accv[:, bass.ds(b, 1), :].rearrange("p a n -> p (a n)")
                    dve.tensor_tensor(v, v, ps[4 + k % 4][:, 0:D + 1], ALU.add).then_inc(sem("pair_added"), 1)

            def gather_edges(r):
                link(dve.memset(acc[:, :], 0.0))
                for k in range(2):
                    build_onehot(k, 0, k)
                add_pairs(0, r, isinstance(r, int))
                with dve.Fori(1, ROUNDS) as i:
                    add_pairs(i, r, False)

            gather_edges(0)
            dve.wait_ge(sem("pair_added"), PAIRS)
            dve.wait_ge(sem("bn_mean"), 1)
            g3 = accv[:, 0:T, 0:D]
            link.mark(dve.tensor_copy(col[:, 1, :], ps[4][:, 0:D]))
            link.settle()
            link(dve.tensor_tensor(g3, g3, col[:, 1:2, :].to_broadcast([P, T, D]), ALU.subtract))
            dve.sem_inc(sem("centred"), 1)
            dve.wait_ge(sem("bn_sd"), 1)
            link(dve.tensor_scalar(col[:, 1, :], ps[5][:, 0:D], EPS, None, ALU.add))
            refine(col[:, 0, :], col[:, 1, :], col[:, 2, :], col[:, 3, :])
            link(dve.tensor_tensor(col[:, 2, :], col[:, 2, :], gamma_b, ALU.mult))
            link(dve.tensor_tensor(g3, g3, col[:, 2:3, :].to_broadcast([P, T, D]), ALU.mult))
            link(dve.tensor_tensor(x[:, :, :], x[:, :, :], g3, ALU.add))
            link(dve.tensor_tensor(x[:, :, :], x[:, :, :], beta_b.unsqueeze(1).to_broadcast([P, T, D]), ALU.add))
            normalise(x, h, 1)
            per = 4

            def softmax_tile(t, use, slot):
                v = swv[:, bass.ds(t, 1), :].rearrange("p a n -> p (a n)")
                v3 = v.rearrange("p (a n) -> p a n", a=HEADS)
                mx = soft[:, slot * 8:slot * 8 + 8]
                dve.wait_ge(sem("l_mm"), t + 1)
                dve.tensor_tensor(v, ps[2 + slot][:, :], bc[:, :], ALU.add).then_inc(sem("l_read"), 1)
                dve.wait_ge(sem("l_read"), t + 1)
                dve.nop(nofuse=True)
                link(dve.tensor_reduce(mx, v3, AX, ALU.max))
                dve.tensor_tensor(v3, v3, mx.unsqueeze(2).to_broadcast([P, HEADS, HD]), ALU.subtract)\
                    .then_inc(sem("l_shifted"), 1)

            def weights_tile(t, use, slot):
                v = swv[:, bass.ds(t, 1), :].rearrange("p a n -> p (a n)")
                v3 = v.rearrange("p (a n) -> p a n", a=HEADS)
                rs = soft[:, 16 + slot * 8:24 + slot * 8]
                dve.wait_ge(sem("l_exp"), t + 1)
                dve.nop(nofuse=True)
                link(dve.tensor_reduce(rs, v3, AX, ALU.add))
                link(dve.reciprocal(rs, rs))
                if not first_use(t):
                    dve.wait_ge(sem("slices_mm"), t - 1)
                    dve.wait_ge(sem("sw_kept"), t - 1)
                dve.tensor_tensor(sw_stage[:, slot, :].rearrange("p (a n) -> p a n", a=HEADS), v3,
                                  rs.unsqueeze(2).to_broadcast([P, HEADS, HD]), ALU.mult).then_inc(sem("sw_ready"), 1)

            softmax_tile(0, 0, 0)
            softmax_tile(1, 0, 1)
            weights_tile(0, 0, 0)
            softmax_tile(2, 0, 0)
            weights_tile(1, 0, 1)
            with link.loop(1, T // 2, 6) as i:
                softmax_tile(2 * i + 1, i, 1)
                weights_tile(2 * i, i, 0)
                softmax_tile(2 * i + 2, i, 0)
                weights_tile(2 * i + 1, i, 1)
            weights_tile(T - 1, 0, 0)
            dve.wait_ge(sem("sw_ready"), T)

            dve.wait_ge(sem("slices_mm"), T)
            dve.wait_ge(sem("sw_kept"), T)
            for g in range(HP):
                link.mark(dve.tensor_scalar(hs[:, g:g + 1], ps[4 + g][:, D:D + 1], EPS, None, ALU.add))
            link.settle()
            link(dve.reciprocal(hs[:, 4:4 + HP], hs[:, 0:HP]))
            for g in range(HP):
                link.mark(dve.tensor_scalar(tn[:, g, :], ps[4 + g][:, 0:D + 1], hs[:, 4 + g:5 + g], None, ALU.mult))
            link.settle()
            dve.sem_inc(sem("tn_ready"), 1)
            dve.wait_ge(sem("attn_mm"), 1)
            av = attn.rearrange("p (a n) -> p a n", a=HEADS)
            sv = ps[3][0:HD, :].rearrange("p (a n) -> p a n", a=HEADS)
            mx, rs = soft[0:HD, 0:8], soft[0:HD, 8:16]
            link(dve.tensor_reduce(mx, sv, AX, ALU.max))
            link(dve.tensor_tensor(av, sv, mx.unsqueeze(2).to_broadcast([HD, HEADS, HD]), ALU.subtract))
            dve.sem_inc(sem("attn_shifted"), 1)
            dve.wait_ge(sem("attn_exp"), 1)
            link(dve.tensor_reduce(rs, av, AX, ALU.add))
            link(dve.reciprocal(rs, rs))
            link(dve.tensor_tensor(av, av, rs.unsqueeze(2).to_broadcast([HD, HEADS, HD]), ALU.mult))
            dve.sem_inc(sem("attn_ready"), 1)

            def add_spread(t, use, slot):
                v = x[:, bass.ds(t, 1), :].rearrange("p a n -> p (a n)")
                dve.wait_ge(sem("spread_mm"), t + 1)
                dve.tensor_tensor(v, v, ps[4 + slot][:, 0:D], ALU.add).then_inc(sem("o_added"), 1)

            node_tiles(dve, add_spread)
            dve.wait_ge(sem("o_added"), T)
            link(dve.tensor_tensor(x[:, :, :], x[:, :, :], bout_b.unsqueeze(1).to_broadcast([P, T, D]), ALU.add))
            normalise(x, h, 2)
            rdeg = nrm[:, 2, :]
            with link.loop(1, LAYERS + 1, 3) as r:
                gather_edges(r)
                dve.wait_ge(sem("pair_added"), r * PAIRS + PAIRS)
                b = (r - 1) * T
                link(dve.tensor_scalar(rdeg, accv[:, 0:T, D], 1.0, None, ALU.max))
                link(dve.reciprocal(rdeg, rdeg))

                def aggregate(t, slot):
                    if not first_use(t):
                        dve.wait_ge(sem("transposed"), b + (t + (SAGE - 1)))
                    dve.tensor_scalar(stage4[:, slot, 0:D], accv[:, bass.ds(t, 1), 0:D].rearrange("p a n -> p (a n)"),
                                      rdeg[:, bass.ds(t, 1)], None, ALU.mult).then_inc(sem("agg_ready"), 1)

                def elu_in(t, use, slot):
                    dve.wait_ge(sem("g_mm"), b + (t + 1))
                    if not first_use(t):
                        dve.wait_ge(sem("layer_out"), b + (t - 1))
                    dve.tensor_tensor(elu_v[:, slot], ps[2 + slot][:, 0:D],
                                      bl_b[:, bass.ds(r - 1, 1), :].rearrange("p a n -> p (a n)"), ALU.add)\
                        .then_inc(sem("elu_read"), 1)
                    dve.wait_ge(sem("elu_read"), b + (t + 1))
                    dve.tensor_scalar(elu_n[:, slot], elu_v[:, slot], 0.0, None, ALU.min)\
                        .then_inc(sem("elu_neg"), 1)

                def elu_out(t, use, slot):
                    dve.wait_ge(sem("elu_exp"), b + (t + 1))
                    dve.scalar_tensor_tensor(elu_v[:, slot], elu_v[:, slot], 0.0, elu_e[:, slot], ALU.max, ALU.add)\
                        .then_inc(sem("elu_sum"), 1)
                    dve.wait_ge(sem("elu_sum"), b + (t + 1))
                    dve.tensor_scalar(h[:, bass.ds(t, 1), 0:D].rearrange("p a n -> p (a n)"), elu_v[:, slot],
                                      -1.0, None, ALU.add).then_inc(sem("layer_out"), 1)

                aggregate(0, 0)
                aggregate(1, 1)
                elu_in(0, 0, 0)
                with dve.Fori(0, T // 2 - 1) as i:
                    aggregate(2 * i + 2, 0)
                    elu_in(2 * i + 1, i, 1)
                    elu_out(2 * i, i, 0)
                    aggregate(2 * i + 3, 1)
                    elu_in(2 * i + 2, i, 0)
                    elu_out(2 * i + 1, i, 1)
                aggregate(T - 1, 0)
                elu_in(T - 2, 0, 1)
                elu_out(T - 3, 0, 0)
                elu_in(T - 1, 0, 0)
                elu_out(T - 2, 0, 1)
                elu_out(T - 1, 0, 0)
            dve.wait_ge(sem("layer_out"), LAYERS * T)
            link(dve.tensor_tensor(x[:, :, :], x[:, :, :], h[:, :, 0:D], ALU.add))
            dve.sem_inc(sem("layers_done"), 1)
            dve.wait_ge(sem("nodes_stored"), 16 * LAYERS)
            normalise(x, h, 3)
            dve.wait_ge(sem("gate_mm"), T)
            link(dve.tensor_tensor(logits, ps[7][:, 0:T * X16].rearrange("p (t e) -> p t e", t=T),
                                   gb_b.unsqueeze(1).to_broadcast([P, T, X16]), ALU.add))

            for t in range(T):
                link.mark(dve.max(top8[:, t, :], logits[:, t, :]))
            link.settle()
            for t in range(T):
                link.mark(dve.max_index(at8[:, t, :], top8[:, t, :], logits[:, t, :]))
            link.mark(dve.tensor_tensor(gate_t[:, 0, :], top8[:, :, 1], top8[:, :, 0], ALU.subtract))
            link.settle()
            dve.sem_inc(sem("gate_diff"), 1)
            ent3 = ent.rearrange("p (t k) -> p t k", k=TOPK)
            link.mark(dve.tensor_scalar(hs[:, 8:9], pidx[:, 0:1], float(LAST), 99.0, ALU.is_ge, ALU.mult))
            link(dve.tensor_copy(ent3, at8[:, :, 0:TOPK]))
            link(dve.tensor_scalar(ent3[:, T - 1, :], ent3[:, T - 1, :], hs[:, 8:9], None, ALU.add))
            with link.loop(0, X16, 1) as e:
                link(dve.tensor_scalar(ent_m, ent, iota[:, bass.ds(e, 1)], 0.0, ALU.is_equal, ALU.add,
                                       accum_out=counts[:, bass.ds(e, 1)]))
            dve.sem_inc(sem("counts_ready"), 1)
            dve.wait_ge(sem("gate_exp"), 1)
            link(dve.tensor_scalar(gate_t[:, 2, :], gate_t[:, 1, :], 1.0, None, ALU.add))
            link(dve.reciprocal(gates[:, :, 0], gate_t[:, 2, :]))
            link(dve.tensor_tensor(gates[:, :, 1], gates[:, :, 0], gate_t[:, 1, :], ALU.mult))
            dve.wait_ge(sem("counts_mm"), 2)
            nt, ts, off = (small_f[:, j, 0:X16] for j in range(3))
            nti = small_i[:, 0, 0:X16]
            link(dve.tensor_scalar(nt, ps[6][:, 0:X16], float(P - 1), None, ALU.add))
            link(dve.tensor_copy(nti, nt))
            link(dve.tensor_scalar(nti, nti, 7, None, ALU.arith_shift_right))
            link(dve.tensor_copy(nt, nti))
            link(dve.tensor_tensor_scan(ts, ones[:, 0:X16], nt, 0.0, ALU.mult, ALU.add))
            link(dve.tensor_tensor(ts, ts, nt, ALU.subtract))
            link(dve.scalar_tensor_tensor(off, ts, float(P), ps[6][:, 32:32 + X16], ALU.mult, ALU.add))
            link.mark(dve.tensor_scalar(off, off, -1.0, None, ALU.add))
            link(dve.tensor_tensor(cmp_e, iota[:, 0:ETILES].unsqueeze(2).to_broadcast([P, ETILES, X16 - 1]),
                                   ts[:, 1:X16].unsqueeze(1).to_broadcast([P, ETILES, X16 - 1]), ALU.is_ge))
            link(dve.tensor_reduce(tile_x, cmp_e, AX, ALU.add))
            link(dve.tensor_copy(tile_xi, tile_x))
            dve.sem_inc(sem("tile_experts"), 1)
            link(dve.memset(ent_pos, 0.0))
            with link.loop(0, X16, 4) as e:
                link(dve.tensor_scalar(ent_m, ent, iota[:, bass.ds(e, 1)], None, ALU.is_equal))
                link(dve.tensor_tensor_scan(ent_s, ones[:, 0:ENTRIES], ent_m, 0.0, ALU.mult, ALU.add))
                link(dve.scalar_tensor_tensor(ent_s, ent_s, off[:, bass.ds(e, 1)], ent_m, ALU.add, ALU.mult))
                link(dve.tensor_tensor(ent_pos, ent_pos, ent_s, ALU.add))
            link(dve.tensor_copy(ent_posi, ent_pos))
            shift = ETILES.bit_length() - 1
            assert 1 << shift == ETILES
            link.mark(dve.tensor_scalar(ent_row, ent_posi, P - 1, shift, ALU.bitwise_and, ALU.logical_shift_left))
            link(dve.tensor_scalar(ent_row2, ent_posi, 7, None, ALU.arith_shift_right))
            link(dve.tensor_tensor(ent_row, ent_row, ent_row2, ALU.bitwise_or))
            dve.sem_inc(sem("places"), 1)

            def copy_y(c, use, slot):
                dve.wait_ge(sem("y_done"), c + 1)
                if not first_use(c):
                    dve.wait_ge(sem(f"y_stored{slot}"), 16 * use)
                dve.tensor_copy(y_out[:, slot], ps[4 + slot][:, 0:D]).then_inc(sem("y_copied"), 1)

            copy_y(0, 0, 0)
            copy_y(1, 0, 1)
            with dve.Fori(1, ETILES // 2) as i:
                copy_y(2 * i, i, 0)
                copy_y(2 * i + 1, i, 1)


            def combine(i, n):
                for k in range(n):
                    j = i * RING + k
                    t = i * (RING // TOPK) + k // TOPK
                    v = h[:, bass.ds(t, 1), 0:D].rearrange("p a n -> p (a n)")
                    w = gates[:, bass.ds(t, 1), k % TOPK:k % TOPK + 1].rearrange("p a n -> p (a n)")
                    dve.wait_ge(sem(f"rows_in{k}"), scattered(k) + 16 * (ETILES // RING) + (i * 16 + 16))
                    if not (isinstance(i, int) and i == 0 and k == 0):
                        dve.wait_ge(sem("combined"), j)
                    dve.scalar_tensor_tensor(v, rows[:, k, 0:D], w, v, ALU.mult, ALU.add)\
                        .then_inc(sem("combined"), 1)

            combine(0, RING)
            with dve.Fori(1, 3) as i:
                combine(i, RING)
            combine(3, TOPK)
            dve.wait_ge(sem("combined"), ENTRIES)
            normalise(h, h, 4)
            hv = h[:, :, 0:D]
            link(dve.tensor_tensor(hv, hv, gf_b.unsqueeze(1).to_broadcast([P, T, D]), ALU.mult))
            link(dve.tensor_tensor(hv, hv, bf_b.unsqueeze(1).to_broadcast([P, T, D]), ALU.add))
            link(dve.tensor_tensor(hv, hv, x[:, :, :], ALU.add))
            dve.sem_inc(sem("result_ready"), 1)


PARAMS = 6 + 10 + 1 + 3 + 3 + 1 + 2

_INPUTS = ["x", "src", "dst", "edge_type_8", "L0_gnn_weight", "L0_gnn_gamma", "L0_gnn_beta", "L0_ffn_W_fx",
           "L0_ffn_b_fx", "L0_ffn_W_x", "L0_ffn_b_x", "L0_ffn_W_slice", "L0_ffn_b_slice", "L0_ffn_W_q",
           "L0_ffn_W_k", "L0_ffn_W_v", "L0_ffn_W_out", "L0_ffn_b_out", "L0_ffn_temperature", "L1_gnn_Wl1",
           "L1_gnn_bl1", "L1_gnn_Wr1", "L1_gnn_Wl2", "L1_gnn_bl2", "L1_gnn_Wr2", "L1_gnn_Wl3", "L1_gnn_bl3",
           "L1_gnn_Wr3", "L1_ffn_gate_w", "L1_ffn_gate_b", "L1_ffn_w1", "L1_ffn_b1", "L1_ffn_w2", "L1_ffn_b2",
           "L1_ffn_gamma", "L1_ffn_beta"]


def kernel(**inputs):
    import numpy as np
    import concourse.bacc as bacc
    from concourse.bass_utils import run_bass_kernel_spmd

    nc = bacc.Bacc("TRN2", target_bir_lowering=False, num_devices=1)
    arrays, views = {}, {}
    for name in _INPUTS:
        a = np.ascontiguousarray(inputs[name])
        arrays[f"in_{name}"] = a
        views[name] = nc.dram_tensor(f"in_{name}", a.shape, mybir.dt.from_np(a.dtype), kind="ExternalInput").ap()
    out = nc.dram_tensor("out_0", (N, D), FP32, kind="ExternalOutput").ap()
    gnn_ffn_moe_program(nc, views, out)
    r = run_bass_kernel_spmd(nc, [arrays], core_ids=[0])
    return r.results[0]["out_0"]
```

```python
from contextlib import ExitStack, contextmanager

import concourse.bass as bass
from concourse import mybir

FP32 = mybir.dt.float32
I32 = mybir.dt.int32
U32 = mybir.dt.uint32
ALU = mybir.AluOpType
ACT = mybir.ActivationFunctionType
AX = mybir.AxisListType.X

P = 128
D = 256
KD = D // P
N = 3125
T = -(-N // P)
LAST = N - (T - 1) * P
NP = T * P
E = 50000
R = 8
EC = -(-E // P)
EK = -(-EC // P)
EP, EF = 125, 400
RING = 16
GROUP = RING // 2
UNROLL = 5
BATCH = 4
PAIRS = -(-(EC + T - 1) // RING) * RING
ROUNDS = PAIRS // RING
HEADS, HD = 8, 64
INNER = HEADS * HD
HP = INNER // P
SCALE = HD ** -0.5
LAYERS = 3
X16, FF, TOPK = 16, 512, 2
KF = FF // P
ENTRIES = T * TOPK
ETILES = (N * TOPK + X16 * (P - 1)) // P
EPS = 1e-5
assert T % UNROLL == 0
NOWHERE = -1.0e6


class Chain:

    def __init__(self, eng, sem):
        self.eng, self.sem, self.n, self.shift = eng, sem, 0, 0

    def mark(self, ins):
        ins.then_inc(self.sem, 1)
        self.n += 1

    def settle(self):
        self.eng.wait_ge(self.sem, self.n + self.shift)

    def __call__(self, ins):
        self.mark(ins)
        self.settle()

    @contextmanager
    def loop(self, start, end, per):
        before, at = self.shift, self.n
        with self.eng.Fori(start, end) as i:
            self.shift = (i - start) * per + before
            yield i
            assert self.n - at == per, (self.n - at, per)
        self.shift, self.n = before, at + per * (end - start)


def node_tiles(eng, body, chain=None, per=0):
    body(0, 0, 0)
    body(1, 0, 1)
    loop = chain.loop(1, T // 2, 2 * per) if chain else eng.Fori(1, T // 2)
    with loop as i:
        body(2 * i, i, 0)
        body(2 * i + 1, i, 1)
    body(T - 1, T // 2, 0)


def first_use(t):
    return isinstance(t, int) and t < 2


def gnn_ffn_moe_program(nc, A, out):
    ctx = ExitStack()
    sems = {}

    def sem(name):
        if name not in sems:
            sems[name] = ctx.enter_context(nc.semaphore(name))
        return sems[name]

    def sb(name, shape, dt=FP32):
        return ctx.enter_context(nc.sbuf_tensor(name, shape, dt))

    with ctx:
        projected = nc.dram_tensor("projected", (NP * R, D), FP32)
        nodes = nc.dram_tensor("nodes", (NP, D), FP32)
        in_order = nc.dram_tensor("in_order", (EC * P, 2), FP32)
        slots = nc.dram_tensor("slots", (P * ETILES, 1), I32)
        expert_rows = nc.dram_tensor("expert_rows", (ETILES * P, D), FP32)

        x = sb("x_res", [P, T, D])
        h = sb("h_now", [P, T, D + 1])
        acc = sb("acc", [P, (T + 1) * (D + 1)])
        accv = acc[:, :].rearrange("p (t d) -> p t d", d=D + 1)
        sw = sb("sw", [P, T * INNER])
        swv = sw[:, :].rearrange("p (t d) -> p t d", d=INNER)
        rows = sb("rows", [P, RING, D + 1])
        ident = sb("ident", [P, P])
        before = sb("before", [P, P])
        ones = sb("ones", [P, P])
        iota = sb("iota", [P, PAIRS + 2])
        pidx = sb("pidx", [P, EK])
        eps = sb("eps", [P, 1])
        onehot = sb("onehot", [P, 2 * BATCH, P])
        pair_dst = sb("pair_dst", [P, PAIRS + BATCH])
        pair_row0 = sb("pair_row0", [P, PAIRS], I32)
        pair_row = sb("pair_row", [P, PAIRS], I32)
        pair_tile = sb("pair_tile", [P, PAIRS], I32)
        staged = sb("staged", [P, 2, GROUP], I32)
        staged_tok = sb("staged_tok", [P, 2, GROUP], I32)
        pair_index = sb("pair_index", [P, 2, GROUP], I32)
        bst = sb("bst", [P, T, 6])
        mv = sb("mv", [P, T, 2])
        nrm = sb("nrm", [P, 4, T])
        hT = sb("hT", [P, 2, 4, P])
        wide = sb("wide", [P, 8, D])
        gamma_b, beta_b, bout_b, gf_b, bf_b = (wide[:, j, :] for j in range(5))
        bl_b = wide[:, 5:8, :]
        col = sb("col", [P, 4, D])
        w_fx = sb("w_fx", [P, KD, INNER])
        w_out = sb("w_out", [HD, HEADS, D])
        wc = sb("wc", [P, KD, INNER])
        bc = sb("bc", [P, INNER])
        sage_w = sb("sage_w", [P, LAYERS * 4, D])
        gate_w = sb("gate_w", [P, KD, X16])
        smalls = sb("smalls", [P, 640])
        small_i = sb("small_i", [P, 3, 32], I32)
        small_f = sb("small_f", [P, 10, 32])
        flag = sb("flag", [P, 1], I32)

        at = [0]

        def small(shape):
            n = 1
            for s in shape[1:]:
                n *= s
            v = smalls[0:shape[0], at[0]:at[0] + n]
            at[0] += n
            return v

        w_slice2 = small([P, P])
        w_q, w_k, w_v = (small([HD, HD]) for _ in range(3))
        bslice_b = small([P, HD])
        temp_b = small([P, HEADS])
        gb_b = small([P, X16])
        bx_col = small([P, HP])
        hs = small([P, 16])
        soft = small([P, 4 * HEADS])

        def carve(tile, start, shape, dt=FP32):
            n = 1
            for s in shape[1:]:
                n *= s
            v = tile[0:shape[0], start:start + n]
            return (v.bitcast(dt) if dt != FP32 else v), start + n

        dst_a, a = carve(acc, 0, [EP, EF], I32)
        dst_b, a = carve(acc, a, [EP, EF], I32)
        src_a, a = carve(acc, a, [EP, EF], I32)
        rel_a, a = carve(acc, a, [EP, EF], I32)
        junk, a = carve(acc, a, [EP, EF])
        edge_int, a = carve(acc, a, [P, EK * P], I32)
        edges, a = carve(acc, a, [P, EK * P * 2])
        chosen, a = carve(acc, a, [P, EK * PAIRS])
        pair_c, a = carve(acc, a, [P, PAIRS])
        pair_b, a = carve(acc, a, [P, PAIRS])
        assert a <= (T + 1) * (D + 1), a
        edges_v = edges.rearrange("p (k e w) -> p k e w", k=EK, w=2)
        chosen_v = chosen.rearrange("p (k t) -> p k t", k=EK)
        w_rel, a = carve(sw, 0, [P, KD * R * D])
        w_rel = w_rel.rearrange("p (k r o) -> p k r o", k=KD, r=R)
        w_rel_mm = sw[:, 0:KD * R * D].rearrange("p (k n) -> p k n", k=KD)
        proj, a = carve(sw, a, [P, 2 * R * D])
        proj = proj.rearrange("p (s n) -> p s n", s=2)
        edge_src, a = carve(sw, a, [P, EK * P], I32)
        edge_rel, a = carve(sw, a, [P, EK * P], I32)
        cum, a = carve(sw, a, [EP, T + 2])
        f_blk, a = carve(sw, a, [EP, EF])
        f_m, a = carve(sw, a, [EP, EF])
        f_s, a = carve(sw, a, [EP, EF])
        f_pos, a = carve(sw, a, [EP, EF])
        f_posi, a = carve(sw, a, [EP, EF], I32)
        f_pay, a = carve(sw, a, [EP, EF * 2])
        f_pay = f_pay.rearrange("p (e w) -> p e w", w=2)
        h_stage1, a = carve(sw, a, [P, 2 * D])
        h_stage1 = h_stage1.rearrange("p (s d) -> p s d", s=2)
        assert a <= T * INNER, a
        fone_idx = staged[0:EP, 0, 0:1]
        fone_pay = small_f[0:EP, 9, 0:2]
        squares = sw[:, 0:T * D].rearrange("p (t d) -> p t d", d=D)
        w_x, a = carve(sw, T * D, [P, KD * INNER])
        w_x = w_x.rearrange("p (k n) -> p k n", k=KD)
        w_xT, a = carve(sw, a, [P, HP * D])
        w_xT = w_xT.rearrange("p (g n) -> p g n", g=HP)
        bx_rep, a = carve(sw, a, [P, HP * P])
        bx_rep = bx_rep.rearrange("p (g n) -> p g n", g=HP)
        inv_n, a = carve(sw, a, [P, P])
        assert a <= T * INNER, a
        sage_raw = rows[:, :, :].rearrange("p a b -> p (a b)")[:, 0:6 * KD * D]
        sage_raw = sage_raw.rearrange("p (m k i) -> p m k i", m=6, k=KD)
        tn, a = carve(acc, 0, [P, HP * (D + 1)])
        tn = tn.rearrange("p (g d) -> p g d", g=HP)
        tnT, a = carve(acc, a, [P, KD * INNER])
        tnT = tnT.rearrange("p (k n) -> p k n", k=KD)
        norm_row, a = carve(acc, a, [1, INNER])
        slice_t, a = carve(acc, a, [HD, INNER])
        q_t, a = carve(acc, a, [HD, INNER])
        k_t, a = carve(acc, a, [HD, INNER])
        v_s, a = carve(acc, a, [HD, INNER])
        attn, a = carve(acc, a, [HD, INNER])
        attn_t, o_t = q_t, k_t
        mid, a = carve(acc, a, [P, HP * D])
        mid = mid.rearrange("p (g d) -> p g d", g=HP)
        b_fx, a = carve(acc, a, [1, INNER])
        odd = wc[0:HD, :, :].rearrange("p k n -> p (k n)").rearrange("p (g d) -> p g d", g=HP)
        assert a <= (T + 1) * (D + 1), a
        sw_stage, a = carve(acc, 0, [P, 2 * INNER])
        sw_stage = sw_stage.rearrange("p (s n) -> p s n", s=2)
        h_stage2, a = carve(acc, a, [P, 2 * D])
        h_stage2 = h_stage2.rearrange("p (s d) -> p s d", s=2)
        h_stage3, a = carve(sw, 0, [P, 2 * D])
        h_stage3 = h_stage3.rearrange("p (s d) -> p s d", s=2)
        elu_v, a = carve(sw, a, [P, 2 * D])
        elu_v = elu_v.rearrange("p (s d) -> p s d", s=2)
        elu_n, a = carve(sw, a, [P, 2 * D])
        elu_n = elu_n.rearrange("p (s d) -> p s d", s=2)
        elu_e, a = carve(sw, a, [P, 2 * D])
        elu_e = elu_e.rearrange("p (s d) -> p s d", s=2)
        elu_p, a = carve(sw, a, [P, 2 * D])
        elu_p = elu_p.rearrange("p (s d) -> p s d", s=2)
        layers_end = a
        z_out, a = carve(sw, a, [P, 2 * D])
        z_out = z_out.rearrange("p (s d) -> p s d", s=2)
        root_part, a = carve(sw, a, [P, T * D])
        root_part = root_part.rearrange("p (t d) -> p t d", t=T)
        assert a <= T * INNER, a
        a = layers_end
        w1, a = carve(sw, a, [P, 2 * KD * FF])
        w1 = w1.rearrange("p (s k f) -> p s k f", s=2, k=KD)
        w2, a = carve(sw, a, [P, 2 * KF * D])
        w2 = w2.rearrange("p (s k d) -> p s k d", s=2, k=KF)
        hidden, a = carve(sw, a, [P, 2 * KF * P])
        hidden = hidden.rearrange("p (s k n) -> p s k n", s=2, k=KF)
        y_out, a = carve(sw, a, [P, 2 * D])
        y_out = y_out.rearrange("p (s d) -> p s d", s=2)
        b2_b, a = carve(sw, a, [P, 2 * D])
        b2_b = b2_b.rearrange("p (s d) -> p s d", s=2)
        b1_col, a = carve(sw, a, [P, 2 * KF])
        b1_col = b1_col.rearrange("p (s k) -> p s k", s=2)
        logits, a = carve(sw, a, [P, T * X16])
        logits = logits.rearrange("p (t e) -> p t e", t=T)
        top8, a = carve(sw, a, [P, T * 8])
        top8 = top8.rearrange("p (t e) -> p t e", t=T)
        at8, a = carve(sw, a, [P, T * 8], U32)
        at8 = at8.rearrange("p (t e) -> p t e", t=T)
        ent, a = carve(sw, a, [P, ENTRIES])
        chose, a = carve(sw, a, [P, X16 * ENTRIES])
        chose = chose.rearrange("p (e n) -> p e n", e=X16)
        place, a = carve(sw, a, [P, X16 * ENTRIES])
        place = place.rearrange("p (e n) -> p e n", e=X16)
        ent_pos, a = carve(sw, a, [P, ENTRIES])
        ent_posi, a = carve(sw, a, [P, ENTRIES], I32)
        ent_row, a = carve(sw, a, [P, ENTRIES], I32)
        ent_row2, a = carve(sw, a, [P, ENTRIES], I32)
        ent_tok, a = carve(sw, a, [P, ENTRIES], I32)
        gates, a = carve(sw, a, [P, ENTRIES])
        gates = gates.rearrange("p (t k) -> p t k", k=TOPK)
        gate_t, a = carve(sw, a, [P, 3 * T])
        gate_t = gate_t.rearrange("p (s t) -> p s t", s=3)
        counts, a = carve(sw, a, [P, X16])
        cmp_e, a = carve(sw, a, [P, ETILES * (X16 - 1)])
        cmp_e = cmp_e.rearrange("p (c e) -> p c e", e=X16 - 1)
        tile_x, a = carve(sw, a, [P, ETILES])
        tile_xi, a = carve(sw, a, [P, ETILES], I32)
        tile_new, a = carve(sw, a, [P, ETILES], I32)
        slot_tok, a = carve(sw, a, [P, ETILES], I32)
        assert a <= T * INNER, a

        ps = [ctx.enter_context(nc.psum_tensor(f"bank{j}", [P, 512], FP32)) for j in range(8)]

        edge_rows = 16 * ROUNDS * (LAYERS + 1)

        def scattered(k):
            return edge_rows + 16 * (ENTRIES // RING + (1 if k < ENTRIES % RING else 0))

        SCORES, SPREAD, TABLE, GATE, EXPERTS = T, 2 * T, 3 * T, 6 * T, 7 * T

        def hid_bank(slot, f):
            return ps[(2 if slot == 0 else 6) + f // 2][:, f % 2 * P:(f % 2 + 1) * P]

        block = ctx.enter_context(nc.Block())

        @block.sync
        def _(sp):
            sp.wait_ge(sem("x_padded"), 1)
            sp.dma_start(x[:, 0:T - 1, :], A["x"][0:(T - 1) * P, :].rearrange("(t p) d -> p t d", p=P))\
                .then_inc(sem("x_in"), 16)
            sp.dma_start(x[0:LAST, T - 1, :], A["x"][(T - 1) * P:N, :]).then_inc(sem("x_in"), 16)
            sp.dma_start(dst_a, A["dst"].rearrange("(p f) -> p f", f=EF)).then_inc(sem("dst_in"), 16)
            sp.wait_ge(sem("dst_b_set"), 1)
            sp.dma_start(dst_b[0:EP - 1, :], A["dst"][1:1 + (EP - 1) * EF].rearrange("(p f) -> p f", f=EF))\
                .then_inc(sem("dst_in"), 16)
            sp.dma_start(dst_b[EP - 1:EP, 0:EF - 1], A["dst"][1 + (EP - 1) * EF:E].unsqueeze(0))\
                .then_inc(sem("dst_in"), 16)
            for m in range(6):
                name = f"L1_gnn_W{'lr'[m % 2]}{m // 2 + 1}"
                sp.dma_start(sage_raw[:, m], A[name].rearrange("(k p) i -> p k i", p=P)).then_inc(sem("sage_in"), 16)
            for k in range(KD):
                sp.dma_start(w_rel[:, k], A["L0_gnn_weight"][:, k * P:(k + 1) * P, :]
                             .rearrange("r p o -> p r o")).then_inc(sem("w_rel_in"), 16)
            sp.wait_ge(sem("edges_zero"), 3)
            full = (EC - 1) // P
            part = EC - 1 - full * P
            for name, tile in (("dst", edge_int), ("src", edge_src), ("edge_type_8", edge_rel)):
                v = tile.rearrange("p (k e) -> p k e", k=EK)
                s = sem("edge_in")
                sp.dma_start(v[:, 0:full, :], A[name][0:full * P * P].rearrange("(k p e) -> p k e", p=P, e=P))\
                    .then_inc(s, 16)
                sp.dma_start(v[0:part, full, :], A[name][full * P * P:(EC - 1) * P].rearrange("(p e) -> p e", e=P))\
                    .then_inc(s, 16)
                sp.dma_start(v[part:part + 1, full, 0:E - (EC - 1) * P], A[name][(EC - 1) * P:E].unsqueeze(0))\
                    .then_inc(s, 16)
            sp.dma_start(src_a, A["src"].rearrange("(p f) -> p f", f=EF)).then_inc(sem("spare_in"), 16)
            sp.dma_start(rel_a, A["edge_type_8"].rearrange("(p f) -> p f", f=EF)).then_inc(sem("spare_in"), 16)

            s = sem("param_in")
            for tile, name in ((gamma_b, "L0_gnn_gamma"), (beta_b, "L0_gnn_beta"), (bout_b, "L0_ffn_b_out"),
                               (gf_b, "L1_ffn_gamma"), (bf_b, "L1_ffn_beta"), (bl_b[:, 0, :], "L1_gnn_bl1"),
                               (bl_b[:, 1, :], "L1_gnn_bl2"), (bl_b[:, 2, :], "L1_gnn_bl3"),
                               (bslice_b, "L0_ffn_b_slice"), (gb_b, "L1_ffn_gate_b")):
                sp.dma_start(tile, A[name].partition_broadcast(P)).then_inc(s, 16)
            sp.dma_start(temp_b, A["L0_ffn_temperature"].rearrange("a h b c -> (a h b c)").partition_broadcast(P))\
                .then_inc(s, 16)
            sp.dma_start(w_fx[:, :, :], A["L0_ffn_W_fx"].rearrange("(k p) n -> p k n", p=P)).then_inc(s, 16)
            sp.dma_start(w_out[:, :, :], A["L0_ffn_W_out"].rearrange("(h c) d -> c h d", c=HD)).then_inc(s, 16)
            sp.dma_start(gate_w[:, :, :], A["L1_ffn_gate_w"].rearrange("(k p) e -> p k e", p=P)).then_inc(s, 16)
            for tile, name in ((w_q, "L0_ffn_W_q"), (w_k, "L0_ffn_W_k"), (w_v, "L0_ffn_W_v")):
                sp.dma_start(tile, A[name]).then_inc(s, 16)
            sp.dma_start(bx_col, A["L0_ffn_b_x"].rearrange("(g p) -> p g", p=P),
                         allow_slow_non_contiguous=True).then_inc(s, 16)
            sp.wait_ge(sem("slice2_zero"), 1)
            for b in range(2):
                sp.dma_start(w_slice2[b * HD:(b + 1) * HD, b * HD:(b + 1) * HD], A["L0_ffn_W_slice"])\
                    .then_inc(s, 16)

            table = projected.ap().rearrange("(t p r) d -> t p (r d)", p=P, r=R)

            def store_projected(t, use, slot):
                sp.wait_ge(sem("proj_copied"), t + 1)
                sp.dma_start(table[bass.ds(t, 1), :, :].rearrange("a p n -> p (a n)"), proj[:, slot, :])\
                    .then_inc(sem(f"proj_stored{slot}"), 16)

            node_tiles(sp, store_projected)
            sp.wait_ge(sem("proj_stored0"), 16 * (T // 2 + 1))
            sp.wait_ge(sem("proj_stored1"), 16 * (T // 2))
            sp.wait_ge(sem("edges_ready"), 1)
            sp.dma_start(w_x, A["L0_ffn_W_x"].rearrange("(k p) n -> p k n", p=P)).then_inc(sem("w_x_in"), 16)

            sp.wait_ge(sem("h_ready"), 2 * T)
            sp.dma_start(b_fx, A["L0_ffn_b_fx"].unsqueeze(0)).then_inc(sem("b_fx_in"), 16)
            sp.wait_ge(sem("odd_heads"), 1)
            sp.dma_start(mid[HD:P, :, :], odd).then_inc(sem("mid_moved"), 16)

            nodes_v = nodes.ap().rearrange("(t p) d -> p t d", p=P)

            def store_tables(layer):
                def store(t, use, slot):
                    sp.wait_ge(sem("z_copied"), t + layer * T + 1)
                    sp.dma_start(nodes.ap()[bass.ds(t * P, P), :], z_out[:, slot, :])\
                        .then_inc(sem(f"z_stored{slot}"), 16)

                node_tiles(sp, store)

            with sp.Fori(0, LAYERS) as layer:
                store_tables(layer)
            sp.wait_ge(sem("h_ready"), 4 * T)
            sp.dma_start(nodes_v, h[:, :, 0:D]).then_inc(sem("nodes_stored"), 16)
            sp.wait_ge(sem("slots_set"), 1)
            sp.dma_start(slots.ap().rearrange("(p c) a -> p (c a)", p=P), slot_tok)\
                .then_inc(sem("slots_cleared"), 16)
            for j in range(RING):
                sp.wait_ge(sem(f"rows_in{j}"), scattered(j))
            sp.wait_ge(sem("slots_cleared"), 16)
            sp.dma_start(slot_tok, slots.ap().rearrange("(p c) a -> p (c a)", p=P))\
                .then_inc(sem("slot_tok_in"), 16)

            def expert_w1(e, slot):
                s = sem(f"w1_in{slot}")
                sp.dma_start(w1[:, slot], A["L1_ffn_w1"][bass.ds(e, 1), :, :]
                             .rearrange("a (k p) f -> p (a k) f", p=P)).then_inc(s, 16)
                sp.dma_start(b1_col[:, slot], A["L1_ffn_b1"][bass.ds(e, 1), :]
                             .rearrange("a (k p) -> p (a k)", p=P),
                             allow_slow_non_contiguous=True).then_inc(s, 16)

            def expert_w2(e, slot):
                s = sem(f"w2_in{slot}")
                sp.dma_start(w2[:, slot], A["L1_ffn_w2"][bass.ds(e, 1), :, :]
                             .rearrange("a (k p) d -> p (a k) d", p=P)).then_inc(s, 16)
                sp.dma_start(b2_b[:, slot], A["L1_ffn_b2"][bass.ds(e, 1), :]
                             .rearrange("a d -> (a d)").partition_broadcast(P)).then_inc(s, 16)

            def load_expert(c, use, slot):
                e = sp.value_load(tile_xi[0:1, bass.ds(c, 1)], min_val=0, max_val=X16 - 1)
                if first_use(c):
                    expert_w1(e, slot)
                    expert_w2(e, slot)
                    return
                new = sp.value_load(tile_new[0:1, bass.ds(c, 1)], min_val=0, max_val=1)
                with sp.If(new > 0):
                    sp.wait_ge(sem("hid_ready"), c * KF - KF)
                    expert_w1(e, slot)
                    sp.wait_ge(sem("y_copied"), c - 1)
                    expert_w2(e, slot)
                with sp.If(1 - new > 0):
                    for w in (1, 2):
                        sp.wait_ge(sem(f"w{w}_in{slot}"), 32 * use)
                        sp.sem_inc(sem(f"w{w}_in{slot}"), 32)

            def store_y(c, slot):
                sp.wait_ge(sem("y_copied"), c + 1)
                sp.dma_start(expert_rows.ap()[bass.ds(c * P, P), :], y_out[:, slot])\
                    .then_inc(sem(f"y_stored{slot}"), 16)

            sp.wait_ge(sem("tile_experts"), 1)
            load_expert(0, 0, 0)
            load_expert(1, 0, 1)
            with sp.Fori(1, ETILES // 2) as i:
                load_expert(2 * i, i, 0)
                store_y(2 * i - 2, 0)
                load_expert(2 * i + 1, i, 1)
                store_y(2 * i - 1, 1)
            store_y(ETILES - 2, 0)
            store_y(ETILES - 1, 1)
            for n in range(T // UNROLL):
                t = n * UNROLL
                sp.wait_ge(sem("result_ready"), n + 1)
                whole = UNROLL if t + UNROLL < T else UNROLL - 1
                sp.dma_start(out[t * P:(t + whole) * P, :].rearrange("(t p) d -> p t d", p=P), h[:, t:t + whole, 0:D])\
                    .then_inc(sem("out_stored"), 16)
            sp.dma_start(out[(T - 1) * P:N, :], h[0:LAST, T - 1, 0:D]).then_inc(sem("out_stored"), 16)
            sp.wait_ge(sem("out_stored"), 16 * (T // UNROLL + 1))

        @block.gpsimd
        def _(pool):
            pool.memset(x[:, T - 1, :], 0.0).then_inc(sem("x_padded"), 1)
            pool.memset(dst_b[:, EF - 1:EF], N).then_inc(sem("dst_b_set"), 1)
            pool.iota(iota[:, :], [[1, PAIRS + 2]], base=0, channel_multiplier=0,
                      allow_small_or_imprecise_dtypes=True).then_inc(sem("const"), 1)
            pool.iota(pidx[:, :], [[P, EK]], base=0, channel_multiplier=1,
                      allow_small_or_imprecise_dtypes=True).then_inc(sem("const"), 1)
            pool.memset(ones[:, :], 1.0).then_inc(sem("const"), 1)
            pool.memset(eps[:, :], EPS).then_inc(sem("const"), 1)
            pool.memset(h[:, :, D:D + 1], 1.0).then_inc(sem("const"), 1)
            pool.memset(edge_int, int(NOWHERE)).then_inc(sem("edges_zero"), 1)
            pool.memset(edge_rel, 0).then_inc(sem("edges_zero"), 1)
            pool.memset(edge_src, 0).then_inc(sem("edges_zero"), 1)
            pool.memset(w_slice2, 0.0).then_inc(sem("slice2_zero"), 1)

            def stage(t, slot, out_, tile, ready, used):
                if ready:
                    pool.wait_ge(*ready)
                if not first_use(t):
                    pool.wait_ge(*used)
                pool.nop(nofuse=True)
                pool.tensor_copy(out_, tile[:, bass.ds(t, 1), 0:out_.shape[1]].rearrange("p a n -> p (a n)"))\
                    .then_inc(sem("tile_staged"), 1)

            node_tiles(pool, lambda t, use, slot: stage(
                t, slot, h_stage1[:, slot, :], h, (sem("h_ready"), t + 1), (sem("transposed"), t - 1)))

            pool.wait_ge(sem("flag_ready"), 1)
            late = pool.value_load(flag[0:1, 0:1], min_val=0, max_val=E)
            with pool.If(late > 0):
                pool.wait_ge(sem("f_ready"), 1)
                behind = junk[0:1, 0:2 * P].rearrange("p (e w) -> p e w", w=2)
                pool.memset(behind[:, :, 0], 0.0).then_inc(sem("f_tail"), 1)
                pool.memset(behind[:, :, 1], NOWHERE).then_inc(sem("f_tail"), 1)
                pool.wait_ge(sem("f_tail"), 2)
                tail = in_order.ap().rearrange("(c e) w -> c (e w)", e=P)[EC - 1:EC, :]
                pool.dma_start(tail, junk[0:1, 0:2 * P]).then_inc(sem("f_moved"), 16)
                pool.wait_ge(sem("f_moved"), 16)
                with pool.Fori(0, EF) as c:
                    pool.tensor_copy(fone_idx, f_posi[:, bass.ds(c, 1)]).then_inc(sem("f_staged"), 1)
                    pool.tensor_copy(fone_pay, f_pay[:, bass.ds(c, 1), :].rearrange("p a w -> p (a w)"))\
                        .then_inc(sem("f_staged"), 1)
                    pool.wait_ge(sem("f_staged"), 2 * c + 2)
                    pool.nop(nofuse=True)
                    pool.indirect_dma_start(out=in_order.ap(), out_offset=bass.IndirectOffsetOnAxis(ap=fone_idx, axis=0),
                                            in_=fone_pay, in_offset=None).then_inc(sem("f_moved"), 16)
                    pool.wait_ge(sem("f_moved"), 16 * c + 32)
                back = in_order.ap().rearrange("(c e) w -> c (e w)", e=P)
                flat = edges.rearrange("p (k n) -> p k n", k=EK)
                pool.wait_ge(sem("edges_float"), 1)
                pool.dma_start(flat[:, 0:EK - 1, :], back[0:(EK - 1) * P, :].rearrange("(k p) n -> p k n", p=P))\
                    .then_inc(sem("f_back"), 16)
                pool.dma_start(flat[0:EC - (EK - 1) * P, EK - 1, :], back[(EK - 1) * P:EC, :])\
                    .then_inc(sem("f_back"), 16)
                pool.wait_ge(sem("f_back"), 32)
            pool.wait_ge(sem("spare_in"), 32)
            pool.wait_ge(sem("edges_float"), 1)
            pool.memset(onehot[:, 0, 0:1], 0.0).then_inc(sem("edges_ready"), 1)
            pool.wait_ge(sem("edges_ready"), 1)
            pool.wait_ge(sem("sage_done"), 6)
            pool.memset(rows[:, :, D:D + 1], 1.0).then_inc(sem("rows_ones"), 1)
            pool.wait_ge(sem("rows_ones"), 1)

            def gather_group(g, table, indices):
                for k in range(GROUP):
                    slot = g * GROUP + k
                    pool.indirect_dma_start(
                        out=rows[:, slot, 0:D], out_offset=None, in_=table,
                        in_offset=bass.IndirectOffsetOnAxis(ap=indices[:, g, k:k + 1], axis=0),
                    ).then_inc(sem(f"rows_in{slot}"), 16)

            def gathers(i, table, index, done, base, count):
                for g in range(2):
                    t = i * RING + g * GROUP
                    if not (isinstance(i, int) and i == 0):
                        pool.wait_ge(sem(done), base + t + (GROUP - RING))
                    pool.nop(nofuse=True)
                    pool.tensor_copy(staged[:, g, :], index[:, bass.ds(t, GROUP)]).then_inc(sem("staged"), 1)
                    count[0] = count[0] + 1
                    pool.wait_ge(sem("staged"), count[0])
                    pool.nop(nofuse=True)
                    gather_group(g, table, staged)

            def gather_edges(r, table):
                with pool.Fori(0, ROUNDS) as i:
                    for g in range(2):
                        pool.wait_ge(sem("index_staged"), i * 2 + (r * 2 * ROUNDS + g + 1))
                        pool.nop(nofuse=True)
                        gather_group(g, table, pair_index)

            pool.wait_ge(sem("pair_tables"), 1)
            pool.wait_ge(sem("proj_stored0"), 16 * (T // 2 + 1))
            pool.wait_ge(sem("proj_stored1"), 16 * (T // 2))
            pool.memset(inv_n, 1.0 / N).then_inc(sem("inv_n_set"), 1)
            gather_edges(0, projected.ap())
            def keep_weights(t, use, slot):
                pool.wait_ge(sem("sw_ready"), t + 1)
                pool.nop(nofuse=True)
                pool.tensor_copy(swv[:, bass.ds(t, 1), :].rearrange("p a n -> p (a n)"), sw_stage[:, slot, :])\
                    .then_inc(sem("sw_kept"), 1)

            node_tiles(pool, keep_weights)
            node_tiles(pool, lambda t, use, slot: stage(
                t, slot, h_stage3[:, slot, :], h, (sem("h_ready"), t + (2 * T + 1)), (sem("transposed"), t + (TABLE - 1))))

            pool.sem_inc(sem("layer_out"), 1)

            def layer_tiles(layer):
                def layer_tile(t, use, slot):
                    n = layer * T
                    pool.wait_ge(sem("h_staged"), t + n + 1)
                    pool.nop(nofuse=True)
                    pool.tensor_copy(h[:, bass.ds(t, 1), 0:D].rearrange("p a n -> p (a n)"), h_stage3[:, slot, :])\
                        .then_inc(sem("layer_out"), 1)

                node_tiles(pool, layer_tile)

            def gather_layer(layer):
                for slot in range(2):
                    pool.wait_ge(sem(f"z_stored{slot}"), (layer + 1) * (16 * ((T + 1 - slot) // 2)))
                pool.nop(nofuse=True)
                gather_edges(layer + 1, nodes.ap())

            with pool.Fori(0, LAYERS - 1) as layer:
                gather_layer(layer)
                layer_tiles(layer)
            gather_layer(LAYERS - 1)
            n = 0
            node_tiles(pool, lambda t, use, slot: stage(
                t, slot, h_stage3[:, slot, :], h, (sem("h_ready"), t + (3 * T + 1)), (sem("transposed"), t + (GATE - 1))))
            pool.wait_ge(sem("layers_done"), 1)
            pool.iota(ent_tok.rearrange("p (t k) -> p t k", k=TOPK), [[P, T], [0, TOPK]], base=0,
                      channel_multiplier=1).then_inc(sem("toks"), 1)
            pool.memset(slot_tok, 0).then_inc(sem("slots_set"), 1)
            pool.wait_ge(sem("toks"), 1)
            pool.wait_ge(sem("places"), 1)
            pool.wait_ge(sem("slots_cleared"), 16)

            def scatter(j0, m, parts, g, before_):
                for k in before_:
                    pool.wait_ge(*k)
                pool.nop(nofuse=True)
                pool.tensor_copy(staged[0:parts, g, 0:m], ent_row[0:parts, bass.ds(j0, m)])\
                    .then_inc(sem("staged"), 1)
                pool.tensor_copy(staged_tok[0:parts, g, 0:m], ent_tok[0:parts, bass.ds(j0, m)])\
                    .then_inc(sem("staged"), 1)

            def send(g, m, parts):
                for k in range(m):
                    pool.indirect_dma_start(
                        out=slots.ap(), out_offset=bass.IndirectOffsetOnAxis(ap=staged[0:parts, g, k:k + 1], axis=0),
                        in_=staged_tok[0:parts, g, k:k + 1], in_offset=None,
                    ).then_inc(sem(f"rows_in{g * GROUP + k}"), 16)

            for g in range(2):
                scatter(g * GROUP, GROUP, P, g, ())
                n += 2
                pool.wait_ge(sem("staged"), n)
                send(g, GROUP, P)
            with pool.Fori(1, 3) as i:
                for g in range(2):
                    scatter(i * RING + g * GROUP, GROUP, P, g,
                            [(sem(f"rows_in{g * GROUP + k}"), 16 * i + edge_rows) for k in range(GROUP)])
                    pool.wait_ge(sem("staged"), (i - 1) * 4 + (n + 2 * g + 2))
                    pool.nop(nofuse=True)
                    send(g, GROUP, P)
            n += 8
            scatter(3 * RING, TOPK, LAST, 0, [(sem(f"rows_in{k}"), edge_rows + 48) for k in range(GROUP)])
            n += 2
            pool.wait_ge(sem("staged"), n)
            send(0, TOPK, LAST)

            pool.wait_ge(sem("slot_tok_in"), 16)
            pool.wait_ge(sem("nodes_stored"), 16)
            gathers(0, nodes.ap(), slot_tok, "x_used", 0, [n])
            with pool.Fori(1, ETILES // RING) as i:
                gathers(i, nodes.ap(), slot_tok, "x_used", 0, [n + i * 2])
            n += 2 * (ETILES // RING)
            pool.wait_ge(sem("y_stored0"), 16 * (ETILES // 2))
            pool.wait_ge(sem("y_stored1"), 16 * (ETILES // 2))
            pool.wait_ge(sem("x_used"), ETILES)
            gathers(0, expert_rows.ap(), ent_posi, "combined", 0, [n])
            with pool.Fori(1, 3) as i:
                gathers(i, expert_rows.ap(), ent_posi, "combined", 0, [n + i * 2])
            n += 6
            pool.wait_ge(sem("combined"), 2 * RING + GROUP)
            pool.tensor_copy(staged[:, 0, 0:TOPK], ent_posi[:, 3 * RING:3 * RING + TOPK]).then_inc(sem("staged"), 1)
            pool.wait_ge(sem("staged"), n + 1)
            for k in range(TOPK):
                pool.indirect_dma_start(
                    out=rows[:, k, 0:D], out_offset=None, in_=expert_rows.ap(),
                    in_offset=bass.IndirectOffsetOnAxis(ap=staged[:, 0, k:k + 1], axis=0),
                ).then_inc(sem(f"rows_in{k}"), 16)

        @block.scalar
        def _(act):
            def root(k):
                act.wait_ge(sem("var_ready"), k + 1)
                act.activation(nrm[:, 0, :], mv[:, :, 1], ACT.Sqrt, bias=eps[:, 0:1]).then_inc(sem("sd_ready"), 1)

            act.wait_ge(sem("const"), 5)
            for m in range(6):
                act.wait_ge(sem("sage_tp"), m + 1)
                act.copy(sage_w[:, 2 * m:2 * m + 2, :], ps[m % 2][:, :].rearrange("p (k n) -> p k n", k=KD))\
                    .then_inc(sem("sage_done"), 1)
            root(0)

            def project_h(t, slot):
                act.wait_ge(sem("transposed"), t + 1)
                if not first_use(t):
                    act.wait_ge(sem("p_mm"), t * 4 - 4)
                act.copy(hT[:, slot, 0:KD, :], ps[slot][:, 0:D].rearrange("p (k n) -> p k n", k=KD))\
                    .then_inc(sem("hT_ready"), 1)

            def project(t, use, slot):
                if not (isinstance(t, int) and t == T - 1):
                    project_h(t + 1, 1 - slot)
                if not first_use(t):
                    act.wait_ge(sem(f"proj_stored{slot}"), 16 * use)
                for j in range(4):
                    act.wait_ge(sem("p_mm"), t * 4 + (j + 1))
                    ins = act.copy(proj[:, slot, j * 512:(j + 1) * 512], ps[2 + j][:, :])
                    ins.then_inc(sem("proj_copied") if j == 3 else sem("p_evac"), 1)
                    if j == 3:
                        act.wait_ge(sem("proj_copied"), t + 1)
                        act.sem_inc(sem("p_evac"), 1)

            project_h(0, 0)
            node_tiles(act, project)
            for k in range(KD):
                act.wait_ge(sem("wx_tp"), k + 1)
                act.copy(w_xT[:, :, k * P:(k + 1) * P], ps[2 + k][:, :].rearrange("p (g n) -> p g n", g=HP))\
                    .then_inc(sem("wxT_ready"), 1)

            def stage_indices(i, r, index):
                for g in range(2):
                    if not (isinstance(i, int) and i == 0 and r is None):
                        act.wait_ge(sem("pair_done"), i * RING + ((0 if r is None else r * PAIRS) + g * GROUP + GROUP - RING))
                    act.nop(nofuse=True)
                    act.copy(pair_index[:, g, :], index[:, bass.ds(i * RING + g * GROUP, GROUP)])\
                        .then_inc(sem("index_staged"), 1)

            act.wait_ge(sem("pair_tables"), 1)
            stage_indices(0, None, pair_row0)
            with act.Fori(1, ROUNDS) as i:
                stage_indices(i, None, pair_row0)
            for n in range(T // UNROLL):
                q = slice(n * UNROLL, n * UNROLL + UNROLL)
                act.wait_ge(sem("centred"), n + 1)
                act.activation(squares[:, q, :], accv[:, q, 0:D], ACT.Square).then_inc(sem("squared"), 1)
            act.wait_ge(sem("bn_var"), 1)
            act.activation(col[:, 0, :], ps[5][:, 0:D], ACT.Sqrt, bias=eps[:, 0:1]).then_inc(sem("bn_sd"), 1)
            root(1)

            def stage_tile(out_, tile, t):
                act.nop(nofuse=True)
                act.copy(out_, tile[:, bass.ds(t, 1), 0:out_.shape[1]].rearrange("p a n -> p (a n)"))\
                    .then_inc(sem("tile_staged"), 1)

            def score_stage(t, slot):
                act.wait_ge(sem("h_ready"), t + (T + 1))
                stage_tile(h_stage2[:, slot, :], h, t)

            def score_tile(t, slot):
                act.wait_ge(sem("transposed"), t + (SCORES + 1))
                act.copy(hT[:, slot, 0:KD, :], ps[slot][:, 0:D].rearrange("p (k n) -> p k n", k=KD))\
                    .then_inc(sem("hT_ready"), 1)

            def score_exp(t):
                act.wait_ge(sem("l_shifted"), t + 1)
                v = swv[:, bass.ds(t, 1), :].rearrange("p a n -> p (a n)")
                act.nop(nofuse=True)
                act.activation(v, v, ACT.Exp).then_inc(sem("l_exp"), 1)

            score_stage(0, 0)
            score_stage(1, 1)
            score_tile(0, 0)
            score_stage(2, 0)
            with act.Fori(0, T // 2 - 1) as i:
                score_tile(2 * i + 1, 1)
                score_stage(2 * i + 3, 1)
                score_exp(2 * i)
                score_tile(2 * i + 2, 0)
                score_stage(2 * i + 4, 0)
                score_exp(2 * i + 1)
            score_tile(T - 2, 1)
            score_exp(T - 3)
            score_tile(T - 1, 0)
            score_exp(T - 2)
            score_exp(T - 1)
            for k in range(KD):
                act.wait_ge(sem("tn_tp"), k + 1)
                act.copy(tnT[:, k, :], ps[k][:, :]).then_inc(sem("s_evac"), 1)
            act.wait_ge(sem("tn_tp"), 3)
            act.copy(norm_row, ps[2][0:1, :]).then_inc(sem("s_evac"), 1)
            act.wait_ge(sem("st_mm"), 1)
            act.copy(slice_t, ps[3][0:HD, :]).then_inc(sem("s_evac"), 1)
            for j, tile in enumerate((q_t, k_t, v_s)):
                act.wait_ge(sem("qkv_mm"), j + 1)
                act.copy(tile, ps[j][0:HD, :]).then_inc(sem("s_evac"), 1)
            act.wait_ge(sem("attn_shifted"), 1)
            act.activation(attn, attn, ACT.Exp, scale=SCALE).then_inc(sem("attn_exp"), 1)
            act.wait_ge(sem("attn_tp"), 1)
            act.copy(attn_t, ps[4][0:HD, :]).then_inc(sem("s_evac"), 1)
            act.wait_ge(sem("o_mm"), 1)
            act.copy(o_t, ps[5][0:HD, :]).then_inc(sem("s_evac"), 1)
            for g in range(HP):
                act.wait_ge(sem("m_mm"), g + 1)
                act.copy(mid[0:HD, g, :], ps[g][0:HD, 0:D]).then_inc(sem("mid_even"), 1)
                ins = act.copy(odd[:, g, :], ps[g][0:HD, D:2 * D])
                ins.then_inc(sem("odd_copied"), 1)
            act.wait_ge(sem("odd_copied"), HP)
            act.sem_inc(sem("odd_heads"), 1)

            def spread(t, slot):
                act.wait_ge(sem("transposed"), t + (SPREAD + 1))
                act.copy(hT[:, slot, :, :], ps[slot][:, :].rearrange("p (k n) -> p k n", k=4))\
                    .then_inc(sem("hT_ready"), 1)

            act.wait_ge(sem("sw_kept"), T)
            act.wait_ge(sem("m_mm"), HP)
            for t in range(2):
                stage_tile(sw_stage[:, t, :], swv, t)
            with act.Fori(0, T // 2 - 1) as i:
                for slot in range(2):
                    spread(2 * i + slot, slot)
                    stage_tile(sw_stage[:, slot, :], swv, 2 * i + (slot + 2))
            spread(T - 3, 0)
            stage_tile(sw_stage[:, 0, :], swv, T - 1)
            spread(T - 2, 1)
            spread(T - 1, 0)
            root(2)

            def table_tile(t, layer, slot):
                act.wait_ge(sem("transposed"), t + layer * T + (TABLE + 1))
                act.copy(hT[:, slot, 0:KD, :], ps[slot][:, 0:D].rearrange("p (k n) -> p k n", k=KD))\
                    .then_inc(sem("hT_ready"), 1)

            def table_out(t, layer, use, slot):
                act.wait_ge(sem("z_mm"), t + layer * T + 1)
                stores = (T + 1 - slot) // 2
                if not (first_use(t) and isinstance(layer, int) and layer == 0):
                    act.wait_ge(sem(f"z_stored{slot}"), (layer * stores + use) * 16)
                act.nop(nofuse=True)
                act.copy(z_out[:, slot, :], ps[6 + slot][:, 0:D]).then_inc(sem("z_copied"), 1)

            def first_table(t, use, slot):
                table_tile(t, 0, slot)
                table_out(t, 0, use, slot)

            node_tiles(act, first_table)

            def root_copies(i, layer):
                act.wait_ge(sem("root_tp"), layer * T + (i + 1))
                act.copy(hT[:, 0, 0:KD, :], ps[0][:, 0:D].rearrange("p (k n) -> p k n", k=KD))\
                    .then_inc(sem("root_hT"), 1)

            def root_stage(i, layer):
                act.nop(nofuse=True)
                act.copy(h_stage3[:, 0, :], h[:, bass.ds(i, 1), 0:D].rearrange("p a n -> p (a n)"))\
                    .then_inc(sem("root_staged"), 1)

            def gather_layer(layer):
                stage_indices(0, layer + 1, pair_row)
                act.wait_ge(sem("layer_out"), layer * T + 1)
                root_stage(0, layer)
                root_copies(0, layer)
                root_stage(1, layer)
                with act.Fori(1, T - 1) as i:
                    stage_indices(i, layer + 1, pair_row)
                    root_copies(i, layer)
                    root_stage(i + 1, layer)
                stage_indices(T - 1, layer + 1, pair_row)
                root_copies(T - 1, layer)
                for i in range(T, ROUNDS):
                    stage_indices(i, layer + 1, pair_row)

            def layer_exp(t, layer, slot):
                act.wait_ge(sem("elu_neg"), t + layer * T + 1)
                act.activation(elu_e[:, slot], elu_n[:, slot], ACT.Exp).then_inc(sem("elu_exp"), 1)
                act.activation(elu_p[:, slot], elu_v[:, slot], ACT.Relu).then_inc(sem("elu_pos"), 1)

            with act.Fori(0, LAYERS - 1) as layer:
                gather_layer(layer)
                layer_exp(0, layer, 0)
                layer_exp(1, layer, 1)
                table_tile(0, layer + 1, 0)
                with act.Fori(0, T // 2 - 1) as i:
                    layer_exp(2 * i + 2, layer, 0)
                    table_tile(2 * i + 1, layer + 1, 1)
                    table_out(2 * i, layer + 1, i, 0)
                    layer_exp(2 * i + 3, layer, 1)
                    table_tile(2 * i + 2, layer + 1, 0)
                    table_out(2 * i + 1, layer + 1, i, 1)
                layer_exp(T - 1, layer, 0)
                table_tile(T - 2, layer + 1, 1)
                table_out(T - 3, layer + 1, T // 2 - 1, 0)
                table_tile(T - 1, layer + 1, 0)
                table_out(T - 2, layer + 1, T // 2 - 1, 1)
                table_out(T - 1, layer + 1, T // 2, 0)
            gather_layer(LAYERS - 1)
            node_tiles(act, lambda t, use, slot: layer_exp(t, LAYERS - 1, slot))
            root(3)

            def gate_tile(t, use, slot):
                act.wait_ge(sem("transposed"), t + (GATE + 1))
                act.copy(hT[:, slot, 0:KD, :], ps[slot][:, 0:D].rearrange("p (k n) -> p k n", k=KD))\
                    .then_inc(sem("hT_ready"), 1)

            node_tiles(act, gate_tile)
            act.wait_ge(sem("gate_diff"), 1)
            act.activation(gate_t[:, 1, :], gate_t[:, 0, :], ACT.Exp).then_inc(sem("gate_exp"), 1)

            def x_copy(c, slot):
                act.wait_ge(sem("x_used"), c + 1)
                act.copy(hT[:, slot, 0:KD, :], ps[slot][:, 0:D].rearrange("p (k n) -> p k n", k=KD))\
                    .then_inc(sem("hT_ready"), 1)

            def expert_act(c, slot, last=False):
                for f in range(KF):
                    if f % 2 == 0:
                        act.wait_ge(sem("hid_mm"), c * KF + (f + 2))
                    act.activation(hidden[:, slot, f, :], hid_bank(slot, f), ACT.Relu,
                                   bias=b1_col[:, slot, f:f + 1]).then_inc(sem("hid_ready"), 1)
                if not last:
                    x_copy(c + 1, 1 - slot)

            x_copy(0, 0)
            with act.Fori(0, ETILES // 2 - 1) as i:
                expert_act(2 * i, 0)
                expert_act(2 * i + 1, 1)
            expert_act(ETILES - 2, 0)
            expert_act(ETILES - 1, 1, last=True)
            root(4)
            act.wait_ge(sem("moments_ready"), 1)
            for t in range(T):
                act.activation(h[:, t, 0:D], h[:, t, 0:D], ACT.Identity, bias=nrm[:, 3, t:t + 1],
                               scale=nrm[:, 2, t:t + 1]).then_inc(sem("h_scaled"), 1)

        @block.tensor
        def _(pe):
            pe.wait_ge(sem("ident_ready"), 1)
            pe.wait_ge(sem("const"), 5)

            def tile_of(v, t):
                return v[:, bass.ds(t, 1), :].rearrange("p a n -> p (a n)")

            def transpose_h(t, slot, stage, before_):
                pe.wait_ge(sem("tile_staged"), t + (before_ + 1))
                for k in range(KD):
                    ins = pe.transpose(ps[slot][:, k * P:(k + 1) * P], stage[:, slot, k * P:(k + 1) * P], ident[:, :])
                ins.then_inc(sem("transposed"), 1)

            pe.wait_ge(sem("sage_in"), 6 * 16)
            for m in range(6):
                if m >= 2:
                    pe.wait_ge(sem("sage_done"), m - 1)
                for ki in range(KD):
                    for ko in range(KD):
                        c = (ki * KD + ko) * P
                        ins = pe.transpose(ps[m % 2][:, c:c + P], sage_raw[:, m, ko, ki * P:(ki + 1) * P], ident[:, :])
                ins.then_inc(sem("sage_tp"), 1)
            pe.wait_ge(sem("sage_done"), 6)
            pe.wait_ge(sem("w_rel_in"), 32)

            def project(t, use, slot):
                if not (isinstance(t, int) and t == T - 1):
                    transpose_h(t + 1, 1 - slot, h_stage1, 0)
                pe.wait_ge(sem("hT_ready"), t + 1)
                for j in range(4):
                    if not (isinstance(t, int) and t == 0):
                        pe.wait_ge(sem("p_evac"), t * 4 + (j - 3))
                    for k in range(KD):
                        ins = pe.matmul(ps[2 + j][:, :], hT[:, slot, k, :], w_rel_mm[:, k, j * 512:(j + 1) * 512],
                                        start=k == 0, stop=k == KD - 1)
                    ins.then_inc(sem("p_mm"), 1)

            transpose_h(0, 0, h_stage1, 0)
            project(0, 0, 0)
            project(1, 0, 1)
            half = T // 4
            with pe.Fori(1, half) as i:
                project(2 * i, i, 0)
                project(2 * i + 1, i, 1)
            pe.wait_ge(sem("cum_ready"), 1)
            pe.matmul(ps[6][:, 0:T + 2], ones[0:EP, :], cum, start=True, stop=True).then_inc(sem("tot_mm"), 1)
            pe.matmul(ps[7][:, 0:T + 2], before[0:EP, :], cum, start=True, stop=True).then_inc(sem("tot_mm"), 1)
            with pe.Fori(half, T // 2) as i:
                project(2 * i, i, 0)
                project(2 * i + 1, i, 1)
            project(T - 1, T // 2, 0)

            pe.wait_ge(sem("chosen_ready"), 1)
            pe.wait_ge(sem("edges_ready"), 1)
            for w in range(2):
                for k in range(EK):
                    ins = pe.matmul(ps[6 + w][:, 0:PAIRS], edges_v[:, k, :, w], chosen_v[:, k, :],
                                    start=k == 0, stop=k == EK - 1)
                ins.then_inc(sem("pairs_mm"), 1)

            pe.wait_ge(sem("param_in"), PARAMS * 16)
            pe.wait_ge(sem("w_x_in"), 16)
            pe.wait_ge(sem("p_evac"), 4 * T)
            for k in range(KD):
                for g in range(HP):
                    ins = pe.transpose(ps[2 + k][:, g * P:(g + 1) * P], w_x[:, k, g * P:(g + 1) * P], ident[:, :])
                ins.then_inc(sem("wx_tp"), 1)
            pe.wait_ge(sem("wxT_ready"), KD)
            pe.wait_ge(sem("bx_ready"), 1)
            for k in range(KD):
                for g in range(HP):
                    ins = pe.matmul(ps[4 + k][:, g * P:(g + 1) * P], w_xT[:, g, k * P:(k + 1) * P], w_slice2,
                                    start=True, stop=True)
                ins.then_inc(sem("wc_mm"), 1)
            for g in range(HP):
                ins = pe.matmul(ps[3][:, g * P:(g + 1) * P], bx_rep[:, g, :], w_slice2, start=True, stop=True)
            ins.then_inc(sem("wc_mm"), 1)

            def pair_sums(i, r, first, ks=range(RING)):
                for k in ks:
                    t = r * PAIRS + (i * RING + k)
                    if k % BATCH == 0:
                        pe.wait_ge(sem("onehot_ready"), r * (PAIRS // BATCH + 1) + (i * (RING // BATCH) + k // BATCH + 1))
                    if not (first and k < BATCH):
                        pe.wait_ge(sem("pair_added"), t - (BATCH - 1))
                    pe.wait_ge(sem(f"rows_in{k}"), r * (16 * ROUNDS) + (i * 16 + 16))
                    pe.matmul(ps[4 + k % BATCH][:, 0:D + 1], onehot[:, k % (2 * BATCH), :], rows[:, k, :],
                              start=True, stop=True).then_inc(sem("pair_done"), 1)

            def gather_edges(r):
                pair_sums(0, r, isinstance(r, int))
                with pe.Fori(1, ROUNDS) as i:
                    pair_sums(i, r, False)

            pe.wait_ge(sem("pair_tables"), 1)
            gather_edges(0)
            pe.wait_ge(sem("inv_n_set"), 1)
            pe.wait_ge(sem("pair_added"), PAIRS)

            def column_mean(bank, v, done, last, ready=None):
                for t in range(T):
                    if ready and t % UNROLL == 0:
                        pe.wait_ge(sem(ready), t // UNROLL + 1)
                    n = last if t == T - 1 else P
                    ins = pe.matmul(bank, inv_n[0:n, :], v[0:n, t, 0:D], start=t == 0, stop=t == T - 1)
                ins.then_inc(sem(done), 1)

            column_mean(ps[4][:, 0:D], accv, "bn_mean", LAST)
            column_mean(ps[5][:, 0:D], squares, "bn_var", LAST, ready="squared")
            pe.wait_ge(sem("wc_ready"), 1)

            def slice_sums(t, slot, rows_, start=False, stop=False):
                pe.wait_ge(sem("sw_ready"), t + 1)
                v = sw_stage[:, slot, :]
                x1 = tile_of(h, t)
                for g in range(HP):
                    ins = pe.matmul(ps[4 + g][:, 0:D + 1], v[0:rows_, g * P:(g + 1) * P], x1[0:rows_, :],
                                    start=start, stop=stop)
                ins.then_inc(sem("slices_mm"), 1)

            def scores(t, use, slot):
                if not (isinstance(t, int) and t == T - 1):
                    transpose_h(t + 1, 1 - slot, h_stage2, SCORES)
                pe.wait_ge(sem("hT_ready"), t + (SCORES + 1))
                if not first_use(t):
                    pe.wait_ge(sem("l_read"), t - 1)
                for k in range(KD):
                    ins = pe.matmul(ps[2 + slot][:, :], hT[:, slot, k, :], wc[:, k, :],
                                    start=k == 0, stop=k == KD - 1)
                ins.then_inc(sem("l_mm"), 1)
                if not first_use(t):
                    slice_sums(t - 2, slot, P, start=isinstance(t, int) and t == 2)

            transpose_h(0, 0, h_stage2, SCORES)
            scores(0, 0, 0)
            scores(1, 0, 1)
            scores(2, 1, 0)
            with pe.Fori(1, T // 2 - 1) as i:
                scores(2 * i + 1, i, 1)
                scores(2 * i + 2, i + 1, 0)
            scores(T - 2, T // 2 - 1, 1)
            scores(T - 1, T // 2, 0)
            slice_sums(T - 2, 1, P)
            slice_sums(T - 1, 0, LAST, stop=True)

            pe.wait_ge(sem("tn_ready"), 1)
            for k in range(KD):
                for g in range(HP):
                    ins = pe.transpose(ps[k][:, g * P:(g + 1) * P], tn[:, g, k * P:(k + 1) * P], ident[:, :])
                ins.then_inc(sem("tn_tp"), 1)
            for g in range(HP):
                ins = pe.transpose(ps[2][0:1, g * P:(g + 1) * P], tn[:, g, D:D + 1], ident[:, :])
            ins.then_inc(sem("tn_tp"), 1)
            pe.wait_ge(sem("s_evac"), 3)
            pe.wait_ge(sem("b_fx_in"), 16)
            for a_ in range(HEADS):
                c = slice(a_ * HD, (a_ + 1) * HD)
                for k in range(KD):
                    pe.matmul(ps[3][0:HD, c], w_fx[:, k, c], tnT[:, k, c], start=k == 0, stop=False)
                ins = pe.matmul(ps[3][0:HD, c], b_fx[0:1, c], norm_row[0:1, c], start=False, stop=True)
            ins.then_inc(sem("st_mm"), 1)
            pe.wait_ge(sem("s_evac"), 4)
            pe.matmul(ps[0][0:HD, :], w_q, slice_t, start=True, stop=True).then_inc(sem("qkv_mm"), 1)
            pe.matmul(ps[1][0:HD, :], w_k, slice_t, start=True, stop=True).then_inc(sem("qkv_mm"), 1)
            for a_ in range(HEADS):
                c = slice(a_ * HD, (a_ + 1) * HD)
                ins = pe.matmul(ps[2][0:HD, c], slice_t[:, c], w_v, start=True, stop=True)
            ins.then_inc(sem("qkv_mm"), 1)
            pe.wait_ge(sem("s_evac"), 7)
            for a_ in range(HEADS):
                c = slice(a_ * HD, (a_ + 1) * HD)
                ins = pe.matmul(ps[3][0:HD, c], q_t[:, c], k_t[:, c], start=True, stop=True)
            ins.then_inc(sem("attn_mm"), 1)
            pe.wait_ge(sem("attn_ready"), 1)
            for a_ in range(HEADS):
                c = slice(a_ * HD, (a_ + 1) * HD)
                ins = pe.transpose(ps[4][0:HD, c], attn[:, c], ident[0:HD, 0:HD])
            ins.then_inc(sem("attn_tp"), 1)
            pe.wait_ge(sem("s_evac"), 8)
            for a_ in range(HEADS):
                c = slice(a_ * HD, (a_ + 1) * HD)
                ins = pe.matmul(ps[5][0:HD, c], v_s[:, c], attn_t[:, c], start=True, stop=True)
            ins.then_inc(sem("o_mm"), 1)
            pe.wait_ge(sem("s_evac"), 9)
            for g in range(HP):
                for b in range(2):
                    a_ = 2 * g + b
                    ins = pe.matmul(ps[g][0:HD, b * D:(b + 1) * D], o_t[:, a_ * HD:(a_ + 1) * HD], w_out[:, a_, :],
                                    start=True, stop=True)
                ins.then_inc(sem("m_mm"), 1)
            pe.wait_ge(sem("mid_even"), HP)
            pe.wait_ge(sem("odd_heads"), 1)
            pe.wait_ge(sem("mid_moved"), 16)

            def transpose_sw(t, slot):
                pe.wait_ge(sem("tile_staged"), t + (SPREAD + 1))
                for g in range(HP):
                    ins = pe.transpose(ps[slot][:, g * P:(g + 1) * P], sw_stage[:, slot, g * P:(g + 1) * P],
                                       ident[:, :])
                ins.then_inc(sem("transposed"), 1)

            def spread(t, use, slot):
                if not (isinstance(t, int) and t == T - 1):
                    transpose_sw(t + 1, 1 - slot)
                pe.wait_ge(sem("hT_ready"), t + (SPREAD + 1))
                if not first_use(t):
                    pe.wait_ge(sem("o_added"), t - 1)
                for g in range(HP):
                    ins = pe.matmul(ps[4 + slot][:, 0:D], hT[:, slot, g, :], mid[:, g, :],
                                    start=g == 0, stop=g == HP - 1)
                ins.then_inc(sem("spread_mm"), 1)

            transpose_sw(0, 0)
            node_tiles(pe, spread)

            def w_sage(layer, q):
                return sage_w[:, bass.ds(layer * 4 + q, 1), :].rearrange("p a d -> p (a d)")

            def table_tile(t, layer, slot):
                pe.wait_ge(sem("hT_ready"), t + layer * T + (TABLE + 1))
                if not (first_use(t) and isinstance(layer, int) and layer == 0):
                    pe.wait_ge(sem("z_copied"), t + layer * T - 1)
                for k in range(KD):
                    ins = pe.matmul(ps[6 + slot][:, 0:D], hT[:, slot, k, :], w_sage(layer, k),
                                    start=k == 0, stop=k == KD - 1)
                ins.then_inc(sem("z_mm"), 1)

            transpose_h(0, 0, h_stage3, TABLE)

            def first_table(t, use, slot):
                if not (isinstance(t, int) and t == T - 1):
                    transpose_h(t + 1, 1 - slot, h_stage3, TABLE)
                table_tile(t, 0, slot)

            node_tiles(pe, first_table)

            def root_tile(i, layer, first):
                pe.wait_ge(sem("root_staged"), layer * T + (i + 1))
                for k in range(KD):
                    ins = pe.transpose(ps[0][:, k * P:(k + 1) * P], h_stage3[:, 0, k * P:(k + 1) * P], ident[:, :])
                ins.then_inc(sem("root_tp"), 1)
                pair_sums(i, layer + 1, first, range(0, GROUP))
                pe.wait_ge(sem("root_hT"), layer * T + (i + 1))
                pe.wait_ge(sem("root_kept"), layer * T + (i + 1))
                for k in range(KD):
                    ins = pe.matmul(ps[2][:, 0:D], hT[:, 0, k, :], w_sage(layer, KD + k),
                                    start=k == 0, stop=k == KD - 1)
                ins.then_inc(sem("root_mm"), 1)
                pair_sums(i, layer + 1, first, range(GROUP, RING))

            def gather_layer(layer):
                root_tile(0, layer, False)
                with pe.Fori(1, T) as i:
                    root_tile(i, layer, False)
                for i in range(T, ROUNDS):
                    pair_sums(i, layer + 1, False)

            def transpose_out(t, layer, slot):
                pe.wait_ge(sem("h_staged"), t + layer * T + 1)
                for k in range(KD):
                    ins = pe.transpose(ps[slot][:, k * P:(k + 1) * P], h_stage3[:, slot, k * P:(k + 1) * P], ident[:, :])
                ins.then_inc(sem("transposed"), 1)

            with pe.Fori(0, LAYERS - 1) as layer:
                gather_layer(layer)
                transpose_out(0, layer, 0)

                def next_table(t, use, slot):
                    if not (isinstance(t, int) and t == T - 1):
                        transpose_out(t + 1, layer, 1 - slot)
                    table_tile(t, layer + 1, slot)

                node_tiles(pe, next_table)
            gather_layer(LAYERS - 1)

            def gate_tile(t, use, slot):
                if not (isinstance(t, int) and t == T - 1):
                    transpose_h(t + 1, 1 - slot, h_stage3, TABLE + T)
                pe.wait_ge(sem("hT_ready"), t + (GATE + 1))
                for k in range(KD):
                    ins = pe.matmul(ps[7][:, bass.ds(t * X16, X16)], hT[:, slot, k, :], gate_w[:, k, :],
                                    start=k == 0, stop=k == KD - 1)
                ins.then_inc(sem("gate_mm"), 1)

            transpose_h(0, 0, h_stage3, TABLE + T)
            node_tiles(pe, gate_tile)
            pe.wait_ge(sem("counts_ready"), 1)
            pe.matmul(ps[6][:, 0:X16], ones[:, :], counts, start=True, stop=True).then_inc(sem("counts_mm"), 1)
            pe.matmul(ps[6][:, 32:32 + X16], before[:, :], counts, start=True, stop=True)\
                .then_inc(sem("counts_mm"), 1)

            def transpose_tokens(c, use, k16, slot):
                pe.wait_ge(sem(f"rows_in{k16}"), scattered(k16) + 16 + use * 16)
                for k in range(KD):
                    ins = pe.transpose(ps[slot][:, k * P:(k + 1) * P], rows[:, k16, k * P:(k + 1) * P], ident[:, :])
                ins.then_inc(sem("x_used"), 1)

            def expert(c, use, j, last=False):
                slot = j % 2
                loads = use * (32 * RING // 2) + 32 * (j // 2 + 1)
                pe.wait_ge(sem(f"w1_in{slot}"), loads)
                pe.wait_ge(sem("hT_ready"), c + (EXPERTS + 1))
                for f in range(KF):
                    for k in range(KD):
                        ins = pe.matmul(hid_bank(slot, f), w1[:, slot, k, f * P:(f + 1) * P],
                                        hT[:, slot, k, :], start=k == 0, stop=k == KD - 1)
                    ins.then_inc(sem("hid_mm"), 1)
                if not last:
                    transpose_tokens(c + 1, use + (j + 1) // RING, (j + 1) % RING, 1 - slot)
                if not (isinstance(use, int) and use == 0 and j < 2):
                    pe.wait_ge(sem("y_copied"), c - 1)
                pe.wait_ge(sem(f"w2_in{slot}"), loads)
                for f in range(KF):
                    pe.wait_ge(sem("hid_ready"), c * KF + (f + 1))
                    ins = pe.matmul(ps[4 + slot][:, 0:D], hidden[:, slot, f, :], w2[:, slot, f, :],
                                    start=f == 0, stop=f == KF - 1)
                ins.then_inc(sem("y_done"), 1)

            transpose_tokens(0, 0, 0, 0)
            for j in range(RING):
                expert(j, 0, j)
            with pe.Fori(1, ETILES // RING - 1) as i:
                for j in range(RING):
                    expert(i * RING + j, i, j)
            use = ETILES // RING - 1
            for j in range(RING):
                expert(use * RING + j, use, j, last=j == RING - 1)

        @block.vector
        def _(dve):
            link = Chain(dve, sem("link"))

            dve.wait_ge(sem("const"), 5)
            link(dve.tensor_scalar(before[:, :], iota[:, 0:P], pidx[:, 0:1], None, ALU.is_gt))
            dve.tensor_scalar(ident[:, :], iota[:, 0:P], pidx[:, 0:1], None, ALU.is_equal).then_inc(sem("ident_ready"), 1)

            def tile_stats(src, t):
                return dve.bn_stats(bst[:, bass.ds(t, 1), :].rearrange("p a n -> p (a n)"),
                                    src[:, bass.ds(t, 1), 0:D].rearrange("p a n -> p (a n)"))

            def all_stats(src):
                with link.loop(0, T // UNROLL, UNROLL) as i:
                    for j in range(UNROLL):
                        link.mark(tile_stats(src, UNROLL * i + j))
                link.settle()

            def moments(k):
                mean, var, half, tmp = mv[:, :, 0], mv[:, :, 1], nrm[:, 2, :], nrm[:, 3, :]
                link.mark(dve.tensor_tensor(mean, bst[:, :, 1], bst[:, :, 4], ALU.add))
                link.mark(dve.tensor_tensor(half, bst[:, :, 1], bst[:, :, 4], ALU.subtract))
                link(dve.tensor_tensor(var, bst[:, :, 2], bst[:, :, 5], ALU.add))
                link.mark(dve.tensor_scalar(mean, mean, 0.5, None, ALU.mult))
                link.mark(dve.tensor_scalar(var, var, 1.0 / D, None, ALU.mult))
                link(dve.scalar_tensor_tensor(tmp, half, 0.25, half, ALU.mult, ALU.mult))
                link(dve.tensor_tensor(var, var, tmp, ALU.add))
                dve.sem_inc(sem("var_ready"), 1)
                link(dve.tensor_scalar(nrm[:, 1, :], mv[:, :, 1], EPS, None, ALU.add))
                dve.wait_ge(sem("sd_ready"), k + 1)
                refine(nrm[:, 0, :], nrm[:, 1, :], nrm[:, 2, :], nrm[:, 3, :])

            def normalise(src, dst, k, stats=True):
                if stats:
                    all_stats(src)
                moments(k)
                with dve.Fori(0, T // UNROLL) as i:
                    for j in range(UNROLL):
                        t = UNROLL * i + j
                        dve.tensor_scalar(dst[:, bass.ds(t, 1), 0:D].rearrange("p a n -> p (a n)"),
                                          src[:, bass.ds(t, 1), 0:D].rearrange("p a n -> p (a n)"),
                                          mv[:, bass.ds(t, 1), 0:1].rearrange("p a n -> p (a n)"),
                                          nrm[:, 2, bass.ds(t, 1)], ALU.subtract, ALU.mult)\
                            .then_inc(sem("h_ready"), 1)
                dve.wait_ge(sem("h_ready"), (k + 1) * T)

            def refine(sd, v, y, tmp):
                link(dve.reciprocal(y, sd))
                link(dve.tensor_tensor(tmp, y, y, ALU.mult))
                link(dve.tensor_tensor(tmp, tmp, v, ALU.mult))
                link(dve.tensor_scalar(tmp, tmp, -0.5, 1.5, ALU.mult, ALU.add))
                link(dve.tensor_tensor(y, y, tmp, ALU.mult))

            dve.wait_ge(sem("x_in"), 32)
            normalise(x, h, 0)
            dve.wait_ge(sem("dst_in"), 48)
            blk_a = f_posi
            blk_b = f_pay.rearrange("p e w -> p (e w)")[:, 0:EF].bitcast(I32)
            link.mark(dve.tensor_scalar(blk_a, dst_a, 7, None, ALU.arith_shift_right))
            link(dve.tensor_scalar(blk_b, dst_b, 7, None, ALU.arith_shift_right))
            link(dve.tensor_tensor(junk, blk_a, blk_b, ALU.is_gt))
            link.mark(dve.tensor_reduce(cum[:, T + 1:T + 2], junk, AX, ALU.add))
            link(dve.tensor_copy(f_blk, blk_a))
            for b in range(T + 1):
                link(dve.tensor_scalar(junk, f_blk, float(b), 0.0, ALU.is_lt, ALU.add, accum_out=cum[:, b:b + 1]))
            dve.sem_inc(sem("cum_ready"), 1)


            dve.wait_ge(sem("tot_mm"), 2)
            tot, pre, cf, np_, ps_, dl, dd = (small_f[:, j, 0:T + 2] for j in range(7))
            link.mark(dve.tensor_copy(tot, ps[6][:, 0:T + 2]))
            link(dve.tensor_copy(pre, ps[7][:, 0:T + 2]))
            dve.tensor_copy(flag[:, :], tot[:, T + 1:T + 2]).then_inc(sem("flag_ready"), 1)
            dve.wait_ge(sem("flag_ready"), 1)

            late = dve.value_load(flag[0:1, 0:1], min_val=0, max_val=E)
            n_before = link.n
            flink = Chain(dve, sem("flink"))
            with dve.If(late > 0):
                off = small_f[0:EP, 7, 0:T]
                dve.wait_ge(sem("spare_in"), 32)
                flink(dve.tensor_tensor(off, pre[0:EP, 1:T + 1], pre[0:EP, 0:T], ALU.subtract))
                flink(dve.tensor_tensor(off, off, tot[0:EP, 0:T], ALU.add))
                flink(dve.tensor_scalar(off, off, -1.0, None, ALU.add))
                flink(dve.memset(junk, 1.0))
                flink(dve.memset(f_pos, 0.0))
                with flink.loop(0, T, 4) as b:
                    flink(dve.tensor_scalar(f_m, f_blk, iota[0:EP, bass.ds(b, 1)], None, ALU.is_equal))
                    flink(dve.tensor_tensor_scan(f_s, junk, f_m, 0.0, ALU.mult, ALU.add))
                    flink(dve.scalar_tensor_tensor(f_s, f_s, off[:, bass.ds(b, 1)], f_m, ALU.add, ALU.mult))
                    flink(dve.tensor_tensor(f_pos, f_pos, f_s, ALU.add))
                flink(dve.tensor_copy(f_posi, f_pos))
                flink(dve.tensor_copy(f_m, src_a))
                flink(dve.scalar_tensor_tensor(f_pay[:, :, 0], f_m, float(R), rel_a, ALU.mult, ALU.add))
                flink(dve.tensor_copy(f_pay[:, :, 1], dst_a))
                dve.sem_inc(sem("f_ready"), 1)
            assert link.n == n_before
            dve.wait_ge(sem("edge_in"), 9 * 16)
            ev = edges.rearrange("p (n w) -> p n w", w=2)
            link(dve.tensor_copy(ev[:, :, 1], edge_int))
            link(dve.tensor_copy(ev[:, :, 0], edge_src))
            link(dve.scalar_tensor_tensor(ev[:, :, 0], ev[:, :, 0], float(R), edge_rel, ALU.mult, ALU.add))
            dve.sem_inc(sem("edges_float"), 1)

            first, last_, seg = (small_i[:, j, 0:T + 1] for j in range(3))
            link.mark(dve.tensor_copy(seg, tot[:, 0:T + 1]))
            link(dve.tensor_scalar(cf[:, 0:T], tot[:, 1:T + 1], -1.0, None, ALU.add))
            link(dve.tensor_copy(last_[:, 0:T], cf[:, 0:T]))
            link.mark(dve.tensor_scalar(first, seg, 7, None, ALU.arith_shift_right))
            link(dve.tensor_scalar(last_[:, 0:T], last_[:, 0:T], 7, None, ALU.arith_shift_right))
            link.mark(dve.tensor_copy(cf[:, 0:T], first[:, 0:T]))
            link(dve.tensor_copy(np_[:, 0:T], last_[:, 0:T]))
            link(dve.tensor_tensor(np_[:, 0:T], np_[:, 0:T], cf[:, 0:T], ALU.subtract))
            link.mark(dve.tensor_scalar(np_[:, 0:T], np_[:, 0:T], 1.0, None, ALU.add))
            link(dve.tensor_tensor(dd[:, 0:T], tot[:, 1:T + 1], tot[:, 0:T], ALU.is_gt))
            link(dve.tensor_tensor(np_[:, 0:T], np_[:, 0:T], dd[:, 0:T], ALU.mult))
            link.mark(dve.memset(ps_[:, 0:1], 0.0))
            link(dve.tensor_tensor_scan(ps_[:, 1:T + 1], ones[:, 0:T], np_[:, 0:T], 0.0, ALU.mult, ALU.add))
            link.mark(dve.tensor_tensor(dl[:, 0:T], cf[:, 0:T], ps_[:, 0:T], ALU.subtract))
            link(dve.memset(dl[:, T:T + 1], 0.0))
            link(dve.tensor_tensor(dd[:, 1:T + 1], dl[:, 1:T + 1], dl[:, 0:T], ALU.subtract))
            link.mark(dve.tensor_scalar(pair_c, iota[:, 0:PAIRS], dl[:, 0:1], None, ALU.add))
            link(dve.memset(pair_b, 0.0))
            tm = pair_dst[:, 0:PAIRS]
            for b in range(1, T + 1):
                link(dve.tensor_scalar(tm, iota[:, 0:PAIRS], ps_[:, b:b + 1], None, ALU.is_ge))
                link.mark(dve.scalar_tensor_tensor(pair_c, tm, dd[:, b:b + 1], pair_c, ALU.mult, ALU.add))
                link(dve.tensor_tensor(pair_b, pair_b, tm, ALU.add))
            link.mark(dve.tensor_copy(pair_tile[:, :], pair_b))
            link(dve.tensor_scalar(pair_c, pair_c, float(EC - 1), None, ALU.min))
            for k in range(EK):
                link.mark(dve.tensor_scalar(chosen_v[:, k, :], pair_c, pidx[:, k:k + 1], None, ALU.is_equal))
            link.settle()
            dve.sem_inc(sem("chosen_ready"), 1)

            dve.wait_ge(sem("param_in"), PARAMS * 16)
            link(dve.tensor_tensor(x[:, :, :], x[:, :, :], beta_b.unsqueeze(1).to_broadcast([P, T, D]), ALU.add))
            dve.wait_ge(sem("edges_ready"), 1)
            dve.wait_ge(sem("proj_stored0"), 16 * (T // 2 + 1))
            dve.wait_ge(sem("proj_stored1"), 16 * (T // 2))
            for g in range(HP):
                link.mark(dve.tensor_scalar(bx_rep[:, g, :], ones[:, :], bx_col[:, g:g + 1], None, ALU.mult))
            link(dve.tensor_scalar(temp_b, temp_b, 0.1, 5.0, ALU.max, ALU.min))
            link(dve.reciprocal(temp_b, temp_b))
            dve.sem_inc(sem("bx_ready"), 1)
            tb = temp_b.unsqueeze(2).to_broadcast([P, HEADS, HD])
            for k in range(KD):
                dve.wait_ge(sem("wc_mm"), k + 1)
                link.mark(dve.tensor_tensor(wc[:, k, :].rearrange("p (a n) -> p a n", a=HEADS),
                                            ps[4 + k][:, :].rearrange("p (a n) -> p a n", a=HEADS), tb, ALU.mult))
            dve.wait_ge(sem("wc_mm"), 3)
            bcv = bc[:, :].rearrange("p (a n) -> p a n", a=HEADS)
            link(dve.tensor_tensor(bcv, ps[3][:, :].rearrange("p (a n) -> p a n", a=HEADS),
                                   bslice_b.unsqueeze(1).to_broadcast([P, HEADS, HD]), ALU.add))
            link(dve.tensor_tensor(bcv, bcv, tb, ALU.mult))
            dve.sem_inc(sem("wc_ready"), 1)

            dve.wait_ge(sem("pairs_mm"), 2)
            link.mark(dve.tensor_copy(pair_row0[:, :], ps[6][:, 0:PAIRS]))
            link.mark(dve.memset(pair_dst[:, PAIRS:PAIRS + BATCH], -1.0))
            link(dve.scalar_tensor_tensor(pair_dst[:, 0:PAIRS], pair_b, -float(P), ps[7][:, 0:PAIRS], ALU.mult, ALU.add))
            link(dve.tensor_scalar(pair_row[:, :], pair_row0[:, :], 3, None, ALU.arith_shift_right))
            dve.sem_inc(sem("pair_tables"), 1)

            def build_onehots(t, k):
                dve.tensor_tensor(onehot[:, k % (2 * BATCH):k % (2 * BATCH) + BATCH, :],
                                  iota[:, 0:P].unsqueeze(1).to_broadcast([P, BATCH, P]),
                                  pair_dst[:, bass.ds(t, BATCH)].unsqueeze(2).to_broadcast([P, BATCH, P]),
                                  ALU.is_equal).then_inc(sem("onehot_ready"), 1)

            def add_pairs(i, r, first):
                for k0 in range(0, RING, BATCH):
                    build_onehots(i * RING + k0 + BATCH, k0 + BATCH)
                    _, tiles = nc.values_load_multi_w_load_instructions(
                        pair_tile[0:1, bass.ds(i * RING + k0, BATCH)], engines=(mybir.EngineType.DVE,),
                        min_val=0, max_val=T,
                        skip_runtime_bounds_check_because="a pair's tile counts some of T tiles' starts")
                    for k in range(k0, k0 + BATCH):
                        g = r * PAIRS + (i * RING + k)
                        if not (first and k == 0):
                            dve.wait_ge(sem("pair_added"), g)
                        dve.wait_ge(sem("pair_done"), g + 1)
                        v = accv[:, bass.ds(tiles[k - k0], 1), :].rearrange("p a n -> p (a n)")
                        dve.tensor_tensor(v, v, ps[4 + k % BATCH][:, 0:D + 1], ALU.add)\
                            .then_inc(sem("pair_added"), 1)

            def gather_edges(r):
                link(dve.memset(acc[:, :], 0.0))
                build_onehots(0, 0)
                add_pairs(0, r, isinstance(r, int))
                with dve.Fori(1, ROUNDS) as i:
                    add_pairs(i, r, False)

            gather_edges(0)
            dve.wait_ge(sem("pair_added"), PAIRS)
            dve.wait_ge(sem("bn_mean"), 1)
            g3 = accv[:, 0:T, 0:D]
            link.mark(dve.tensor_copy(col[:, 1, :], ps[4][:, 0:D]))
            link.settle()
            groups = [slice(t, t + UNROLL) for t in range(0, T, UNROLL)]
            spread_over = [P, UNROLL, D]
            for q in groups:
                dve.tensor_tensor(g3[:, q, :], g3[:, q, :], col[:, 1:2, :].to_broadcast(spread_over), ALU.subtract)\
                    .then_inc(sem("centred"), 1)
            dve.wait_ge(sem("centred"), len(groups))
            dve.wait_ge(sem("bn_sd"), 1)
            link(dve.tensor_scalar(col[:, 1, :], ps[5][:, 0:D], EPS, None, ALU.add))
            refine(col[:, 0, :], col[:, 1, :], col[:, 2, :], col[:, 3, :])
            link(dve.tensor_tensor(col[:, 2, :], col[:, 2, :], gamma_b, ALU.mult))
            for n, q in enumerate(groups + [None]):
                if q:
                    link.mark(dve.tensor_tensor(g3[:, q, :], g3[:, q, :], col[:, 2:3, :].to_broadcast(spread_over), ALU.mult))
                if n:
                    link.mark(dve.tensor_tensor(x[:, groups[n - 1], :], x[:, groups[n - 1], :], g3[:, groups[n - 1], :], ALU.add))
                link.settle()
            all_stats(x)
            normalise(x, h, 1, stats=False)
            per = 4

            def softmax_tile(t, use, slot):
                v = swv[:, bass.ds(t, 1), :].rearrange("p a n -> p (a n)")
                v3 = v.rearrange("p (a n) -> p a n", a=HEADS)
                mx = soft[:, slot * 8:slot * 8 + 8]
                dve.wait_ge(sem("l_mm"), t + 1)
                dve.tensor_tensor(v, ps[2 + slot][:, :], bc[:, :], ALU.add).then_inc(sem("l_read"), 1)
                dve.wait_ge(sem("l_read"), t + 1)
                dve.nop(nofuse=True)
                link(dve.tensor_reduce(mx, v3, AX, ALU.max))
                dve.tensor_tensor(v3, v3, mx.unsqueeze(2).to_broadcast([P, HEADS, HD]), ALU.subtract)\
                    .then_inc(sem("l_shifted"), 1)

            def weights_tile(t, use, slot):
                v = swv[:, bass.ds(t, 1), :].rearrange("p a n -> p (a n)")
                v3 = v.rearrange("p (a n) -> p a n", a=HEADS)
                rs = soft[:, 16 + slot * 8:24 + slot * 8]
                dve.wait_ge(sem("l_exp"), t + 1)
                dve.nop(nofuse=True)
                link(dve.tensor_reduce(rs, v3, AX, ALU.add))
                link(dve.reciprocal(rs, rs))
                if not first_use(t):
                    dve.wait_ge(sem("slices_mm"), t - 1)
                    dve.wait_ge(sem("sw_kept"), t - 1)
                dve.tensor_tensor(sw_stage[:, slot, :].rearrange("p (a n) -> p a n", a=HEADS), v3,
                                  rs.unsqueeze(2).to_broadcast([P, HEADS, HD]), ALU.mult).then_inc(sem("sw_ready"), 1)

            softmax_tile(0, 0, 0)
            softmax_tile(1, 0, 1)
            weights_tile(0, 0, 0)
            softmax_tile(2, 0, 0)
            weights_tile(1, 0, 1)
            with link.loop(1, T // 2, 6) as i:
                softmax_tile(2 * i + 1, i, 1)
                weights_tile(2 * i, i, 0)
                softmax_tile(2 * i + 2, i, 0)
                weights_tile(2 * i + 1, i, 1)
            weights_tile(T - 1, 0, 0)
            dve.wait_ge(sem("sw_ready"), T)

            dve.wait_ge(sem("slices_mm"), T)
            dve.wait_ge(sem("sw_kept"), T)
            for g in range(HP):
                link.mark(dve.tensor_scalar(hs[:, g:g + 1], ps[4 + g][:, D:D + 1], EPS, None, ALU.add))
            link.settle()
            link(dve.reciprocal(hs[:, 4:4 + HP], hs[:, 0:HP]))
            for g in range(HP):
                link.mark(dve.tensor_scalar(tn[:, g, :], ps[4 + g][:, 0:D + 1], hs[:, 4 + g:5 + g], None, ALU.mult))
            link.settle()
            dve.sem_inc(sem("tn_ready"), 1)
            link(dve.tensor_tensor(x[:, :, :], x[:, :, :], bout_b.unsqueeze(1).to_broadcast([P, T, D]), ALU.add))
            dve.wait_ge(sem("attn_mm"), 1)
            av = attn.rearrange("p (a n) -> p a n", a=HEADS)
            sv = ps[3][0:HD, :].rearrange("p (a n) -> p a n", a=HEADS)
            mx, rs = soft[0:HD, 0:8], soft[0:HD, 8:16]
            link(dve.tensor_reduce(mx, sv, AX, ALU.max))
            link(dve.tensor_tensor(av, sv, mx.unsqueeze(2).to_broadcast([HD, HEADS, HD]), ALU.subtract))
            dve.sem_inc(sem("attn_shifted"), 1)
            dve.wait_ge(sem("attn_exp"), 1)
            link(dve.tensor_reduce(rs, av, AX, ALU.add))
            link(dve.reciprocal(rs, rs))
            link(dve.tensor_tensor(av, av, rs.unsqueeze(2).to_broadcast([HD, HEADS, HD]), ALU.mult))
            dve.sem_inc(sem("attn_ready"), 1)

            def add_spread(t, use, slot):
                v = x[:, bass.ds(t, 1), :].rearrange("p a n -> p (a n)")
                dve.wait_ge(sem("spread_mm"), t + 1)
                dve.tensor_tensor(v, v, ps[4 + slot][:, 0:D], ALU.add).then_inc(sem("o_added"), 1)
                dve.wait_ge(sem("o_added"), t + 1)
                dve.nop(nofuse=True)
                link.mark(tile_stats(x, t))

            node_tiles(dve, add_spread, link, 1)
            link.settle()
            normalise(x, h, 2, stats=False)
            rdeg = nrm[:, 2, :]

            dve.sem_inc(sem("root_kept"), 1)

            def gather_layer(layer, bl):
                def keep_root(i):
                    dve.wait_ge(sem("root_mm"), layer * T + (i + 1))
                    dve.tensor_tensor(root_part[:, bass.ds(i, 1), :].rearrange("p a n -> p (a n)"), ps[2][:, 0:D],
                                      bl, ALU.add).then_inc(sem("root_kept"), 1)

                link(dve.memset(acc[:, :], 0.0))
                build_onehots(0, 0)
                add_pairs(0, layer + 1, False)
                keep_root(0)
                with dve.Fori(1, T) as i:
                    add_pairs(i, layer + 1, False)
                    keep_root(i)
                for i in range(T, ROUNDS):
                    add_pairs(i, layer + 1, False)

            def elu_in(t, layer, slot):
                n = layer * T
                if not first_use(t):
                    dve.wait_ge(sem("elu_pos"), t + n - 1)
                dve.scalar_tensor_tensor(elu_v[:, slot], accv[:, bass.ds(t, 1), 0:D].rearrange("p a n -> p (a n)"),
                                         rdeg[:, bass.ds(t, 1)],
                                         root_part[:, bass.ds(t, 1), :].rearrange("p a n -> p (a n)"),
                                         ALU.mult, ALU.add).then_inc(sem("elu_in"), 1)
                dve.wait_ge(sem("elu_in"), t + n + 1)
                if not first_use(t):
                    dve.wait_ge(sem("elu_exp"), t + n - 1)
                dve.nop(nofuse=True)
                dve.tensor_scalar(elu_n[:, slot], elu_v[:, slot], 0.0, None, ALU.min).then_inc(sem("elu_neg"), 1)

            def elu_out(t, layer, slot, last):
                n = layer * T
                dve.wait_ge(sem("elu_exp"), t + n + 1)
                dve.wait_ge(sem("elu_pos"), t + n + 1)
                if not first_use(t) and not last:
                    dve.wait_ge(sem("layer_out"), t + n)
                    dve.wait_ge(sem("transposed"), t + (layer + 1) * T + (TABLE - 1))
                dve.nop(nofuse=True)
                dve.scalar_tensor_tensor(h_stage3[:, slot], elu_e[:, slot], -1.0, elu_p[:, slot], ALU.add, ALU.add)\
                    .then_inc(sem("h_staged"), 1)
                if last:
                    v = x[:, bass.ds(t, 1), :].rearrange("p a n -> p (a n)")
                    dve.wait_ge(sem("h_staged"), t + n + 1)
                    dve.nop(nofuse=True)
                    link(dve.tensor_tensor(v, v, h_stage3[:, slot], ALU.add))
                    link.mark(tile_stats(x, t))

            def layer_tiles(layer, last):
                dve.wait_ge(sem("pair_added"), layer * PAIRS + 2 * PAIRS)
                dve.wait_ge(sem("root_kept"), layer * T + (T + 1))
                link(dve.tensor_scalar(rdeg, accv[:, 0:T, D], 1.0, None, ALU.max))
                link(dve.reciprocal(rdeg, rdeg))
                elu_in(0, layer, 0)
                elu_in(1, layer, 1)
                elu_out(0, layer, 0, last)
                elu_in(2, layer, 0)
                elu_out(1, layer, 1, last)
                with link.loop(1, T // 2, 4 if last else 0) as i:
                    elu_in(2 * i + 1, layer, 1)
                    elu_out(2 * i, layer, 0, last)
                    elu_in(2 * i + 2, layer, 0)
                    elu_out(2 * i + 1, layer, 1, last)
                elu_out(T - 1, layer, 0, last)

            with link.loop(0, LAYERS - 1, 3) as layer:
                gather_layer(layer, bl_b[:, bass.ds(layer, 1), :].rearrange("p a n -> p (a n)"))
                layer_tiles(layer, False)
            gather_layer(LAYERS - 1, bl_b[:, LAYERS - 1, :])
            layer_tiles(LAYERS - 1, True)
            link.settle()
            dve.sem_inc(sem("layers_done"), 1)
            dve.wait_ge(sem("layer_out"), (LAYERS - 1) * T + 1)
            normalise(x, h, 3, stats=False)
            dve.wait_ge(sem("gate_mm"), T)
            link(dve.tensor_tensor(logits, ps[7][:, 0:T * X16].rearrange("p (t e) -> p t e", t=T),
                                   gb_b.unsqueeze(1).to_broadcast([P, T, X16]), ALU.add))

            for t in range(T):
                link.mark(dve.max(top8[:, t, :], logits[:, t, :]))
            link.settle()
            for t in range(T):
                link.mark(dve.max_index(at8[:, t, :], top8[:, t, :], logits[:, t, :]))
            link.mark(dve.tensor_tensor(gate_t[:, 0, :], top8[:, :, 1], top8[:, :, 0], ALU.subtract))
            link.settle()
            dve.sem_inc(sem("gate_diff"), 1)
            ent3 = ent.rearrange("p (t k) -> p t k", k=TOPK)
            link.mark(dve.tensor_scalar(hs[:, 8:9], pidx[:, 0:1], float(LAST), 99.0, ALU.is_ge, ALU.mult))
            link(dve.tensor_copy(ent3, at8[:, :, 0:TOPK]))
            link(dve.tensor_scalar(ent3[:, T - 1, :], ent3[:, T - 1, :], hs[:, 8:9], None, ALU.add))
            by_expert = [P, X16, ENTRIES]
            link(dve.tensor_tensor(chose, ent.unsqueeze(1).to_broadcast(by_expert),
                                   iota[:, 0:X16].unsqueeze(2).to_broadcast(by_expert), ALU.is_equal))
            link(dve.tensor_reduce(counts, chose, AX, ALU.add))
            dve.sem_inc(sem("counts_ready"), 1)
            dve.wait_ge(sem("gate_exp"), 1)
            link(dve.tensor_scalar(gate_t[:, 2, :], gate_t[:, 1, :], 1.0, None, ALU.add))
            link(dve.reciprocal(gates[:, :, 0], gate_t[:, 2, :]))
            link(dve.tensor_tensor(gates[:, :, 1], gates[:, :, 0], gate_t[:, 1, :], ALU.mult))
            base = small_f[:, 3, 0:X16]
            link.mark(dve.tensor_tensor_scan(place.rearrange("p e n -> p (e n)"),
                                             ones[:, 0:1].to_broadcast([P, X16 * ENTRIES]),
                                             chose.rearrange("p e n -> p (e n)"), 0.0, ALU.mult, ALU.add))
            link(dve.tensor_tensor_scan(base, ones[:, 0:X16], counts, 0.0, ALU.mult, ALU.add))
            link(dve.tensor_tensor(base, base, counts, ALU.subtract))
            dve.wait_ge(sem("counts_mm"), 2)
            nt, ts, off = (small_f[:, j, 0:X16] for j in range(3))
            nti = small_i[:, 0, 0:X16]
            link(dve.tensor_scalar(nt, ps[6][:, 0:X16], float(P - 1), None, ALU.add))
            link(dve.tensor_copy(nti, nt))
            link(dve.tensor_scalar(nti, nti, 7, None, ALU.arith_shift_right))
            link(dve.tensor_copy(nt, nti))
            link(dve.tensor_tensor_scan(ts, ones[:, 0:X16], nt, 0.0, ALU.mult, ALU.add))
            link(dve.tensor_tensor(ts, ts, nt, ALU.subtract))
            link(dve.scalar_tensor_tensor(off, ts, float(P), ps[6][:, 32:32 + X16], ALU.mult, ALU.add))
            link(dve.scalar_tensor_tensor(off, off, -1.0, base, ALU.add, ALU.subtract))
            link(dve.tensor_tensor(cmp_e, iota[:, 0:ETILES].unsqueeze(2).to_broadcast([P, ETILES, X16 - 1]),
                                   ts[:, 1:X16].unsqueeze(1).to_broadcast([P, ETILES, X16 - 1]), ALU.is_ge))
            link(dve.tensor_reduce(tile_x, cmp_e, AX, ALU.add))
            link.mark(dve.memset(tile_new[:, 0:2], 1))
            link.mark(dve.tensor_tensor(tile_new[:, 2:ETILES], tile_x[:, 2:ETILES], tile_x[:, 0:ETILES - 2], ALU.is_gt))
            link(dve.tensor_copy(tile_xi, tile_x))
            dve.sem_inc(sem("tile_experts"), 1)
            link(dve.tensor_tensor(place, place, off.unsqueeze(2).to_broadcast(by_expert), ALU.add))
            link(dve.tensor_tensor(place, place, chose, ALU.mult))
            link(dve.tensor_reduce(ent_pos, place.rearrange("p e n -> p n e"), AX, ALU.add))
            link(dve.tensor_copy(ent_posi, ent_pos))
            shift = ETILES.bit_length() - 1
            assert 1 << shift == ETILES
            link.mark(dve.tensor_scalar(ent_row, ent_posi, P - 1, shift, ALU.bitwise_and, ALU.logical_shift_left))
            link(dve.tensor_scalar(ent_row2, ent_posi, 7, None, ALU.arith_shift_right))
            link(dve.tensor_tensor(ent_row, ent_row, ent_row2, ALU.bitwise_or))
            dve.sem_inc(sem("places"), 1)

            link(dve.tensor_tensor(x[:, :, :], x[:, :, :], bf_b.unsqueeze(1).to_broadcast([P, T, D]), ALU.add))

            def copy_y(c, use, slot):
                dve.wait_ge(sem("y_done"), c + 1)
                if not first_use(c):
                    dve.wait_ge(sem(f"y_stored{slot}"), 16 * use)
                dve.tensor_tensor(y_out[:, slot], ps[4 + slot][:, 0:D], b2_b[:, slot], ALU.add)\
                    .then_inc(sem("y_copied"), 1)

            copy_y(0, 0, 0)
            copy_y(1, 0, 1)
            with dve.Fori(1, ETILES // 2) as i:
                copy_y(2 * i, i, 0)
                copy_y(2 * i + 1, i, 1)


            def combine(i, n):
                for k in range(n):
                    j = i * RING + k
                    t = i * (RING // TOPK) + k // TOPK
                    v = h[:, bass.ds(t, 1), 0:D].rearrange("p a n -> p (a n)")
                    w = gates[:, bass.ds(t, 1), k % TOPK:k % TOPK + 1].rearrange("p a n -> p (a n)")
                    dve.wait_ge(sem(f"rows_in{k}"), scattered(k) + 16 * (ETILES // RING) + (i * 16 + 16))
                    if not (isinstance(i, int) and i == 0 and k == 0):
                        dve.wait_ge(sem("combined"), j)
                    dve.scalar_tensor_tensor(v, rows[:, k, 0:D], w, v, ALU.mult, ALU.add)\
                        .then_inc(sem("combined"), 1)
                    if k % TOPK == TOPK - 1:
                        dve.wait_ge(sem("combined"), j + 1)
                        dve.nop(nofuse=True)
                        link.mark(tile_stats(h, t))

            combine(0, RING)
            with link.loop(1, 3, RING // TOPK) as i:
                combine(i, RING)
            combine(3, TOPK)
            link.settle()
            dve.wait_ge(sem("combined"), ENTRIES)
            moments(4)
            link(dve.scalar_tensor_tensor(nrm[:, 3, :], mv[:, :, 0], -1.0, nrm[:, 2, :], ALU.mult, ALU.mult))
            dve.sem_inc(sem("moments_ready"), 1)
            for n, q in enumerate(groups):
                hv = h[:, q, 0:D]
                dve.wait_ge(sem("h_scaled"), n * UNROLL + UNROLL)
                link(dve.tensor_tensor(hv, hv, gf_b.unsqueeze(1).to_broadcast(spread_over), ALU.mult))
                dve.tensor_tensor(hv, hv, x[:, q, :], ALU.add).then_inc(sem("result_ready"), 1)


PARAMS = 10 + 1 + 3 + 3 + 1 + 2

_INPUTS = ["x", "src", "dst", "edge_type_8", "L0_gnn_weight", "L0_gnn_gamma", "L0_gnn_beta", "L0_ffn_W_fx",
           "L0_ffn_b_fx", "L0_ffn_W_x", "L0_ffn_b_x", "L0_ffn_W_slice", "L0_ffn_b_slice", "L0_ffn_W_q",
           "L0_ffn_W_k", "L0_ffn_W_v", "L0_ffn_W_out", "L0_ffn_b_out", "L0_ffn_temperature", "L1_gnn_Wl1",
           "L1_gnn_bl1", "L1_gnn_Wr1", "L1_gnn_Wl2", "L1_gnn_bl2", "L1_gnn_Wr2", "L1_gnn_Wl3", "L1_gnn_bl3",
           "L1_gnn_Wr3", "L1_ffn_gate_w", "L1_ffn_gate_b", "L1_ffn_w1", "L1_ffn_b1", "L1_ffn_w2", "L1_ffn_b2",
           "L1_ffn_gamma", "L1_ffn_beta"]


def kernel(**inputs):
    import numpy as np
    import concourse.bacc as bacc
    from concourse.bass_utils import run_bass_kernel_spmd

    nc = bacc.Bacc("TRN2", target_bir_lowering=False, num_devices=1)
    arrays, views = {}, {}
    for name in _INPUTS:
        a = np.ascontiguousarray(inputs[name])
        arrays[f"in_{name}"] = a
        views[name] = nc.dram_tensor(f"in_{name}", a.shape, mybir.dt.from_np(a.dtype), kind="ExternalInput").ap()
    out = nc.dram_tensor("out_0", (N, D), FP32, kind="ExternalOutput").ap()
    gnn_ffn_moe_program(nc, views, out)
    r = run_bass_kernel_spmd(nc, [arrays], core_ids=[0])
    return r.results[0]["out_0"]
```
